# Optimizing a Trainium2 kernel written in Bass

```python
import numpy as np
import jax
import jax.numpy as jnp

def _softmax(x, axis=-1):
    return jax.nn.softmax(x, axis=axis)

def _gelu(x):
    return jax.nn.gelu(x, approximate=True)

def _silu(x):
    return jax.nn.silu(x)

def _sigmoid(x):
    return jax.nn.sigmoid(x)

def _layernorm(x, axis=-1, eps=1e-05):
    m = jnp.mean(x, axis=axis, keepdims=True)
    v = jnp.var(x, axis=axis, keepdims=True)
    return (x - m) / jnp.sqrt(v + eps)

def _scatter_add(tgt, idx, src, axis=0):
    return tgt.at[idx].add(src)

def _segment_sum(src, seg, n):
    return jax.ops.segment_sum(src, seg, n)
kernel_name = 'mk_sandwich_d2_jaxref_r8_d45f38'

def setup_inputs(seed: int=0):
    np.random.seed(seed)
    _w = jnp.asarray

    def _L0_attn_setup():
        import jax, jax.numpy as jnp
        import numpy as np
        D_MODEL = 128
        N_HEADS = 16
        HEAD_DIM = D_MODEL // N_HEADS
        D_LATENT = 32
        LAMBDA_DECAY = 0.01
        TIME_STEP = 0.01
        CLAMP = 10000.0

        def _reference_tuple_inner(x, Wq, Wk, Wv, Wo, W_down_kv, W_up_k, W_up_v):
            B, S, _ = x.shape
            q = x @ Wq
            k = x @ Wk
            v = x @ Wv
            latent_kv = (k + v) @ W_down_kv
            k_rec = latent_kv @ W_up_k
            v_rec = latent_kv @ W_up_v

            def heads(t):
                return t.reshape(B, S, N_HEADS, HEAD_DIM).transpose(0, 2, 1, 3)
            qh, kh, vh = (heads(q), heads(k_rec), heads(v_rec))
            scale = 1.0 / (jnp.sqrt(jnp.float32(D_MODEL)) + 1e-08)
            scores = jnp.einsum('bhqd,bhkd->bhqk', qh, kh) * scale
            scores = jnp.clip(jnp.nan_to_num(scores, nan=-1000000000.0), -CLAMP, CLAMP)
            idx = jnp.arange(S, dtype=jnp.float32)
            decay = jnp.exp(-LAMBDA_DECAY * TIME_STEP * jnp.abs(idx[:, None] - idx[None, :]))
            scores = scores * decay[None, None, :, :]
            scores = jnp.clip(jnp.nan_to_num(scores, nan=-1000000000.0), -CLAMP, CLAMP)
            attn = jax.nn.softmax(scores, axis=-1)
            out = jnp.einsum('bhqk,bhkd->bhqd', attn, vh)
            out = out.transpose(0, 2, 1, 3).reshape(B, S, D_MODEL)
            return (out @ Wo, latent_kv)
        key = jax.random.key(seed)
        ks = jax.random.split(key, 8)
        B, S = (2, 256)

        def w(k, i, o):
            return jax.random.normal(k, (i, o), dtype=jnp.float32) * 0.02
        return {'x': jax.random.normal(ks[0], (B, S, D_MODEL), dtype=jnp.float32), 'Wq': w(ks[1], D_MODEL, D_MODEL), 'Wk': w(ks[2], D_MODEL, D_MODEL), 'Wv': w(ks[3], D_MODEL, D_MODEL), 'Wo': w(ks[4], D_MODEL, D_MODEL), 'W_down_kv': w(ks[5], D_MODEL, D_LATENT), 'W_up_k': w(ks[6], D_LATENT, D_MODEL), 'W_up_v': w(ks[7], D_LATENT, D_MODEL)}
    _L0_attn_in = _L0_attn_setup()

    def _L0_ffn_setup():
        import jax, jax.numpy as jnp
        import numpy as np
        DIM = 128
        HIDDEN = 384
        SCALE = 1.0 / 127.0

        def _dequant(w_int, dtype):
            return w_int.astype(dtype) * jnp.asarray(SCALE, dtype)
        key = jax.random.key(seed)
        k_x, k_g, k_u, k_d = jax.random.split(key, 4)
        x = jax.random.normal(k_x, (4, 256, DIM), dtype=jnp.float32)
        w_gate = jax.random.randint(k_g, (HIDDEN, DIM), -127, 128, dtype=jnp.int32)
        w_up = jax.random.randint(k_u, (HIDDEN, DIM), -127, 128, dtype=jnp.int32)
        w_down = jax.random.randint(k_d, (DIM, HIDDEN), -127, 128, dtype=jnp.int32)
        return {'x': x, 'w_gate': w_gate, 'w_up': w_up, 'w_down': w_down}
    _L0_ffn_in = _L0_ffn_setup()

    def _L1_attn_setup():
        import jax, jax.numpy as jnp
        import numpy as np
        import math
        BATCH, SEQLEN, DMODEL, NSTATE, DFF = (4, 256, 128, 16, 512)
        EPS = 1e-06

        def rmsnorm(x, scale):
            return x * jax.lax.rsqrt(jnp.mean(x * x, axis=-1, keepdims=True) + EPS) * scale

        def ssm_scan(u, A_ssm, B_ssm, C_ssm, D_ssm):
            dt = jnp.exp(jnp.linspace(math.log(0.001), math.log(0.1), NSTATE))
            expA = jnp.exp(A_ssm)
            dA = jnp.exp(-expA * dt)
            dB = B_ssm * (1.0 - dA) / expA

            def step(s, u_t):
                s = s * dA + u_t[..., None] * dB
                y = jnp.einsum('bdn,dn->bd', s, C_ssm)
                return (s, y)
            s0 = jnp.zeros((u.shape[0], DMODEL, NSTATE), dtype=u.dtype)
            _, ys = jax.lax.scan(step, s0, jnp.transpose(u, (1, 0, 2)))
            return jnp.transpose(ys, (1, 0, 2)) + u * D_ssm
        key = jax.random.key(seed)
        ks = jax.random.split(key, 6)
        return {'x': jax.random.normal(ks[0], (BATCH, SEQLEN, DMODEL), jnp.float32), 'A_ssm': jax.random.normal(ks[1], (DMODEL, NSTATE), jnp.float32), 'B_ssm': jax.random.normal(ks[2], (DMODEL, NSTATE), jnp.float32), 'C_ssm': jax.random.normal(ks[3], (DMODEL, NSTATE), jnp.float32), 'D_ssm': jnp.zeros((DMODEL,), jnp.float32), 'scale1': jnp.ones((DMODEL,), jnp.float32), 'scale2': jnp.ones((DMODEL,), jnp.float32), 'w1': jax.random.normal(ks[4], (DMODEL, DFF), jnp.float32) * 0.02, 'b1': jnp.zeros((DFF,), jnp.float32), 'w2': jax.random.normal(ks[5], (DFF, DMODEL), jnp.float32) * 0.02, 'b2': jnp.zeros((DMODEL,), jnp.float32)}
    _L1_attn_in = _L1_attn_setup()

    def _L1_ffn_setup():
        import jax, jax.numpy as jnp
        import numpy as np
        B, S, D, H, M, E, K = (4, 256, 128, 256, 64, 8, 2)

        def _layernorm(x, g, b, eps=1e-05):
            mu = x.mean(-1, keepdims=True)
            var = ((x - mu) ** 2).mean(-1, keepdims=True)
            return (x - mu) * jax.lax.rsqrt(var + eps) * g + b

        def _forward(inputs_embeds, enc_W, enc_b, s2c_W, s2c_b, rW1, rb1, rW2, rb2, We1, be1, We2, be2, c2s_W, c2s_b, dec_W, dec_b, ln_g, ln_b):
            b, s, _ = inputs_embeds.shape
            spikes_enc = jax.nn.sigmoid(inputs_embeds @ enc_W + enc_b)
            flat = spikes_enc.reshape(b * s, H)
            cont = flat @ s2c_W + s2c_b
            logits = jnp.tanh(cont @ rW1 + rb1) @ rW2 + rb2
            probs = jax.nn.softmax(logits, axis=-1)
            topw, topi = jax.lax.top_k(probs, K)
            w = topw / topw.sum(-1, keepdims=True)
            gates = (jax.nn.one_hot(topi, E, dtype=cont.dtype) * w[..., None]).sum(1)
            h = jax.nn.relu(jnp.einsum('nm,emh->enh', cont, We1) + be1[:, None, :])
            expert_out = jnp.einsum('enh,ehm->enm', h, We2) + be2[:, None, :]
            output_flat = jnp.einsum('enm,ne->nm', expert_out, gates)
            spikes_moe = jax.nn.sigmoid(output_flat @ c2s_W + c2s_b).reshape(b, s, H)
            decoded = jax.nn.sigmoid(spikes_moe @ dec_W + dec_b)
            return _layernorm(decoded, ln_g, ln_b)
        key = jax.random.key(seed)
        ks = jax.random.split(key, 10)
        r = lambda k, shape: jax.random.normal(k, shape, dtype=jnp.float32) * 0.02
        return {'inputs_embeds': jax.random.normal(ks[0], (B, S, D), dtype=jnp.float32), 'enc_W': r(ks[1], (D, H)), 'enc_b': jnp.zeros((H,), jnp.float32), 's2c_W': r(ks[2], (H, M)), 's2c_b': jnp.zeros((M,), jnp.float32), 'rW1': r(ks[3], (M, 64)), 'rb1': jnp.zeros((64,), jnp.float32), 'rW2': r(ks[4], (64, E)), 'rb2': jnp.zeros((E,), jnp.float32), 'We1': r(ks[5], (E, M, H // 2)), 'be1': jnp.zeros((E, H // 2), jnp.float32), 'We2': r(ks[6], (E, H // 2, M)), 'be2': jnp.zeros((E, M), jnp.float32), 'c2s_W': r(ks[7], (M, H)), 'c2s_b': jnp.zeros((H,), jnp.float32), 'dec_W': r(ks[8], (H, D)), 'dec_b': jnp.zeros((D,), jnp.float32), 'ln_g': jnp.ones((D,), jnp.float32), 'ln_b': jnp.zeros((D,), jnp.float32)}
    _L1_ffn_in = _L1_ffn_setup()
    _d = {'L0_attn_x': _L0_attn_in['x'], 'L0_attn_Wq': _L0_attn_in['Wq'], 'L0_attn_Wk': _L0_attn_in['Wk'], 'L0_attn_Wv': _L0_attn_in['Wv'], 'L0_attn_Wo': _L0_attn_in['Wo'], 'L0_attn_W_down_kv': _L0_attn_in['W_down_kv'], 'L0_attn_W_up_k': _L0_attn_in['W_up_k'], 'L0_attn_W_up_v': _L0_attn_in['W_up_v'], 'L0_ffn_w_gate': _L0_ffn_in['w_gate'], 'L0_ffn_w_up': _L0_ffn_in['w_up'], 'L0_ffn_w_down': _L0_ffn_in['w_down'], 'L1_attn_A_ssm': _L1_attn_in['A_ssm'], 'L1_attn_B_ssm': _L1_attn_in['B_ssm'], 'L1_attn_C_ssm': _L1_attn_in['C_ssm'], 'L1_attn_D_ssm': _L1_attn_in['D_ssm'], 'L1_attn_scale1': _L1_attn_in['scale1'], 'L1_attn_scale2': _L1_attn_in['scale2'], 'L1_attn_w1': _L1_attn_in['w1'], 'L1_attn_b1': _L1_attn_in['b1'], 'L1_attn_w2': _L1_attn_in['w2'], 'L1_attn_b2': _L1_attn_in['b2'], 'L1_ffn_enc_W': _L1_ffn_in['enc_W'], 'L1_ffn_enc_b': _L1_ffn_in['enc_b'], 'L1_ffn_s2c_W': _L1_ffn_in['s2c_W'], 'L1_ffn_s2c_b': _L1_ffn_in['s2c_b'], 'L1_ffn_rW1': _L1_ffn_in['rW1'], 'L1_ffn_rb1': _L1_ffn_in['rb1'], 'L1_ffn_rW2': _L1_ffn_in['rW2'], 'L1_ffn_rb2': _L1_ffn_in['rb2'], 'L1_ffn_We1': _L1_ffn_in['We1'], 'L1_ffn_be1': _L1_ffn_in['be1'], 'L1_ffn_We2': _L1_ffn_in['We2'], 'L1_ffn_be2': _L1_ffn_in['be2'], 'L1_ffn_c2s_W': _L1_ffn_in['c2s_W'], 'L1_ffn_c2s_b': _L1_ffn_in['c2s_b'], 'L1_ffn_dec_W': _L1_ffn_in['dec_W'], 'L1_ffn_dec_b': _L1_ffn_in['dec_b'], 'L1_ffn_ln_g': _L1_ffn_in['ln_g'], 'L1_ffn_ln_b': _L1_ffn_in['ln_b']}
    _x0 = _d['L0_attn_x']
    _d['L0_attn_x'] = jax.random.normal(jax.random.fold_in(jax.random.key(seed), 1), (16, 512, 128), dtype=_x0.dtype)
    del _x0
    return _d

def reference(L0_attn_x, L0_attn_Wq, L0_attn_Wk, L0_attn_Wv, L0_attn_Wo, L0_attn_W_down_kv, L0_attn_W_up_k, L0_attn_W_up_v, L0_ffn_w_gate, L0_ffn_w_up, L0_ffn_w_down, L1_attn_A_ssm, L1_attn_B_ssm, L1_attn_C_ssm, L1_attn_D_ssm, L1_attn_scale1, L1_attn_scale2, L1_attn_w1, L1_attn_b1, L1_attn_w2, L1_attn_b2, L1_ffn_enc_W, L1_ffn_enc_b, L1_ffn_s2c_W, L1_ffn_s2c_b, L1_ffn_rW1, L1_ffn_rb1, L1_ffn_rW2, L1_ffn_rb2, L1_ffn_We1, L1_ffn_be1, L1_ffn_We2, L1_ffn_be2, L1_ffn_c2s_W, L1_ffn_c2s_b, L1_ffn_dec_W, L1_ffn_dec_b, L1_ffn_ln_g, L1_ffn_ln_b):

    def _L0_attn_ref(x, Wq, Wk, Wv, Wo, W_down_kv, W_up_k, W_up_v):
        import jax, jax.numpy as jnp
        import numpy as np
        D_MODEL = 128
        N_HEADS = 16
        HEAD_DIM = D_MODEL // N_HEADS
        D_LATENT = 32
        LAMBDA_DECAY = 0.01
        TIME_STEP = 0.01
        CLAMP = 10000.0

        def _reference_tuple_inner(x, Wq, Wk, Wv, Wo, W_down_kv, W_up_k, W_up_v):
            B, S, _ = x.shape
            q = x @ Wq
            k = x @ Wk
            v = x @ Wv
            latent_kv = (k + v) @ W_down_kv
            k_rec = latent_kv @ W_up_k
            v_rec = latent_kv @ W_up_v

            def heads(t):
                return t.reshape(B, S, N_HEADS, HEAD_DIM).transpose(0, 2, 1, 3)
            qh, kh, vh = (heads(q), heads(k_rec), heads(v_rec))
            scale = 1.0 / (jnp.sqrt(jnp.float32(D_MODEL)) + 1e-08)
            scores = jnp.einsum('bhqd,bhkd->bhqk', qh, kh) * scale
            scores = jnp.clip(jnp.nan_to_num(scores, nan=-1000000000.0), -CLAMP, CLAMP)
            idx = jnp.arange(S, dtype=jnp.float32)
            decay = jnp.exp(-LAMBDA_DECAY * TIME_STEP * jnp.abs(idx[:, None] - idx[None, :]))
            scores = scores * decay[None, None, :, :]
            scores = jnp.clip(jnp.nan_to_num(scores, nan=-1000000000.0), -CLAMP, CLAMP)
            attn = jax.nn.softmax(scores, axis=-1)
            out = jnp.einsum('bhqk,bhkd->bhqd', attn, vh)
            out = out.transpose(0, 2, 1, 3).reshape(B, S, D_MODEL)
            return (out @ Wo, latent_kv)
        return _reference_tuple_inner(x, Wq, Wk, Wv, Wo, W_down_kv, W_up_k, W_up_v)[0]

    def _L0_ffn_ref(x, w_gate, w_up, w_down):
        import jax, jax.numpy as jnp
        import numpy as np
        DIM = 128
        HIDDEN = 384
        SCALE = 1.0 / 127.0

        def _dequant(w_int, dtype):
            return w_int.astype(dtype) * jnp.asarray(SCALE, dtype)
        wg = _dequant(w_gate, x.dtype)
        wu = _dequant(w_up, x.dtype)
        wd = _dequant(w_down, x.dtype)
        gate = jnp.einsum('bsd,hd->bsh', x, wg)
        up = jnp.einsum('bsd,hd->bsh', x, wu)
        h = jax.nn.silu(gate) * up
        return jnp.einsum('bsh,dh->bsd', h, wd)

    def _L1_attn_ref(x, A_ssm, B_ssm, C_ssm, D_ssm, scale1, scale2, w1, b1, w2, b2):
        import jax, jax.numpy as jnp
        import numpy as np
        import math
        BATCH, SEQLEN, DMODEL, NSTATE, DFF = (4, 256, 128, 16, 512)
        EPS = 1e-06

        def rmsnorm(x, scale):
            return x * jax.lax.rsqrt(jnp.mean(x * x, axis=-1, keepdims=True) + EPS) * scale

        def ssm_scan(u, A_ssm, B_ssm, C_ssm, D_ssm):
            dt = jnp.exp(jnp.linspace(math.log(0.001), math.log(0.1), NSTATE))
            expA = jnp.exp(A_ssm)
            dA = jnp.exp(-expA * dt)
            dB = B_ssm * (1.0 - dA) / expA

            def step(s, u_t):
                s = s * dA + u_t[..., None] * dB
                y = jnp.einsum('bdn,dn->bd', s, C_ssm)
                return (s, y)
            s0 = jnp.zeros((u.shape[0], DMODEL, NSTATE), dtype=u.dtype)
            _, ys = jax.lax.scan(step, s0, jnp.transpose(u, (1, 0, 2)))
            return jnp.transpose(ys, (1, 0, 2)) + u * D_ssm
        x = x + ssm_scan(rmsnorm(x, scale1), A_ssm, B_ssm, C_ssm, D_ssm)
        h = rmsnorm(x, scale2)
        h = jax.nn.gelu(h @ w1 + b1, approximate=False) @ w2 + b2
        return x + h

    def _L1_ffn_ref(inputs_embeds, enc_W, enc_b, s2c_W, s2c_b, rW1, rb1, rW2, rb2, We1, be1, We2, be2, c2s_W, c2s_b, dec_W, dec_b, ln_g, ln_b):
        import jax, jax.numpy as jnp
        import numpy as np
        B, S, D, H, M, E, K = (4, 256, 128, 256, 64, 8, 2)

        def _layernorm(x, g, b, eps=1e-05):
            mu = x.mean(-1, keepdims=True)
            var = ((x - mu) ** 2).mean(-1, keepdims=True)
            return (x - mu) * jax.lax.rsqrt(var + eps) * g + b

        def _forward(inputs_embeds, enc_W, enc_b, s2c_W, s2c_b, rW1, rb1, rW2, rb2, We1, be1, We2, be2, c2s_W, c2s_b, dec_W, dec_b, ln_g, ln_b):
            b, s, _ = inputs_embeds.shape
            spikes_enc = jax.nn.sigmoid(inputs_embeds @ enc_W + enc_b)
            flat = spikes_enc.reshape(b * s, H)
            cont = flat @ s2c_W + s2c_b
            logits = jnp.tanh(cont @ rW1 + rb1) @ rW2 + rb2
            probs = jax.nn.softmax(logits, axis=-1)
            topw, topi = jax.lax.top_k(probs, K)
            w = topw / topw.sum(-1, keepdims=True)
            gates = (jax.nn.one_hot(topi, E, dtype=cont.dtype) * w[..., None]).sum(1)
            h = jax.nn.relu(jnp.einsum('nm,emh->enh', cont, We1) + be1[:, None, :])
            expert_out = jnp.einsum('enh,ehm->enm', h, We2) + be2[:, None, :]
            output_flat = jnp.einsum('enm,ne->nm', expert_out, gates)
            spikes_moe = jax.nn.sigmoid(output_flat @ c2s_W + c2s_b).reshape(b, s, H)
            decoded = jax.nn.sigmoid(spikes_moe @ dec_W + dec_b)
            return _layernorm(decoded, ln_g, ln_b)
        return _forward(inputs_embeds, enc_W, enc_b, s2c_W, s2c_b, rW1, rb1, rW2, rb2, We1, be1, We2, be2, c2s_W, c2s_b, dec_W, dec_b, ln_g, ln_b)
    x = L0_attn_x
    x = x + _layernorm(_L0_attn_ref(_layernorm(x, axis=-1), L0_attn_Wq, L0_attn_Wk, L0_attn_Wv, L0_attn_Wo, L0_attn_W_down_kv, L0_attn_W_up_k, L0_attn_W_up_v), axis=-1)
    x = x + _layernorm(_L0_ffn_ref(_layernorm(x, axis=-1), L0_ffn_w_gate, L0_ffn_w_up, L0_ffn_w_down), axis=-1)
    x = x + _layernorm(_L1_attn_ref(_layernorm(x, axis=-1), L1_attn_A_ssm, L1_attn_B_ssm, L1_attn_C_ssm, L1_attn_D_ssm, L1_attn_scale1, L1_attn_scale2, L1_attn_w1, L1_attn_b1, L1_attn_w2, L1_attn_b2), axis=-1)
    x = x + _layernorm(_L1_ffn_ref(_layernorm(x, axis=-1), L1_ffn_enc_W, L1_ffn_enc_b, L1_ffn_s2c_W, L1_ffn_s2c_b, L1_ffn_rW1, L1_ffn_rb1, L1_ffn_rW2, L1_ffn_rb2, L1_ffn_We1, L1_ffn_be1, L1_ffn_We2, L1_ffn_be2, L1_ffn_c2s_W, L1_ffn_c2s_b, L1_ffn_dec_W, L1_ffn_dec_b, L1_ffn_ln_g, L1_ffn_ln_b), axis=-1)
    return x

_drawn_inputs = setup_inputs


def setup_inputs(seed=0):
    import zlib

    import numpy as np

    out = dict(_drawn_inputs(seed))
    spreads = {'L1_attn_D_ssm': (0.0, 0.1),
     'L1_attn_scale1': (1.0, 0.2),
     'L1_attn_scale2': (1.0, 0.6),
     'L1_attn_b1': (0.0, 0.8),
     'L1_attn_b2': (0.0, 0.1),
     'L1_ffn_enc_b': (0.0, 0.8),
     'L1_ffn_s2c_b': (0.0, 0.8),
     'L1_ffn_rb1': (0.0, 0.8),
     'L1_ffn_rb2': (0.0, 0.8),
     'L1_ffn_be1': (0.0, 0.8),
     'L1_ffn_be2': (0.0, 0.8),
     'L1_ffn_c2s_b': (0.0, 0.467),
     'L1_ffn_dec_b': (0.0, 0.1),
     'L1_ffn_ln_g': (1.0, 0.2),
     'L1_ffn_ln_b': (0.0, 0.1)}
    factors = {'L0_attn_Wq': 52.023,
     'L0_attn_W_up_k': 49.705,
     'L1_attn_w1': 3.179,
     'L1_attn_w2': 2.909,
     'L1_ffn_enc_W': 8.0,
     'L1_ffn_s2c_W': 8.0,
     'L1_ffn_rW1': 8.0,
     'L1_ffn_rW2': 8.0,
     'L1_ffn_We1': 8.0,
     'L1_ffn_We2': 8.0,
     'L1_ffn_c2s_W': 8.0}
    for name, (base, spread) in spreads.items():
        noise = np.random.default_rng([zlib.crc32(name.encode()), seed]).standard_normal(out[name].shape)
        drawn = base * np.exp(spread * noise) if base else spread * noise
        out[name] = jnp.asarray(drawn.astype(out[name].dtype))
    for name, factor in factors.items():
        out[name] = (out[name] * factor).astype(out[name].dtype)
    return out
```

```python
import math
from contextlib import ExitStack

import concourse.bass as bass
from concourse import mybir

F32 = mybir.dt.float32
BF16 = mybir.dt.bfloat16
I32 = mybir.dt.int32
ALU = mybir.AluOpType
ACT = mybir.ActivationFunctionType
AX = mybir.AxisListType

P = 128
D = 128
HEADS, HD = 16, 8
LATENT = 32
SLOTS = 6
SPLIT = ((0, 0), (0, 1), (0, 2), (1, 0), (1, 1), (2, 0))
VC = 32
CEILING = 60.0
QSCALE = 1.0 / (float(D) ** 0.5 + 1e-8)


class Tally:

    def __init__(self, eng, sem, per=0, start=0):
        self.eng, self.sem, self.per, self.start, self.turn, self.n = eng, sem, per, start, 0, 0

    def begin(self, turn):
        assert self.n in (0, self.per), (self.n, self.per)
        self.turn, self.n = turn, 0

    def mark(self, ins):
        ins.then_inc(self.sem, 1)
        self.n += 1

    def settle(self):
        self.eng.wait_ge(self.sem, self.turn * self.per + (self.start + self.n))

    def step(self, ins):
        self.mark(ins)
        self.settle()


class Core:

    def __init__(self, nc, ctx, B, NT):
        self.nc, self.ctx, self.B, self.NT, self.T = nc, ctx, B, NT, NT * P
        sb = lambda n, s, d=F32: ctx.enter_context(nc.sbuf_tensor(n, s, d))
        XY = sb("XY", [P, 2 * B + 1, NT, D])
        self.X, self.Y = XY[:, 0:B + 1], XY[:, B:2 * B + 1]
        self.xmean = sb("xmean", [P, B + 1, NT])
        self.xrstd = sb("xrstd", [P, B + 1, NT])
        self.urstd = sb("urstd", [P, B + 1, NT])
        self.xst = sb("xst", [P, B, NT, 6])
        self.yst = sb("yst", [P, B + 1, NT, 6])
        self.inv = sb("inv", [P, HEADS // 4 * B + 1, NT, 4])
        self.in_range = sb("in_range", [P, 1], I32)
        self.ident = sb("ident", [P, P])
        self.ones = sb("ones", [P, P])
        self.Wq, self.Wkr, self.Wvr, self.Wo = (sb(n, [D, D]) for n in ("Wq", "Wkr", "Wvr", "Wo"))
        self.turns = self.sem("turns")

    def sem(self, name):
        return self.ctx.enter_context(self.nc.semaphore(name))


def moments(v, tick, st, mean, var, tmp):
    tick.mark(v.tensor_tensor(mean, st[..., 1], st[..., 4], ALU.add))
    tick.mark(v.tensor_tensor(var, st[..., 2], st[..., 5], ALU.add))
    tick.step(v.tensor_tensor(tmp, st[..., 1], st[..., 4], ALU.subtract))
    tick.step(v.tensor_tensor(tmp, tmp, tmp, ALU.mult))
    tick.mark(v.tensor_scalar(mean, mean, 0.5, None, ALU.mult))
    tick.step(v.tensor_scalar(tmp, tmp, 0.25, None, ALU.mult))
    tick.step(v.scalar_tensor_tensor(var, var, 1.0 / D, tmp, ALU.mult, ALU.add))


def setup(core, I):
    nc, B, NT = core.nc, core.B, core.NT
    with ExitStack() as ctx:
        sb = lambda n, s, d=F32: ctx.enter_context(nc.sbuf_tensor(n, s, d))
        wk, wv, wks = sb("wk", [D, D]), sb("wv", [D, D]), sb("wks", [D, D])
        wsT = sb("wsT", [D, D])
        wd = sb("wd", [D, LATENT])
        wuk, wuv = sb("wuk", [LATENT, D]), sb("wuv", [LATENT, D])
        mT = sb("mT", [LATENT, D])
        wqr = sb("wqr", [D, D])
        tmp, var = sb("s_tmp", [P, B, NT]), sb("s_var", [P, B, NT])
        ps = ctx.enter_context(nc.psum_tensor("s_ps", [P, 4, 512], F32))
        xload, wload = core.sem("xload"), core.sem("wload")
        made, ident_done, tick_s = core.sem("setup_made"), core.sem("ident_done"), core.sem("setup_dve")
        on_pe, rooted = core.sem("setup_pe"), core.sem("setup_root")
        half = B // 2
        xv = I["L0_attn_x"].rearrange("b (c p) d -> p b c d", p=P)
        block = ctx.enter_context(nc.Block())

        @block.sync
        def _(sp):
            for n in range(2):
                for b in range(n * half, (n + 1) * half):
                    sp.dma_start(core.X[:, b], xv[:, b]).then_inc(xload, 16)
            sp.wait_ge(xload, 16 * B)

        @block.gpsimd
        def _(pool):
            pool.memset(core.ident[:], 0.0).then_inc(ident_done, 1)
            pool.memset(core.ones[:], 1.0).then_inc(ident_done, 1)
            pool.wait_ge(ident_done, 2)
            pool.affine_select(out=core.ident[:], in_=core.ident[:], compare_op=ALU.not_equal, fill=1.0,
                               base=0, pattern=[[-1, P]], channel_multiplier=1).then_inc(ident_done, 1)
            pool.memset(core.X[:, B], 0.0).then_inc(ident_done, 1)
            pool.memset(core.xmean[:, B], 0.0).then_inc(ident_done, 1)
            pool.memset(core.xrstd[:, B], 0.0).then_inc(ident_done, 1)
            pool.memset(core.urstd[:, B], 0.0).then_inc(ident_done, 1)

        @block.scalar
        def _(act):
            for dst, name in ((wk, "Wk"), (wv, "Wv"), (wd, "W_down_kv"), (wuk, "W_up_k"), (wuv, "W_up_v"),
                              (wqr, "Wq"), (core.Wo, "Wo")):
                act.dma_start(dst[:], I["L0_attn_" + name]).then_inc(wload, 16)
            act.wait_ge(tick_s, 2 + B * NT + 8)
            act.activation(core.xrstd[:, 0:B], core.xrstd[:, 0:B], ACT.Sqrt).then_inc(rooted, 1)

        @block.tensor
        def _(pe):
            pe.wait_ge(ident_done, 3)
            pe.wait_ge(tick_s, 2)
            pe.transpose(ps[:, 0, 0:D], wks[:], core.ident[:]).then_inc(on_pe, 1)
            pe.wait_ge(made, 1)
            pe.matmul(ps[0:LATENT, 1, 0:D], wd[:], wsT[:], start=True, stop=True).then_inc(on_pe, 1)
            pe.wait_ge(made, 2)
            pe.matmul(ps[:, 2, 0:D], mT[:], wuk[:], start=True, stop=True)
            pe.matmul(ps[:, 3, 0:D], mT[:], wuv[:], start=True, stop=True).then_inc(on_pe, 1)

        @block.vector
        def _(v):
            tick = Tally(v, tick_s)
            v.wait_ge(wload, 16 * 7)
            tick.mark(v.tensor_scalar(core.Wq[:], wqr[:], QSCALE, None, ALU.mult))
            tick.mark(v.tensor_tensor(wks[:], wk[:], wv[:], ALU.add))
            v.wait_ge(on_pe, 1)
            v.tensor_copy(wsT[:], ps[:, 0, 0:D]).then_inc(made, 1)
            v.wait_ge(on_pe, 2)
            v.tensor_copy(mT[:], ps[0:LATENT, 1, 0:D]).then_inc(made, 1)
            v.wait_ge(on_pe, 3)
            v.tensor_copy(core.Wkr[:], ps[:, 2, 0:D]).then_inc(made, 1)
            v.tensor_copy(core.Wvr[:], ps[:, 3, 0:D]).then_inc(made, 1)
            v.wait_ge(xload, 16 * B)
            for b in range(B):
                for c in range(NT):
                    tick.mark(v.bn_stats(core.xst[:, b, c], core.X[:, b, c]))
            tick.settle()
            moments(v, tick, core.xst[:], core.xmean[:, 0:B], var[:], tmp[:])
            tick.step(v.tensor_scalar(core.xrstd[:, 0:B], var[:], 1e-5, None, ALU.add))
            v.wait_ge(rooted, 1)
            tick.step(v.reciprocal(core.xrstd[:, 0:B], core.xrstd[:, 0:B]))


def attention(core, I):
    nc, B, NT, T = core.nc, core.B, core.NT, core.T
    HG = HEADS // 4
    STEPS = 2 * HG
    X, Y = core.X, core.Y
    with ExitStack() as ctx:
        sb = lambda n, s, d=F32: ctx.enter_context(nc.sbuf_tensor(n, s, d))
        psum = lambda n: ctx.enter_context(nc.psum_tensor(n, [P, 512], F32))
        decay = sb("a_decay", [P, T + (NT - 1) * P])
        Qs = [sb(f"Qs{p}", [SLOTS * HD, HEADS, T], BF16) for p in range(2)]
        Ks = [sb(f"Ks{p}", [SLOTS * HD, HEADS, T], BF16) for p in range(2)]
        V = [sb(f"V{p}", [P, NT, HEADS, VC]) for p in range(2)]
        probs = sb("probs", [P, 2, 4, 2, T])
        xnT = sb("a_xnT", [D, T])
        parts = [sb("qparts", [D, 3, T], BF16), sb("kparts", [D, 3, T], BF16)]
        heads_out = sb("heads_out", [P, NT, D])
        rest = sb("a_rest", [D, T])
        heads_outT = rest
        Osb = sb("Osb", [P, T])
        xn = Osb[:].rearrange("p (c d) -> p c d", c=NT)
        one_over = sb("one_over", [P, NT, 4])
        S = [ctx.enter_context(nc.psum_tensor(f"S{i}", [P, 2, 512], F32)) for i in range(2)]
        O = [psum(f"O{i}") for i in range(2)]
        OT, M = psum("OT"), psum("M")
        dram = [nc.dram_tensor(f"{n}_parts", [D, 3, T], BF16, kind="Internal").ap() for n in "qk"]

        sem = lambda n: core.sem("a_" + n)
        const, init, xn_done = sem("const"), sem("init"), sem("xn_done")
        m_full, m_free = sem("m_full"), sem("m_free")
        first_part = [sem("q_first"), sem("k_first")]
        low = [sem("q_low"), sem("k_low")]
        stored, spread = [sem("q_stored"), sem("k_stored")], [sem("q_spread"), sem("k_spread")]
        s_full, decayed, exped, pv_done = sem("s_full"), sem("decayed"), sem("exped"), sem("pv_done")
        o_free, ot_full, inverted, heads_done = sem("o_free"), sem("ot_full"), sem("inverted"), sem("heads_done")
        second_part = sem("second_part")
        block = ctx.enter_context(nc.Block())

        FIRST = dict(xT=1, q=2, k=3, v=4)
        USES = dict(xT=1, headsT=2, rows=3, q=4, k=5, v=6)
        base_of = lambda t: t * 6 + 4

        def pairs(eng, body):
            with eng.Fori(0, B - 1, 2) as i:
                for p in range(2):
                    body(i + p, p)

        @block.sync
        def _(sp):
            sp.dma_start(decay[:], I["decay"]).then_inc(const, 16)

            def spread_parts(u, p, first=False):
                for w in range(2):
                    sp.wait_ge(low[w], u + 1)
                    sp.sem_inc(core.turns, 1)
                    if not first:
                        sp.wait_ge(spread[w], 16 * SLOTS * u)
                    sp.dma_start(dram[w], parts[w][:]).then_inc(stored[w], 16)
                    sp.wait_ge(stored[w], 16 * u + 16)
                    for s in range(SLOTS):
                        src = dram[w][:, SPLIT[s][w], :].rearrange("(h d) t -> d h t", d=HD)
                        sp.dma_start((Qs, Ks)[w][p][s * HD:(s + 1) * HD], src).then_inc(spread[w], 16)

            spread_parts(0, 0, first=True)
            pairs(sp, lambda t, p: spread_parts(t + 1, 1 - p))
            for w in range(2):
                sp.wait_ge(spread[w], 16 * SLOTS * (B + 1))

        @block.gpsimd
        def _(pool):
            pool.memset(heads_out[:], 0.0).then_inc(init, 1)
            for p in range(2):
                pool.memset(V[p][:, :, :, 0:HD], 0.0).then_inc(init, 1)
                pool.memset(V[p][:, :, :, HD:HD + 1], 1.0).then_inc(init, 1)
                pool.memset(V[p][:, :, :, HD + 1:VC], 0.0).then_inc(init, 1)
                pool.memset(probs[:, p], 1.0).then_inc(init, 1)

            def lower(u, base, use):
                for w, name in enumerate("qk"):
                    pool.wait_ge(m_free, base + use[name] + 1)
                    pool.sem_inc(core.turns, 1)
                    pool.tensor_copy(parts[w][:, 1], rest[:]).then_inc(second_part, 1)
                    pool.wait_ge(second_part, 2 * u + (w + 1))
                    pool.tensor_tensor(parts[w][:, 2], rest[:], parts[w][:, 1], ALU.subtract).then_inc(low[w], 1)

            lower(0, 0, FIRST)
            pairs(pool, lambda t, p: lower(t + 1, base_of(t), USES))

        @block.scalar
        def _(act):
            act.preload_act_table(ACT.Exp)
            act.sem_inc(exped, 4)

            def body(t, p):
                for g in range(STEPS):
                    for j in range(4):
                        act.wait_ge(decayed, t * (4 * STEPS) + (4 * g + j + 3))
                        pr = probs[:, g % 2, j]
                        act.activation(pr, pr, ACT.Exp).then_inc(exped, 1)

            pairs(act, body)

        @block.tensor
        def _(pe):
            def scores(g, j, p):
                for kk in range(2):
                    kb, h = 2 * (g % 2) + kk, 4 * (g // 2) + j
                    mm = pe.matmul(S[j % 2][:, kk, :], Ks[p][:, h, kb * P:(kb + 1) * P], Qs[p][:, h, :],
                                   start=True, stop=True)
                mm.then_inc(s_full, 1)

            def values(g, half, p):
                kb = 2 * (g % 2) + half
                for j in range(4):
                    mm = pe.matmul(O[g // 2 % 2][VC * j:VC * (j + 1), :], V[p][:, kb, 4 * (g // 2) + j, :],
                                   probs[:, g % 2, j, half, :], start=(kb == 0), stop=(kb == NT - 1),
                                   skip_group_check=True)
                return mm

            def use_M(n, emit):
                pe.wait_ge(m_free, n)
                emit().then_inc(m_full, 1)

            def tiles_T(src):
                for c in range(NT):
                    mm = pe.transpose(M[:, c * P:(c + 1) * P], src[:, c, :], core.ident[:])
                return mm

            def rows(lhsT, w):
                for c in range(NT):
                    mm = pe.matmul(M[:, c * P:(c + 1) * P], lhsT[:, c * P:(c + 1) * P], w[:],
                                   start=True, stop=True)
                return mm

            def x_T(u, n):
                pe.wait_ge(xn_done, u + 1)
                use_M(n, lambda: tiles_T(xn))

            def project(w, n):
                use_M(n, lambda: pe.matmul(M[:], w[:], xnT[:], start=True, stop=True))

            def out_T(y):
                pe.wait_ge(o_free, y + 3)
                pe.wait_ge(heads_done, y + 2)
                for c in range(NT):
                    mm = pe.transpose(OT[:, c * P:(c + 1) * P], Osb[:, c * P:(c + 1) * P], core.ident[:])
                mm.then_inc(ot_full, 1)

            def heads_T(b, n):
                pe.wait_ge(heads_done, b * HG + (HG + 2))
                use_M(n, lambda: tiles_T(heads_out))

            pe.sem_inc(m_free, 1)
            pe.sem_inc(pv_done, 1)
            x_T(0, 1)
            project(core.Wq, 2)
            project(core.Wkr, 3)
            use_M(4, lambda: rows(xnT, core.Wvr))
            pe.wait_ge(m_free, 5)
            pe.wait_ge(init, 9)
            for half in range(2):
                values(STEPS - 2, half, 1)

            def body(t, p):
                base = base_of(t)
                for g in range(STEPS):
                    G = t * STEPS + g
                    for j in range(4):
                        if g == 0 and j == 0:
                            for w in range(2):
                                pe.wait_ge(spread[w], t * (16 * SLOTS) + 16 * SLOTS)
                        pe.wait_ge(decayed, t * (4 * STEPS) + (4 * g + j + 1))
                        scores(g, j, p)
                        if j == 0 and g == 2:
                            x_T(t + 1, base + USES["xT"])
                        if j == 1:
                            if g == 2:
                                heads_T(t - 1, base + USES["headsT"])
                            if g == 3:
                                use_M(base + USES["rows"], lambda: rows(heads_outT, core.Wo))
                            if g == 4:
                                project(core.Wq, base + USES["q"])
                            if g == 5:
                                project(core.Wkr, base + USES["k"])
                            if g == 6:
                                use_M(base + USES["v"], lambda: rows(xnT, core.Wvr))
                        if j == 2:
                            pe.wait_ge(exped, G * 4 + 4)
                            if g % 2:
                                pe.wait_ge(o_free, t * HG + (g // 2 + 1))
                            values((g - 1) % STEPS, 0, p if g else 1 - p)
                            if g % 2:
                                out_T(t * HG + (g // 2 - 1))
                        if j == 3:
                            values((g - 1) % STEPS, 1, p if g else 1 - p).then_inc(pv_done, 1)

            pairs(pe, body)
            pe.wait_ge(exped, 4 * STEPS * B + 4)
            for half in range(2):
                mm = values(STEPS - 1, half, (B - 1) % 2)
            mm.then_inc(pv_done, 1)
            out_T(HG * B - 1)
            heads_T(B - 1, base_of(B) + 1)
            use_M(base_of(B) + 2, lambda: rows(heads_outT, core.Wo))

        @block.vector
        def _(v):
            v.sem_inc(decayed, 2)
            v.sem_inc(o_free, 1)
            v.sem_inc(heads_done, 1)

            def layer_norm(u):
                for c in range(NT):
                    op = v.tensor_scalar(xn[:, c], X[:, u, c], core.xmean[:, u, c:c + 1],
                                         core.xrstd[:, u, c:c + 1], ALU.subtract, ALU.mult)
                op.then_inc(xn_done, 1)

            def take_copy(n, dst):
                v.wait_ge(m_full, n)
                v.tensor_copy(dst, M[:]).then_inc(m_free, 1)

            def take_parts(n, w, u, first=False):
                v.wait_ge(m_full, n)
                if not first:
                    v.wait_ge(stored[w], 16 * u)
                v.tensor_copy(parts[w][:, 0], M[:]).then_inc(first_part[w], 1)
                v.wait_ge(first_part[w], u + 1)
                if w == 1:
                    v.wait_ge(low[0], u + 1)
                elif not first:
                    v.wait_ge(low[1], u)
                v.tensor_tensor(rest[:], M[:], parts[w][:, 0], ALU.subtract).then_inc(m_free, 1)

            def take_values(n, p):
                v.wait_ge(m_full, n)
                v.tensor_copy(V[p][:, :, :, 0:HD], M[:].rearrange("p (c h d) -> p c h d", c=NT, d=HD))\
                    .then_inc(m_free, 1)

            def evacuate(y, par):
                v.wait_ge(pv_done, y * 2 + 4)
                v.tensor_copy(Osb[:], O[par][:]).then_inc(o_free, 1)

            def normalise(y, hg):
                v.wait_ge(ot_full, y + 2)
                ot = OT[:].rearrange("p (c j e) -> p c j e", c=NT, j=4)
                v.tensor_scalar(one_over[:], ot[:, :, :, HD], 1e-30, None, ALU.max).then_inc(inverted, 1)
                v.wait_ge(inverted, y * 3 + 4)
                v.reciprocal(one_over[:], one_over[:]).then_inc(inverted, 1)
                v.wait_ge(inverted, y * 3 + 5)
                dst = heads_out[:, :, hg * 4 * HD:(hg + 1) * 4 * HD].rearrange("p c (j d) -> p c j d", d=HD)
                v.tensor_tensor(dst, ot[:, :, :, 0:HD], one_over[:].unsqueeze(3).to_broadcast([P, NT, 4, HD]),
                                ALU.mult).then_inc(heads_done, 1)
                v.tensor_copy(core.inv[:, y + 1], one_over[:]).then_inc(inverted, 1)

            def take_rows(b, n):
                v.wait_ge(m_full, n)
                v.tensor_copy(Y[:, b + 1].rearrange("p c d -> p (c d)"), M[:])
                for c in range(NT):
                    op = v.bn_stats(core.yst[:, b + 1, c], M[:, c * P:(c + 1) * P])
                op.then_inc(m_free, 1)

            layer_norm(0)
            take_copy(1, xnT[:])
            take_parts(2, 0, 0, first=True)
            take_parts(3, 1, 0, first=True)
            v.wait_ge(init, 9)
            take_values(4, 0)
            v.wait_ge(const, 16)
            full = decay[:]
            decay_of = [bass.AP(full.tensor, full.offset + (NT - 1 - 2 * m) * P, [list(full.ap[0]), [-P, 2], [1, T]])
                        for m in range(2)]

            def body(t, p):
                base = base_of(t)
                for g in range(STEPS):
                    for j in range(4):
                        if j == 0:
                            v.wait_ge(pv_done, t * STEPS + (g + 1))
                        v.wait_ge(s_full, t * (4 * STEPS) + (4 * g + j + 1))
                        v.scalar_tensor_tensor(probs[:, g % 2, j], S[j % 2][:], CEILING, decay_of[g % 2], ALU.min,
                                               ALU.mult).then_inc(decayed, 1)
                        if j == 0 and g % 2:
                            evacuate(t * HG + (g // 2 - 1), (g // 2 - 1) % 2)
                        if j == 1 and g == 2:
                            take_copy(base + USES["xT"], xnT[:])
                        if j == 2:
                            if g == 2:
                                v.wait_ge(low[1], t + 1)
                                take_copy(base + USES["headsT"], heads_outT[:])
                            if g == 3:
                                take_rows(t - 1, base + USES["rows"])
                            if g == 4:
                                take_parts(base + USES["q"], 0, t + 1)
                            if g == 5:
                                take_parts(base + USES["k"], 1, t + 1)
                            if g == 6:
                                take_values(base + USES["v"], 1 - p)
                        if j == 3 and g % 2:
                            normalise(t * HG + (g // 2 - 1), (g // 2 - 1) % HG)
                        if j == 3 and g == 1:
                            layer_norm(t + 1)

            pairs(v, body)
            evacuate(HG * B - 1, (HG - 1) % 2)
            normalise(HG * B - 1, HG - 1)
            v.wait_ge(low[1], B + 1)
            take_copy(base_of(B) + 1, heads_outT[:])
            take_rows(B - 1, base_of(B) + 2)


def check_range(core):
    nc = core.nc
    with ExitStack() as ctx:
        r = core.inv[:, 1:].rearrange("p y c j -> p (y c j)")
        above, below = (ctx.enter_context(nc.sbuf_tensor(n, list(r.shape), F32)) for n in ("r_above", "r_below"))
        least, fine = (ctx.enter_context(nc.sbuf_tensor(n, [P, 1], F32)) for n in ("r_least", "r_fine"))
        count = ctx.enter_context(nc.psum_tensor("r_count", [P, 1], F32))
        steps, least_done, counted = core.sem("r_steps"), core.sem("r_least_done"), core.sem("r_counted")
        known = core.sem("r_known")
        block = ctx.enter_context(nc.Block())

        @block.sync
        def _(sp):
            sp.wait_ge(known, 1)

        @block.gpsimd
        def _(pool):
            pool.wait_ge(known, 1)

        @block.scalar
        def _(act):
            act.wait_ge(known, 1)

        @block.tensor
        def _(pe):
            pe.wait_ge(least_done, 1)
            pe.matmul(count[:], core.ones[:], least[:], start=True, stop=True).then_inc(counted, 1)
            pe.wait_ge(known, 1)

        @block.vector
        def _(v):
            tick = Tally(v, steps)
            tick.mark(v.tensor_scalar(above[:], r, 2.0 ** -60, None, ALU.is_ge))
            tick.step(v.tensor_scalar(below[:], r, 2.0 ** 60, None, ALU.is_le))
            tick.step(v.tensor_tensor(above[:], above[:], below[:], ALU.mult))
            v.tensor_reduce(least[:], above[:], AX.X, ALU.min).then_inc(least_done, 1)
            v.wait_ge(counted, 1)
            tick.step(v.tensor_scalar(fine[:], count[:], float(P), None, ALU.is_equal))
            v.tensor_copy(core.in_range[:], fine[:]).then_inc(known, 1)
            v.wait_ge(known, 1)


def attention_guarded(core, I):
    nc, B, NT, T = core.nc, core.B, core.NT, core.T
    X, Y = core.X, core.Y
    with ExitStack() as ctx:
        sb = lambda n, s, d=F32: ctx.enter_context(nc.sbuf_tensor("c_" + n, s, d))
        psum = lambda n, s: ctx.enter_context(nc.psum_tensor("c_" + n, s, F32))
        decay = sb("decay", [P, T + (NT - 1) * P])
        xn, xnT = sb("xn", [P, NT, D]), sb("xnT", [D, T])
        qT, kT = sb("qT", [D, T]), sb("kT", [D, T])
        q8, k8 = sb("q8", [HD, HEADS, T]), sb("k8", [HD, HEADS, T])
        qh, kh = sb("qh", [HD, T]), sb("kh", [HD, T])
        V = sb("V", [P, NT, D])
        probs, probsT = sb("probs", [P, T]), sb("probsT", [P, NT, P])
        top, total = sb("top", [P, 1]), sb("total", [P, 1])
        heads_out, heads_outT = sb("heads_out", [P, NT, D]), sb("heads_outT", [D, T])
        M, O = psum("M", [P, 512]), psum("O", [P, HD])
        dram = [nc.dram_tensor(f"c_{n}", [D, T], F32, kind="Internal").ap() for n in "qk"]
        const, moved, relay = core.sem("c_const"), core.sem("c_moved"), core.sem("c_relay")
        before = ["xn", "xT", "take_xT", "q", "take_q", "k", "take_k", "v", "take_v", "spread"]
        tile = ["scores", "clip", "decay", "top", "negate", "exp", "total", "invert", "weigh",
                "probsT", "take_probsT", "out", "take_out"]
        head = ["pick"] + [f"{s}{c}" for c in range(NT) for s in tile]
        after = ["headsT", "take_headsT", "rows", "take_rows"]
        BATCH = len(before) + HEADS * len(head) + len(after)
        block = ctx.enter_context(nc.Block())

        def turn(t, name, h=None):
            if name in before:
                return t * BATCH + (before.index(name) + 1)
            if name in after:
                return t * BATCH + (len(before) + HEADS * len(head) + after.index(name) + 1)
            return t * BATCH + h * len(head) + (len(before) + head.index(name) + 1)

        @block.sync
        def _(sp):
            sp.dma_start(decay[:], I["decay"]).then_inc(const, 16)
            sp.wait_ge(const, 16)
            with sp.Fori(0, B) as t:
                sp.wait_ge(relay, turn(t, "spread"))
                sp.dma_start(dram[0], qT[:]).then_inc(moved, 16)
                sp.dma_start(dram[1], kT[:]).then_inc(moved, 16)
                sp.wait_ge(moved, t * 64 + 32)
                for src, dst in zip(dram, (q8, k8)):
                    sp.dma_start(dst[:], src.rearrange("(h d) t -> d h t", d=HD)).then_inc(moved, 16)
                sp.wait_ge(moved, t * 64 + 64)
                sp.sem_inc(relay, 1)

        @block.gpsimd
        def _(pool):
            pool.wait_ge(const, 16)

        @block.scalar
        def _(act):
            act.preload_act_table(ACT.Exp)
            with act.Fori(0, B) as t:
                with act.Fori(0, HEADS) as h:
                    for c in range(NT):
                        act.wait_ge(relay, turn(t, f"exp{c}", h))
                        act.activation(probs[:], probs[:], ACT.Exp, bias=top[:]).then_inc(relay, 1)

        @block.tensor
        def _(pe):
            def tiles_T(src):
                for c in range(NT):
                    mm = pe.transpose(M[:, tile_of(core, c)], src[:, c, :], core.ident[:])
                mm.then_inc(relay, 1)

            def rows(lhsT, w):
                for c in range(NT):
                    mm = pe.matmul(M[:, tile_of(core, c)], lhsT[:, tile_of(core, c)], w[:], start=True, stop=True)
                mm.then_inc(relay, 1)

            with pe.Fori(0, B) as t:
                pe.wait_ge(relay, turn(t, "xT"))
                tiles_T(xn)
                pe.wait_ge(relay, turn(t, "q"))
                pe.matmul(M[:], core.Wq[:], xnT[:], start=True, stop=True).then_inc(relay, 1)
                pe.wait_ge(relay, turn(t, "k"))
                pe.matmul(M[:], core.Wkr[:], xnT[:], start=True, stop=True).then_inc(relay, 1)
                pe.wait_ge(relay, turn(t, "v"))
                rows(xnT, core.Wvr)
                with pe.Fori(0, HEADS) as h:
                    for c in range(NT):
                        pe.wait_ge(relay, turn(t, f"scores{c}", h))
                        pe.matmul(M[:], qh[:, tile_of(core, c)], kh[:], start=True, stop=True).then_inc(relay, 1)
                        pe.wait_ge(relay, turn(t, f"probsT{c}", h))
                        for k in range(NT):
                            mm = pe.transpose(M[:, tile_of(core, k)], probs[:, tile_of(core, k)], core.ident[:])
                        mm.then_inc(relay, 1)
                        pe.wait_ge(relay, turn(t, f"out{c}", h))
                        for k in range(NT):
                            mm = pe.matmul(O[:], probsT[:, k, :], V[:, k, bass.ds(h * HD, HD)], start=(k == 0),
                                           stop=(k == NT - 1))
                        mm.then_inc(relay, 1)
                pe.wait_ge(relay, turn(t, "headsT"))
                tiles_T(heads_out)
                pe.wait_ge(relay, turn(t, "rows"))
                rows(heads_outT, core.Wo)

        @block.vector
        def _(v):
            v.sem_inc(relay, 1)
            v.wait_ge(const, 16)

            def take(t, name, dst):
                v.wait_ge(relay, turn(t, name))
                v.tensor_copy(dst, M[:]).then_inc(relay, 1)

            with v.Fori(0, B) as t:
                v.wait_ge(relay, turn(t, "xn"))
                for c in range(NT):
                    op = v.tensor_scalar(xn[:, c], X[:, t, c], core.xmean[:, t, c:c + 1],
                                         core.xrstd[:, t, c:c + 1], ALU.subtract, ALU.mult)
                op.then_inc(relay, 1)
                take(t, "take_xT", xnT[:])
                take(t, "take_q", qT[:])
                take(t, "take_k", kT[:])
                take(t, "take_v", V[:].rearrange("p c d -> p (c d)"))
                with v.Fori(0, HEADS) as h:
                    v.wait_ge(relay, turn(t, "pick", h))
                    v.tensor_copy(qh[:], q8[:, h, :])
                    v.tensor_copy(kh[:], k8[:, h, :]).then_inc(relay, 1)
                    for c in range(NT):
                        v.wait_ge(relay, turn(t, f"clip{c}", h))
                        v.tensor_scalar(probs[:], M[:], -1e4, 1e4, ALU.max, ALU.min).then_inc(relay, 1)
                        v.wait_ge(relay, turn(t, f"decay{c}", h))
                        v.tensor_tensor(probs[:], probs[:], decay[:, (NT - 1 - c) * P:(NT - 1 - c) * P + T],
                                        ALU.mult).then_inc(relay, 1)
                        v.wait_ge(relay, turn(t, f"top{c}", h))
                        v.tensor_reduce(top[:], probs[:], AX.X, ALU.max).then_inc(relay, 1)
                        v.wait_ge(relay, turn(t, f"negate{c}", h))
                        v.tensor_scalar(top[:], top[:], -1.0, None, ALU.mult).then_inc(relay, 1)
                        v.wait_ge(relay, turn(t, f"total{c}", h))
                        v.tensor_reduce(total[:], probs[:], AX.X, ALU.add).then_inc(relay, 1)
                        v.wait_ge(relay, turn(t, f"invert{c}", h))
                        v.reciprocal(total[:], total[:]).then_inc(relay, 1)
                        v.wait_ge(relay, turn(t, f"weigh{c}", h))
                        v.tensor_scalar(probs[:], probs[:], total[:], None, ALU.mult).then_inc(relay, 1)
                        v.wait_ge(relay, turn(t, f"take_probsT{c}", h))
                        v.tensor_copy(probsT[:].rearrange("p k q -> p (k q)"), M[:]).then_inc(relay, 1)
                        v.wait_ge(relay, turn(t, f"take_out{c}", h))
                        v.tensor_copy(heads_out[:, c, bass.ds(h * HD, HD)], O[:]).then_inc(relay, 1)
                take(t, "take_headsT", heads_outT[:])
                v.wait_ge(relay, turn(t, "take_rows"))
                v.tensor_copy(Y[:, t + 1].rearrange("p c d -> p (c d)"), M[:])
                for c in range(NT):
                    op = v.bn_stats(core.yst[:, t + 1, c], M[:, tile_of(core, c)])
                op.then_inc(relay, 1)


class Bank:

    def __init__(self, core, ctx, name, shape=None):
        self.t = ctx.enter_context(core.nc.psum_tensor(name, shape or [P, 512], F32))
        self.full, self.free = core.sem(name + "_full"), core.sem(name + "_free")

    def open(self, pe):
        pe.sem_inc(self.free, 1)

    def fill(self, pe, n):
        pe.wait_ge(self.free, n)

    def filled(self, ins):
        ins.then_inc(self.full, 1)

    def read(self, eng, n):
        eng.wait_ge(self.full, n)

    def emptied(self, ins):
        ins.then_inc(self.free, 1)

    def after(self, eng, n):
        eng.wait_ge(self.free, n + 1)


def in_pairs(eng, B, body):
    with eng.Fori(0, B // 2) as i:
        for p in range(2):
            body(i * 2 + p, p, i)


def transposed(core, pe, bank, n, src):
    bank.fill(pe, n)
    for c in range(core.NT):
        mm = pe.transpose(bank.t[:, c * P:(c + 1) * P], src[:, c, :], core.ident[:])
    bank.filled(mm)


def tile_of(core, c):
    return slice(c * P, (c + 1) * P)


def add_normed(core, name, rms=False, affine=None, store=None):
    nc, B, NT = core.nc, core.B, core.NT
    X, Y = core.X, core.Y
    with ExitStack() as ctx:
        sb = lambda n, s, d=F32: ctx.enter_context(nc.sbuf_tensor(f"{name}_{n}", s, d))
        mean, var, tmp, rstd, shift = (sb(n, [P, B, NT]) for n in ("mean", "var", "tmp", "rstd", "shift"))
        sem = lambda n: core.sem(f"{name}_{n}")
        steps, rooted, want_root, shift_done = sem("steps"), sem("rooted"), sem("want_root"), sem("shift_done")
        normed, added, stored, gb_load = sem("normed"), sem("added"), sem("stored"), sem("gb_load")
        affined, counted = sem("affined"), sem("counted")
        if affine:
            gain, bias = sb("gain", [P, D]), sb("bias", [P, D])
        if store is not None:
            out = store.rearrange("b (c p) d -> p b c d", p=P)
        rounds = 2 if affine else 1
        roots = rounds + (0 if store is not None else 2 if rms else 1)
        block = ctx.enter_context(nc.Block())

        @block.sync
        def _(sp):
            if affine:
                for dst, src in ((gain, affine[0]), (bias, affine[1])):
                    sp.dma_start(dst[:], src.partition_broadcast(P)).then_inc(gb_load, 16)
            if store is not None:
                with sp.Fori(0, B) as t:
                    sp.wait_ge(added, t + 1)
                    sp.sem_inc(core.turns, 1)
                    sp.dma_start(out[:, t], X[:, t]).then_inc(stored, 16)
                sp.wait_ge(stored, 16 * B)

        @block.scalar
        def _(act):
            def root(n):
                act.wait_ge(want_root, n)
                act.activation(tmp[:], tmp[:], ACT.Sqrt).then_inc(rooted, 1)

            for k in range(rounds):
                root(k + 1)
                act.wait_ge(shift_done, k + 1)
                with act.Fori(0, B) as t:
                    for c in range(NT):
                        y = Y[:, t + 1, c]
                        op = act.activation(y, y, ACT.Identity, bias=shift[:, t, c:c + 1], scale=rstd[:, t, c:c + 1])
                    op.then_inc(normed, 1)
            for k in range(rounds, roots):
                root(k + 1)

        @block.vector
        def _(v):
            tick = Tally(v, steps)

            def inverse_root(n, dst, eps):
                v.tensor_scalar(tmp[:], var[:], eps, None, ALU.add).then_inc(want_root, 1)
                v.wait_ge(rooted, n)
                tick.step(v.reciprocal(dst, tmp[:]))

            for k in range(rounds):
                moments(v, tick, core.yst[:, 1:B + 1], mean[:], var[:], tmp[:])
                inverse_root(k + 1, rstd[:], 1e-5)
                v.scalar_tensor_tensor(shift[:], mean[:], -1.0, rstd[:], ALU.mult, ALU.mult).then_inc(shift_done, 1)
                if k < rounds - 1:
                    v.wait_ge(gb_load, 32)
                    wide = lambda a: a[:].unsqueeze(1).to_broadcast([P, NT, D])
                    with v.Fori(0, B) as t:
                        v.wait_ge(normed, t + 1)
                        v.tensor_tensor(Y[:, t + 1], Y[:, t + 1], wide(gain), ALU.mult).then_inc(affined, 1)
                        v.wait_ge(affined, 2 * t + 1)
                        v.tensor_tensor(Y[:, t + 1], Y[:, t + 1], wide(bias), ALU.add).then_inc(affined, 1)
                        v.wait_ge(affined, 2 * t + 2)
                        for c in range(NT):
                            op = v.bn_stats(core.yst[:, t + 1, c], Y[:, t + 1, c])
                        op.then_inc(counted, 1)
                    v.wait_ge(counted, B)
            done = B * (rounds - 1)
            with v.Fori(0, B) as t:
                v.wait_ge(normed, t + (done + 1))
                v.tensor_tensor(X[:, t], X[:, t], Y[:, t + 1], ALU.add).then_inc(added, 1)
                if store is None:
                    v.wait_ge(added, t + 1)
                    for c in range(NT):
                        op = v.bn_stats(core.xst[:, t, c], X[:, t, c])
                    op.then_inc(counted, 1)
            if store is None:
                v.wait_ge(counted, done + B)
                moments(v, tick, core.xst[:], core.xmean[:, 0:B], var[:], tmp[:])
                inverse_root(rounds + 1, core.xrstd[:, 0:B], 1e-5)
                if rms:
                    r = core.xrstd[:, 0:B]
                    tick.step(v.tensor_tensor(var[:], var[:], r, ALU.mult))
                    tick.step(v.tensor_tensor(var[:], var[:], r, ALU.mult))
                    inverse_root(rounds + 2, tmp[:], 1e-6)
                    tick.step(v.tensor_tensor(core.urstd[:, 0:B], tmp[:], r, ALU.mult))


def take_transposed(eng_copy, eng, bank, n, dst):
    bank.read(eng, n)
    bank.emptied(eng_copy(dst, bank.t[:, 0:dst.shape[-1]]))


def swiglu(core, I):
    nc, B, NT, T = core.nc, core.B, core.NT, core.T
    X, Y = core.X, core.Y
    F = I["L0_ffn_w_gate"].shape[0]
    FC = F // P
    S = 1.0 / 127.0
    with ExitStack() as ctx:
        sb = lambda n, s, d=F32: ctx.enter_context(nc.sbuf_tensor("f_" + n, s, d))
        sem = lambda n: core.sem("f_" + n)
        ints = [sb(f"int{k}", [P, F], I32) for k in range(3)]
        floats = [sb(f"float{k}", [P, F]) for k in range(3)]
        wT = [sb(f"wT{k}", [P, FC, P]) for k in range(3)]
        xn, xnT = sb("xn", [P, NT, D]), [sb(f"xnT{p}", [D, T]) for p in range(2)]
        gated = [sb(f"gated{p}", [P, T]) for p in range(2)]
        hid = [sb(f"hid{p}", [P, FC, T]) for p in range(2)]
        TP = Bank(core, ctx, "f_TP")
        G = [ctx.enter_context(nc.psum_tensor(f"f_G{p}", [P, 512], F32)) for p in range(2)]
        U = [ctx.enter_context(nc.psum_tensor(f"f_U{p}", [P, 512], F32)) for p in range(2)]
        OUT = [Bank(core, ctx, f"f_OUT{p}") for p in range(2)]
        wload, cast, xn_done = sem("wload"), sem("cast"), sem("xn_done")
        gu_full, gated_done, hid_done = sem("gu_full"), sem("gated_done"), sem("hid_done")
        block = ctx.enter_context(nc.Block())
        xT_use = lambda u: u + 4

        @block.sync
        def _(sp):
            for k, n in enumerate(("w_gate", "w_up")):
                sp.dma_start(ints[k][:].rearrange("p (m d) -> p m d", m=FC),
                             I["L0_ffn_" + n].rearrange("(m p) d -> p m d", p=P)).then_inc(wload, 16)
            sp.dma_start(ints[2][:], I["L0_ffn_w_down"]).then_inc(wload, 16)
            sp.wait_ge(wload, 48)

        @block.scalar
        def _(act):
            take_T = lambda u, p: take_transposed(lambda o, i: act.activation(o, i, ACT.Copy), act, TP, xT_use(u),
                                                  xnT[p][:])
            act.preload_act_table(ACT.Silu)
            take_T(0, 0)

            def body(t, p, i):
                for m in range(FC):
                    n = t * FC + m
                    act.wait_ge(gu_full, n + 1)
                    act.wait_ge(hid_done, n + 1)
                    act.activation(gated[(p + m) % 2][:], G[(p + m) % 2][:], ACT.Silu, scale=S)\
                       .then_inc(gated_done, 1)
                take_T(t + 1, 1 - p)

            in_pairs(act, B, body)

        @block.tensor
        def _(pe):
            for bank in (TP, *OUT):
                bank.open(pe)
            for k in range(3):
                pe.wait_ge(cast, k + 1)
                TP.fill(pe, k + 1)
                for m in range(FC):
                    mm = pe.transpose(TP.t[:, tile_of(core, m)], floats[k][:, tile_of(core, m)], core.ident[:])
                TP.filled(mm)

            def x_T(u):
                pe.wait_ge(xn_done, u + 1)
                transposed(core, pe, TP, xT_use(u), xn)

            x_T(0)

            def body(t, p, i):
                TP.after(pe, xT_use(t))
                for m in range(FC):
                    b = (p + m) % 2
                    pe.wait_ge(hid_done, t * FC + (m + 1))
                    pe.matmul(G[b][:], wT[0][:, m, :], xnT[p][:], start=True, stop=True)
                    pe.matmul(U[b][:], wT[1][:, m, :], xnT[p][:], start=True, stop=True).then_inc(gu_full, 1)
                x_T(t + 1)
                pe.wait_ge(hid_done, t * FC + (FC + 2))
                OUT[p].fill(pe, i + 1)
                for c in range(NT):
                    for m in range(FC):
                        mm = pe.matmul(OUT[p].t[:, tile_of(core, c)], hid[p][:, m, tile_of(core, c)], wT[2][:, m, :],
                                       start=(m == 0), stop=(m == FC - 1))
                OUT[p].filled(mm)

            in_pairs(pe, B, body)

        @block.vector
        def _(v):
            v.sem_inc(hid_done, 2)
            v.wait_ge(wload, 48)
            for k in range(3):
                v.tensor_copy(floats[k][:], ints[k][:]).then_inc(cast, 1)
            for k in range(3):
                take_transposed(v.tensor_copy, v, TP, k + 1, wT[k][:].rearrange("p m d -> p (m d)"))

            def layer_norm(u):
                for c in range(NT):
                    op = v.tensor_scalar(xn[:, c], X[:, u, c], core.xmean[:, u, c:c + 1],
                                         core.xrstd[:, u, c:c + 1], ALU.subtract, ALU.mult)
                op.then_inc(xn_done, 1)

            layer_norm(0)
            TP.after(v, xT_use(0))

            def body(t, p, i):
                layer_norm(t + 1)
                for m in range(FC):
                    n = t * FC + m
                    v.wait_ge(gated_done, n + 1)
                    v.scalar_tensor_tensor(hid[p][:, m], U[(p + m) % 2][:], S * S, gated[(p + m) % 2][:], ALU.mult,
                                           ALU.mult).then_inc(hid_done, 1)
                OUT[p].read(v, i + 1)
                v.tensor_copy(Y[:, t + 1].rearrange("p c d -> p (c d)"), OUT[p].t[:])
                for c in range(NT):
                    op = v.bn_stats(core.yst[:, t + 1, c], OUT[p].t[:, tile_of(core, c)])
                OUT[p].emptied(op)

            in_pairs(v, B, body)


def state_space(core, I):
    nc, B, NT, T = core.nc, core.B, core.NT, core.T
    X, Y = core.X, core.Y
    N = I["L1_attn_A_ssm"].shape[1]
    lo, hi = math.log(0.001), math.log(0.1)
    dt = [math.exp(lo + (hi - lo) * n / (N - 1)) for n in range(N)]
    W = 4
    with ExitStack() as ctx:
        sb = lambda n, s, d=F32: ctx.enter_context(nc.sbuf_tensor("m_" + n, s, d))
        sem = lambda n: core.sem("m_" + n)
        A, Bs, C = sb("A", [D, N]), sb("B", [D, N]), sb("C", [D, N])
        Ds, s1 = sb("Ds", [D, 1]), sb("s1", [D, 1])
        dA, coef = sb("dA", [D, N]), sb("coef", [D, N])
        diag = sb("diag", [D, N + 1, D])
        u, uT = sb("u", [P, NT, D]), [sb(f"uT{p}", [D, T]) for p in range(2)]
        state = sb("state", [D, W, T])
        ysb = sb("ysb", [D, T])
        shift = sb("shift", [P, B, NT])
        TP = Bank(core, ctx, "m_TP")
        YT = [Bank(core, ctx, f"m_YT{p}") for p in range(2)]
        Z = Bank(core, ctx, "m_Z")
        wload, dA_done, steps, diag_done = sem("wload"), sem("dA_done"), sem("steps"), sem("diag_done")
        u_done, scanned, summed, a_done, shift_done = (sem(n) for n in ("u_done", "scanned", "summed", "a_done", "shift_done"))
        block = ctx.enter_context(nc.Block())
        xT_use = lambda b: b + 1

        @block.sync
        def _(sp):
            for dst, name in ((A, "A_ssm"), (Bs, "B_ssm"), (C, "C_ssm")):
                sp.dma_start(dst[:], I["L1_attn_" + name]).then_inc(wload, 16)
            for dst, name in ((Ds, "D_ssm"), (s1, "scale1")):
                sp.dma_start(dst[:], I["L1_attn_" + name].unsqueeze(1)).then_inc(wload, 16)
            sp.wait_ge(wload, 80)

        @block.scalar
        def _(act):
            act.wait_ge(wload, 80)
            act.activation(A[:], A[:], ACT.Exp).then_inc(dA_done, 1)
            act.wait_ge(dA_done, 1)
            for n in range(N):
                op = act.activation(dA[:, n:n + 1], A[:, n:n + 1], ACT.Exp, scale=-dt[n])
            op.then_inc(dA_done, 1)
            act.wait_ge(shift_done, 1)

            def take_u(b, p):
                take_transposed(lambda o, i: act.activation(o, i, ACT.Copy), act, TP, xT_use(b), uT[p][:])

            take_u(0, 0)

            def body(t, p, i):
                for c in range(NT):
                    op = act.activation(Y[:, t + 1, c], X[:, t, c], ACT.Identity, bias=shift[:, t, c:c + 1],
                                        scale=core.xrstd[:, t, c:c + 1])
                op.then_inc(a_done, 1)
                take_u(t + 1, 1 - p)
                YT[p].read(act, i + 1)
                Z.read(act, t + 1)
                YT[p].emptied(act.activation(ysb[:], YT[p].t[:], ACT.Copy))

            in_pairs(act, B, body)

        @block.tensor
        def _(pe):
            for bank in (TP, *YT):
                bank.open(pe)
            pe.sem_inc(summed, W)

            def u_T(b):
                pe.wait_ge(u_done, b + 1)
                transposed(core, pe, TP, xT_use(b), u)

            u_T(0)
            pe.wait_ge(diag_done, 1)

            def body(t, p, i):
                u_T(t + 1)
                TP.after(pe, xT_use(t))
                YT[p].fill(pe, i + 1)
                for n in range(N):
                    pe.wait_ge(scanned, t * N + (n + 1))
                    pe.matmul(YT[p].t[:], diag[:, n, :], state[:, n % W, :], start=(n == 0), stop=False)\
                      .then_inc(summed, 1)
                YT[p].filled(pe.matmul(YT[p].t[:], diag[:, N, :], uT[p][:], start=False, stop=True))
                YT[p].after(pe, i + 1)
                Z.fill(pe, t + 2)
                for c in range(NT):
                    mm = pe.transpose(Z.t[:, tile_of(core, c)], ysb[:, tile_of(core, c)], core.ident[:])
                Z.filled(mm)

            in_pairs(pe, B, body)

        @block.vector
        def _(v):
            tick = Tally(v, steps)
            tick.step(v.memset(Z.t[:], 0.0))
            v.sem_inc(Z.full, 1)
            v.sem_inc(Z.free, 1)
            v.sem_inc(a_done, 1)
            v.scalar_tensor_tensor(shift[:], core.xmean[:, 0:B], -1.0, core.xrstd[:, 0:B], ALU.mult, ALU.mult)\
             .then_inc(shift_done, 1)

            def rms_norm(b):
                for c in range(NT):
                    op = v.tensor_scalar(u[:, c], X[:, b, c], core.xmean[:, b, c:c + 1],
                                         core.urstd[:, b, c:c + 1], ALU.subtract, ALU.mult)
                op.then_inc(u_done, 1)

            rms_norm(0)
            v.wait_ge(dA_done, 2)
            tick.step(v.tensor_scalar(coef[:], dA[:], -1.0, 1.0, ALU.mult, ALU.add))
            tick.step(v.reciprocal(A[:], A[:]))
            tick.step(v.tensor_tensor(coef[:], coef[:], Bs[:], ALU.mult))
            tick.step(v.tensor_tensor(coef[:], coef[:], A[:], ALU.mult))
            tick.step(v.tensor_tensor(coef[:], coef[:], C[:], ALU.mult))
            tick.step(v.tensor_scalar(coef[:], coef[:], s1[:], None, ALU.mult))
            tick.step(v.tensor_tensor(Ds[:], Ds[:], s1[:], ALU.mult))
            for n in range(N + 1):
                by = coef[:, n:n + 1] if n < N else Ds[:]
                op = v.tensor_scalar(diag[:, n], core.ident[:], by, None, ALU.mult)
            op.then_inc(diag_done, 1)

            def finish(b):
                Z.read(v, b + 2)
                v.wait_ge(a_done, b + 2)
                y = Y[:, b + 1].rearrange("p c d -> p (c d)")
                Z.emptied(v.tensor_tensor(y, y, Z.t[:], ALU.add))
                Z.after(v, b + 2)
                for c in range(NT):
                    v.bn_stats(core.yst[:, b + 1, c], Y[:, b + 1, c])

            def body(t, p, i):
                TP.after(v, xT_use(t))
                for n in range(N):
                    v.wait_ge(summed, t * N + (n + 1))
                    v.tensor_tensor_scan(state[:, n % W, :], dA[:, n:n + 1].to_broadcast([D, T]), uT[p][:], 0.0,
                                         ALU.mult, ALU.add).then_inc(scanned, 1)
                    if n == 0:
                        rms_norm(t + 1)
                    if n == W + 1:
                        finish(t - 1)

            in_pairs(v, B, body)
            finish(B - 1)


def mlp(core, I):
    nc, B, NT, T = core.nc, core.B, core.NT, core.T
    Y = core.Y
    F = I["L1_attn_w1"].shape[1]
    FC = F // P
    with ExitStack() as ctx:
        sb = lambda n, s, d=F32: ctx.enter_context(nc.sbuf_tensor("g_" + n, s, d))
        sem = lambda n: core.sem("g_" + n)
        w1, w2 = sb("w1", [D, F]), sb("w2", [P, FC, D])
        b1, b2, s2 = sb("b1", [P, FC]), sb("b2", [1, D]), sb("s2", [D, 1])
        mean, var, tmp, rstd = (sb(n, [P, B, NT]) for n in ("mean", "var", "tmp", "rstd"))
        yn, ynT = sb("yn", [P, NT, D]), [sb(f"ynT{p}", [D, T]) for p in range(2)]
        hid = [sb(f"hid{p}", [P, FC, T]) for p in range(2)]
        TP = Bank(core, ctx, "g_TP")
        H = [Bank(core, ctx, f"g_H{k}") for k in range(FC)]
        OUT = [Bank(core, ctx, f"g_OUT{p}") for p in range(2)]
        wload, steps, scaled, rooted, want_root = (sem(n) for n in ("wload", "steps", "scaled", "rooted", "want_root"))
        yn_done = sem("yn_done")
        block = ctx.enter_context(nc.Block())
        yT_use = lambda b: b + 1

        @block.sync
        def _(sp):
            sp.dma_start(w1[:], I["L1_attn_w1"]).then_inc(wload, 16)
            sp.dma_start(w2[:], I["L1_attn_w2"].rearrange("(m p) d -> p m d", p=P)).then_inc(wload, 16)
            with nc.allow_non_contiguous_dma("a bias with its features on partitions"):
                sp.dma_start(b1[:], I["L1_attn_b1"].rearrange("(m p) -> p m", p=P)).then_inc(wload, 16)
            sp.dma_start(b2[:], I["L1_attn_b2"].unsqueeze(0)).then_inc(wload, 16)
            sp.dma_start(s2[:], I["L1_attn_scale2"].unsqueeze(1)).then_inc(wload, 16)
            sp.wait_ge(wload, 80)

        @block.scalar
        def _(act):
            act.wait_ge(want_root, 1)
            act.activation(tmp[:], tmp[:], ACT.Sqrt).then_inc(rooted, 1)
            act.preload_act_table(ACT.Gelu)
            act.wait_ge(wload, 80)

            def body(t, p, i):
                for m in range(FC):
                    H[m].read(act, t + 1)
                    H[m].emptied(act.activation(hid[p][:, m], H[m].t[:], ACT.Gelu, bias=b1[:, m:m + 1]))

            in_pairs(act, B, body)

        @block.tensor
        def _(pe):
            for bank in (TP, *H, *OUT):
                bank.open(pe)
            pe.wait_ge(scaled, 1)

            def y_T(b):
                pe.wait_ge(yn_done, b + 1)
                transposed(core, pe, TP, yT_use(b), yn)

            y_T(0)

            def body(t, p, i):
                TP.after(pe, yT_use(t))
                for m in range(FC):
                    H[m].fill(pe, t + 1)
                    H[m].filled(pe.matmul(H[m].t[:], w1[:, tile_of(core, m)], ynT[p][:], start=True, stop=True))
                y_T(t + 1)
                OUT[p].fill(pe, i + 1)
                for c in range(NT):
                    o = OUT[p].t[:, tile_of(core, c)]
                    pe.matmul(o, core.ones[0:1, :], b2[:], start=True, stop=False)
                    for m in range(FC):
                        if c == 0:
                            H[m].after(pe, t + 1)
                        mm = pe.matmul(o, hid[p][:, m, tile_of(core, c)], w2[:, m, :], start=False, stop=(m == FC - 1))
                OUT[p].filled(mm)

            in_pairs(pe, B, body)

        @block.vector
        def _(v):
            tick = Tally(v, steps)
            moments(v, tick, core.yst[:, 1:B + 1], mean[:], var[:], tmp[:])
            tick.step(v.tensor_tensor(mean[:], mean[:], mean[:], ALU.mult))
            v.scalar_tensor_tensor(tmp[:], var[:], 1e-6, mean[:], ALU.add, ALU.add).then_inc(want_root, 1)
            v.wait_ge(wload, 80)
            v.tensor_scalar(w1[:], w1[:], s2[:], None, ALU.mult).then_inc(scaled, 1)
            v.wait_ge(rooted, 1)
            tick.step(v.reciprocal(rstd[:], tmp[:]))

            def rms_norm(b, last=False):
                for c in range(NT):
                    op = v.tensor_scalar(yn[:, c], Y[:, b + 1, c], rstd[:, b, c:c + 1], None, ALU.mult)
                op.then_inc(yn_done, 1)

            def take_T(b, p):
                take_transposed(v.tensor_copy, v, TP, yT_use(b), ynT[p][:])

            rms_norm(0)
            take_T(0, 0)

            def body(t, p, i, last=False):
                rms_norm(t + 1) if not last else v.tensor_copy(yn[:], Y[:, 0]).then_inc(yn_done, 1)
                take_T(t + 1, 1 - p)
                OUT[p].read(v, i + 1)
                y = Y[:, t + 1].rearrange("p c d -> p (c d)")
                OUT[p].emptied(v.tensor_tensor(y, y, OUT[p].t[:], ALU.add))
                OUT[p].after(v, i + 1)
                for c in range(NT):
                    v.bn_stats(core.yst[:, t + 1, c], Y[:, t + 1, c])

            with v.Fori(0, B // 2 - 1) as i:
                for p in range(2):
                    body(i * 2 + p, p, i)
            body(B - 2, 0, B // 2 - 1)
            body(B - 1, 1, B // 2 - 1, last=True)


def experts(core, I):
    nc, B, NT, T = core.nc, core.B, core.NT, core.T
    X, Y = core.X, core.Y
    H = I["L1_ffn_enc_W"].shape[1]
    E, M, HH = I["L1_ffn_We1"].shape
    HC = H // P
    BIG = 64.0
    with ExitStack() as ctx:
        sb = lambda n, s, d=F32: ctx.enter_context(nc.sbuf_tensor("e_" + n, s, d))
        sem = lambda n: core.sem("e_" + n)
        encW, encb = sb("encW", [D, H]), sb("encb", [P, HC])
        s2cW, s2cb = sb("s2cW", [P, HC, M]), sb("s2cb", [M, 1])
        rW1, rb1, rW2 = sb("rW1", [M, 64]), sb("rb1", [64, 1]), sb("rW2", [65, E])
        We1, be1 = sb("We1", [M, E, HH]), sb("be1", [HH, E])
        We2, be2 = sb("We2", [HH, E, M]), sb("be2", [E, M])
        c2sW, c2sb = sb("c2sW", [M, H]), sb("c2sb", [P, HC])
        decW, decb = sb("decW", [P, HC, D]), sb("decb", [1, D])
        xn, xnT = sb("xn", [P, NT, D]), [sb(f"xnT{p}", [D, T]) for p in range(2)]
        enc, contT, rT = sb("enc", [P, HC, T]), sb("contT", [M, T]), sb("rT", [65, T])
        hid = [sb(f"hid{p}", [HH, E, T]) for p in range(2)]
        gates = [sb(f"gates{p}", [P, NT, E]) for p in range(2)]
        gatesT, moeT, dec_in = sb("gatesT", [E, T]), sb("moeT", [M, T]), sb("dec_in", [P, HC, T])
        weighted, moe = sb("weighted", [P, 2, E, M]), sb("moe", [P, NT, M])
        number = sb("number", [P, E])
        logit, hit, cand = sb("logit", [P, NT, E]), sb("hit", [P, NT, E]), sb("cand", [P, NT, E])
        mask = [sb(f"mask{k}", [P, NT, E]) for k in range(2)]
        top = [sb(f"top{k}", [P, NT]) for k in range(2)]
        first, gap, share = sb("first", [P, NT]), sb("gap", [P, 2, NT]), sb("share", [P, 2, NT])

        TP = Bank(core, ctx, "e_TP")
        EB = [Bank(core, ctx, f"e_E{m}") for m in range(HC)]
        FB = Bank(core, ctx, "e_F")
        HB = [Bank(core, ctx, f"e_H{k}") for k in range(2)]
        GB = [Bank(core, ctx, f"e_G{k}") for k in range(2)]
        wload, steps, init, xn_done = sem("wload"), sem("steps"), sem("init"), sem("xn_done")
        gap_done, share_done, gates_done, moe_done = (sem(n) for n in ("gap_done", "share_done", "gates_done",
                                                                       "moe_done"))
        xT_use = lambda u: u * 2 + 1
        dec_use = lambda t: t * 2 + 2
        enc_use, c2s_use = (lambda t: t * 2 + 1), (lambda t: t * 2 + 2)
        cont_use, router_use, gatesT_use, moeT_use, logits_use = (lambda t, k=k: t * 5 + k for k in range(1, 6))
        loads = [(encW[:], "enc_W", None), (s2cW[:], "s2c_W", "(m p) d -> p m d"), (rW1[:], "rW1", None),
                 (rW2[0:64], "rW2", None), (We1[:], "We1", "e m h -> m e h"), (We2[:], "We2", "e h m -> h e m"),
                 (be2[:], "be2", None), (c2sW[:], "c2s_W", None), (decW[:], "dec_W", "(m p) d -> p m d")]
        rows = [(rW2[64:65], "rb2"), (decb[:], "dec_b")]
        columns = [(s2cb[:], "s2c_b"), (rb1[:], "rb1")]
        NLOAD = 16 * (len(loads) + len(rows) + len(columns) + 3)
        block = ctx.enter_context(nc.Block())

        @block.sync
        def _(sp):
            for dst, name, how in loads:
                src = I["L1_ffn_" + name]
                src = src.rearrange(how, p=P) if how and "(" in how else src.rearrange(how) if how else src
                sp.dma_start(dst, src).then_inc(wload, 16)
            for dst, name in rows:
                sp.dma_start(dst, I["L1_ffn_" + name].unsqueeze(0)).then_inc(wload, 16)
            for dst, name in columns:
                sp.dma_start(dst, I["L1_ffn_" + name].unsqueeze(1)).then_inc(wload, 16)
            with nc.allow_non_contiguous_dma("biases with their features on partitions"):
                sp.dma_start(encb[:], I["L1_ffn_enc_b"].rearrange("(m p) -> p m", p=P)).then_inc(wload, 16)
                sp.dma_start(c2sb[:], I["L1_ffn_c2s_b"].rearrange("(m p) -> p m", p=P)).then_inc(wload, 16)
                sp.dma_start(be1[:], I["L1_ffn_be1"].rearrange("e h -> h e")).then_inc(wload, 16)
            sp.wait_ge(wload, NLOAD)

        @block.gpsimd
        def _(pool):
            for k in range(E):
                pool.memset(number[:, k:k + 1], float(k)).then_inc(init, 1)
            pool.wait_ge(init, E)
            pool.memset(rT[64:65], 1.0).then_inc(init, 1)
            pool.wait_ge(init, E + 1)
            pool.memset(hid[1][:], 0.0).then_inc(init, 1)
            pool.memset(gates[1][:], 0.0).then_inc(init, 1)

        @block.scalar
        def _(act):
            act.preload_act_table(ACT.Sigmoid)
            act.wait_ge(wload, NLOAD)

            def body(t, p, i):
                for m in range(HC):
                    EB[m].read(act, enc_use(t))
                    EB[m].emptied(act.activation(enc[:, m], EB[m].t[:], ACT.Sigmoid, bias=encb[:, m:m + 1]))
                FB.read(act, router_use(t))
                FB.emptied(act.activation(rT[0:64], FB.t[0:64], ACT.Tanh, bias=rb1[:]))
                for e in range(0, E, 2):
                    HB[0].read(act, t * (E // 2) + (e // 2 + 1))
                    HB[0].emptied(act.activation(hid[p][:, e], HB[0].t[:], ACT.Relu, bias=be1[:, e:e + 1]))
                    if e == E // 2:
                        for m in range(HC):
                            EB[m].read(act, c2s_use(t))
                            EB[m].emptied(act.activation(dec_in[:, m], EB[m].t[:], ACT.Sigmoid, bias=c2sb[:, m:m + 1]))
                take_decoded(t - 1, dec_use(t))
                act.wait_ge(gap_done, t + 1)
                act.activation(share[:], gap[:], ACT.Sigmoid).then_inc(share_done, 1)

            def take_decoded(b, n):
                TP.read(act, n)
                TP.emptied(act.activation(Y[:, b + 1].rearrange("p c d -> p (c d)"), TP.t[:], ACT.Sigmoid))

            in_pairs(act, B, body)
            for m in range(HC):
                EB[m].read(act, c2s_use(B) - 1)
                EB[m].emptied(act.activation(dec_in[:, m], EB[m].t[:], ACT.Sigmoid, bias=c2sb[:, m:m + 1]))
            take_decoded(B - 1, dec_use(B))

        @block.tensor
        def _(pe):
            for bank in (TP, *EB, FB, *HB, *GB):
                bank.open(pe)
            pe.wait_ge(wload, NLOAD)
            pe.wait_ge(init, E + 3)

            def x_T(u):
                pe.wait_ge(xn_done, u + 1)
                transposed(core, pe, TP, xT_use(u), xn)

            def encoder(t, p):
                TP.after(pe, xT_use(t))
                for m in range(HC):
                    EB[m].fill(pe, enc_use(t))
                    EB[m].filled(pe.matmul(EB[m].t[:], encW[:, tile_of(core, m)], xnT[p][:], start=True, stop=True))

            def cells(t):
                for m in range(HC):
                    EB[m].after(pe, enc_use(t))
                FB.fill(pe, cont_use(t))
                for m in range(HC):
                    mm = pe.matmul(FB.t[0:M], s2cW[:, m, :], enc[:, m, :], start=(m == 0), stop=(m == HC - 1))
                FB.filled(mm)

            def router(t):
                FB.fill(pe, router_use(t))
                pe.sem_inc(core.turns, 1)
                FB.filled(pe.matmul(FB.t[0:64], rW1[:], contT[:], start=True, stop=True))

            def expert_in(t, e):
                HB[e % 2].fill(pe, t * (E // 2) + (e // 2 + 1))
                HB[e % 2].filled(pe.matmul(HB[e % 2].t[:], We1[:, e, :], contT[:], start=True, stop=True))

            def logits(t):
                FB.fill(pe, logits_use(t))
                for c in range(NT):
                    mm = pe.matmul(FB.t[:, c * E:(c + 1) * E], rT[:, tile_of(core, c)], rW2[:], start=True, stop=True)
                FB.filled(mm)

            def expert_out(t, c, q):
                if c == 0:
                    for k in range(2):
                        HB[k].fill(pe, t * (E // 2) + 1)
                GB[c % 2].fill(pe, t * 2 + (c // 2 + 1))
                for e in range(E):
                    mm = pe.matmul(GB[c % 2].t[:, e * M:(e + 1) * M], hid[q][:, e, tile_of(core, c)], We2[:, e, :],
                                   start=True, stop=True)
                GB[c % 2].filled(mm)

            def gates_T(t, q, n):
                pe.wait_ge(gates_done, t + 1)
                FB.fill(pe, n)
                for c in range(NT):
                    mm = pe.matmul(FB.t[0:E, tile_of(core, c)], gates[q][:, c, :], core.ident[:], start=True, stop=True)
                FB.filled(mm)

            def moe_T(t, n):
                pe.wait_ge(moe_done, t + 1)
                FB.fill(pe, n)
                for c in range(NT):
                    o = FB.t[0:M, tile_of(core, c)]
                    pe.matmul(o, moe[:, c, :], core.ident[:], start=True, stop=False)
                    mm = pe.matmul(o, be2[:], gatesT[:, tile_of(core, c)], start=False, stop=True)
                FB.filled(mm)

            def spikes(n_moe, n):
                FB.after(pe, n_moe)
                for m in range(HC):
                    EB[m].fill(pe, n)
                    EB[m].filled(pe.matmul(EB[m].t[:], c2sW[:, tile_of(core, m)], moeT[:], start=True, stop=True))

            def decode(n_spikes, n):
                for m in range(HC):
                    EB[m].after(pe, n_spikes)
                TP.fill(pe, n)
                for c in range(NT):
                    o = TP.t[:, tile_of(core, c)]
                    pe.matmul(o, core.ones[0:1, :], decb[:], start=True, stop=False)
                    for m in range(HC):
                        mm = pe.matmul(o, dec_in[:, m, tile_of(core, c)], decW[:, m, :], start=False, stop=(m == HC - 1))
                TP.filled(mm)

            x_T(0)

            def body(t, p, i):
                expert_out(t, 0, 1 - p)
                encoder(t, p)
                expert_out(t, 1, 1 - p)
                cells(t)
                expert_out(t, 2, 1 - p)
                router(t)
                expert_out(t, 3, 1 - p)
                gates_T(t, 1 - p, gatesT_use(t))
                for e in range(E // 2):
                    expert_in(t, e)
                moe_T(t, moeT_use(t))
                expert_in(t, E // 2)
                spikes(moeT_use(t), c2s_use(t))
                for e in range(E // 2 + 1, E):
                    expert_in(t, e)
                logits(t)
                decode(c2s_use(t), dec_use(t))
                x_T(t + 1)

            in_pairs(pe, B, body)
            q = (B - 1) % 2
            for c in range(NT):
                expert_out(B, c, q)
            gates_T(B, q, cont_use(B))
            moe_T(B, router_use(B))
            spikes(router_use(B), enc_use(B))
            decode(enc_use(B), dec_use(B))

        @block.vector
        def _(v):
            tick = Tally(v, steps, per=12)

            def layer_norm(u):
                for c in range(NT):
                    op = v.tensor_scalar(xn[:, c], X[:, u, c], core.xmean[:, u, c:c + 1],
                                         core.xrstd[:, u, c:c + 1], ALU.subtract, ALU.mult)
                op.then_inc(xn_done, 1)

            def take_T(u, p):
                take_transposed(v.tensor_copy, v, TP, xT_use(u), xnT[p][:])

            def expert_hidden(t, e, p):
                HB[1].read(v, t * (E // 2) + (e // 2 + 1))
                HB[1].emptied(v.tensor_scalar(hid[p][:, e], HB[1].t[:], be1[:, e:e + 1], 0.0, ALU.add, ALU.max))

            def weigh_tile(t, c, q):
                if c == 0:
                    v.wait_ge(gates_done, t + 1)
                GB[c % 2].read(v, t * 2 + (c // 2 + 1))
                g = gates[q][:, c, :].unsqueeze(2).to_broadcast([P, E, M])
                GB[c % 2].emptied(v.tensor_tensor(weighted[:, c % 2], GB[c % 2].t[:].rearrange("p (e m) -> p e m", e=E),
                                                  g, ALU.mult))
                GB[c % 2].after(v, t * 2 + (c // 2 + 1))
                op = v.tensor_reduce(moe[:, c, :], weighted[:, c % 2].rearrange("p e m -> p m e"), AX.X, ALU.add)
                if c == NT - 1:
                    op.then_inc(moe_done, 1)

            def choose(t, p):
                tick.begin(t)
                wide = lambda a: a.unsqueeze(2).to_broadcast([P, NT, E])
                numbers = number[:].unsqueeze(1).to_broadcast([P, NT, E])
                FB.read(v, logits_use(t))
                FB.emptied(v.tensor_copy(logit[:].rearrange("p c e -> p (c e)"), FB.t[:, 0:NT * E]))
                FB.after(v, logits_use(t))
                for k in range(2):
                    tick.step(v.tensor_reduce(top[k][:], logit[:], AX.X, ALU.max))
                    tick.step(v.tensor_tensor(hit[:], logit[:], wide(top[k][:]), ALU.is_equal))
                    tick.step(v.scalar_tensor_tensor(cand[:], hit[:], -BIG, numbers, ALU.mult, ALU.add))
                    tick.step(v.tensor_reduce(first[:], cand[:], AX.X, ALU.min))
                    tick.step(v.tensor_tensor(mask[k][:], cand[:], wide(first[:]), ALU.is_equal))
                    if k == 0:
                        tick.step(v.scalar_tensor_tensor(logit[:], mask[0][:], -3e38, logit[:], ALU.mult, ALU.add))
                v.tensor_tensor(gap[:, 0], top[0][:], top[1][:], ALU.subtract)
                v.tensor_tensor(gap[:, 1], top[1][:], top[0][:], ALU.subtract).then_inc(gap_done, 1)

            def gate(t, p):
                wide = lambda a: a.unsqueeze(2).to_broadcast([P, NT, E])
                v.wait_ge(share_done, t + 1)
                v.tensor_tensor(hit[:], mask[0][:], wide(share[:, 0]), ALU.mult)
                tick.step(v.tensor_tensor(cand[:], mask[1][:], wide(share[:, 1]), ALU.mult))
                v.tensor_tensor(gates[p][:], hit[:], cand[:], ALU.add).then_inc(gates_done, 1)

            def take(n, rows, dst, bias=None):
                FB.read(v, n)
                if bias is None:
                    FB.emptied(v.tensor_copy(dst, FB.t[0:rows]))
                else:
                    FB.emptied(v.tensor_scalar(dst, FB.t[0:rows], bias, None, ALU.add))

            def statistics(b, n):
                TP.after(v, n)
                for c in range(NT):
                    v.bn_stats(core.yst[:, b + 1, c], Y[:, b + 1, c])

            v.sem_inc(gates_done, 1)
            v.wait_ge(wload, NLOAD)
            v.wait_ge(init, E + 3)
            layer_norm(0)
            take_T(0, 0)

            def body(t, p, i):
                layer_norm(t + 1)
                weigh_tile(t, 0, 1 - p)
                weigh_tile(t, 1, 1 - p)
                take(cont_use(t), M, contT[:], s2cb[:])
                weigh_tile(t, 2, 1 - p)
                weigh_tile(t, 3, 1 - p)
                take(gatesT_use(t), E, gatesT[:])
                expert_hidden(t, 1, p)
                expert_hidden(t, 3, p)
                take(moeT_use(t), M, moeT[:])
                expert_hidden(t, 5, p)
                expert_hidden(t, 7, p)
                choose(t, p)
                statistics(t - 1, dec_use(t))
                take_T(t + 1, 1 - p)
                gate(t, p)

            in_pairs(v, B, body)
            q = (B - 1) % 2
            for c in range(NT):
                weigh_tile(B, c, q)
            take(cont_use(B), E, gatesT[:])
            take(router_use(B), M, moeT[:])
            statistics(B - 1, dec_use(B))


def program(nc, I, out):
    B, S, _ = I["L0_attn_x"].shape
    with ExitStack() as ctx:
        core = Core(nc, ctx, B, S // P)
        setup(core, I)
        attention(core, I)
        check_range(core)
        with nc.If(nc.values_load(core.in_range[0:1, 0:1], min_val=0, max_val=1) == 0):
            attention_guarded(core, I)
        add_normed(core, "r1")
        swiglu(core, I)
        add_normed(core, "r2", rms=True)
        state_space(core, I)
        mlp(core, I)
        add_normed(core, "r3")
        experts(core, I)
        add_normed(core, "r4", affine=(I["L1_ffn_ln_g"], I["L1_ffn_ln_b"]), store=out)


def kernel(**inputs):
    import numpy as np
    import concourse.bacc as bacc
    from concourse import mybir
    from concourse.bass_utils import run_bass_kernel_spmd as launch

    nc = bacc.Bacc("TRN2", target_bir_lowering=False, num_devices=1)
    arrays = {name: np.ascontiguousarray(a) for name, a in inputs.items()}
    B, S, width = arrays["L0_attn_x"].shape
    tiles = S // 128
    distance = np.arange(S + (tiles - 1) * 128)[None, :] - (tiles - 1) * 128 - np.arange(128)[:, None]
    arrays["decay"] = np.exp(-1e-4 * np.abs(distance)).astype(np.float32)
    I = {name: nc.dram_tensor(name, a.shape, mybir.dt.from_np(a.dtype), kind="ExternalInput").ap()
         for name, a in arrays.items()}
    out = nc.dram_tensor("out", (B, S, width), mybir.dt.float32, kind="ExternalOutput").ap()
    program(nc, I, out)
    r = launch(nc, [arrays], core_ids=[0])
    return r.results[0]["out"]
```

```python
import math
from contextlib import ExitStack

import concourse.bass as bass
from concourse import mybir

F32 = mybir.dt.float32
BF16 = mybir.dt.bfloat16
I32 = mybir.dt.int32
ALU = mybir.AluOpType
ACT = mybir.ActivationFunctionType
AX = mybir.AxisListType

P = 128
D = 128
HEADS, HD = 16, 8
LATENT = 32
SLOTS = 6
SPLIT = ((0, 0), (0, 1), (0, 2), (1, 0), (1, 1), (2, 0))
VC = 32
CEILING = 60.0
QSCALE = 1.0 / (float(D) ** 0.5 + 1e-8)


class Tally:

    def __init__(self, eng, sem, per=0, start=0):
        self.eng, self.sem, self.per, self.start, self.turn, self.n = eng, sem, per, start, 0, 0

    def begin(self, turn):
        assert self.n in (0, self.per), (self.n, self.per)
        self.turn, self.n = turn, 0

    def mark(self, ins):
        ins.then_inc(self.sem, 1)
        self.n += 1

    def settle(self):
        self.eng.wait_ge(self.sem, self.turn * self.per + (self.start + self.n))

    def step(self, ins):
        self.mark(ins)
        self.settle()


class Core:

    def __init__(self, nc, ctx, B, NT):
        self.nc, self.ctx, self.B, self.NT, self.T = nc, ctx, B, NT, NT * P
        sb = lambda n, s, d=F32: ctx.enter_context(nc.sbuf_tensor(n, s, d))
        XY = sb("XY", [P, 2 * B + 1, NT, D])
        self.X, self.Y = XY[:, 0:B + 1], XY[:, B:2 * B + 1]
        self.xmean = sb("xmean", [P, B + 1, NT])
        self.xrstd = sb("xrstd", [P, B + 1, NT])
        self.urstd = sb("urstd", [P, B + 1, NT])
        self.xst = sb("xst", [P, B, NT, 6])
        self.yst = sb("yst", [P, B + 1, NT, 6])
        self.fine = sb("fine", [P, NT, 4])
        self.in_range = sb("in_range", [P, 1], I32)
        self.ident = sb("ident", [P, P])
        self.ones = sb("ones", [P, P])
        self.Wq, self.Wkr, self.Wvr, self.Wo = (sb(n, [D, D]) for n in ("Wq", "Wkr", "Wvr", "Wo"))
        self.turns = self.sem("turns")

    def sem(self, name):
        return self.ctx.enter_context(self.nc.semaphore(name))


def moments(v, tick, st, mean, var, tmp):
    tick.mark(v.tensor_tensor(mean, st[..., 1], st[..., 4], ALU.add))
    tick.mark(v.tensor_tensor(var, st[..., 2], st[..., 5], ALU.add))
    tick.step(v.tensor_tensor(tmp, st[..., 1], st[..., 4], ALU.subtract))
    tick.step(v.tensor_tensor(tmp, tmp, tmp, ALU.mult))
    tick.mark(v.tensor_scalar(mean, mean, 0.5, None, ALU.mult))
    tick.step(v.tensor_scalar(tmp, tmp, 0.25, None, ALU.mult))
    tick.step(v.scalar_tensor_tensor(var, var, 1.0 / D, tmp, ALU.mult, ALU.add))


def setup(core, I):
    nc, B, NT = core.nc, core.B, core.NT
    with ExitStack() as ctx:
        sb = lambda n, s, d=F32: ctx.enter_context(nc.sbuf_tensor(n, s, d))
        wk, wv, wks = sb("wk", [D, D]), sb("wv", [D, D]), sb("wks", [D, D])
        wsT = sb("wsT", [D, D])
        wd = sb("wd", [D, LATENT])
        wuk, wuv = sb("wuk", [LATENT, D]), sb("wuv", [LATENT, D])
        mT = sb("mT", [LATENT, D])
        wqr = sb("wqr", [D, D])
        tmp, var = sb("s_tmp", [P, B, NT]), sb("s_var", [P, B, NT])
        ps = ctx.enter_context(nc.psum_tensor("s_ps", [P, 4, 512], F32))
        xload, wload = core.sem("xload"), core.sem("wload")
        made, ident_done, tick_s = core.sem("setup_made"), core.sem("ident_done"), core.sem("setup_dve")
        on_pe, rooted = core.sem("setup_pe"), core.sem("setup_root")
        half = B // 2
        xv = I["L0_attn_x"].rearrange("b (c p) d -> p b c d", p=P)
        block = ctx.enter_context(nc.Block())

        @block.sync
        def _(sp):
            for n in range(2):
                for b in range(n * half, (n + 1) * half):
                    sp.dma_start(core.X[:, b], xv[:, b]).then_inc(xload, 16)
            sp.wait_ge(xload, 16 * B)

        @block.gpsimd
        def _(pool):
            pool.memset(core.ident[:], 0.0).then_inc(ident_done, 1)
            pool.memset(core.ones[:], 1.0).then_inc(ident_done, 1)
            pool.wait_ge(ident_done, 2)
            pool.affine_select(out=core.ident[:], in_=core.ident[:], compare_op=ALU.not_equal, fill=1.0,
                               base=0, pattern=[[-1, P]], channel_multiplier=1).then_inc(ident_done, 1)
            pool.memset(core.X[:, B], 0.0).then_inc(ident_done, 1)
            pool.memset(core.xmean[:, B], 0.0).then_inc(ident_done, 1)
            pool.memset(core.xrstd[:, B], 0.0).then_inc(ident_done, 1)
            pool.memset(core.urstd[:, B], 0.0).then_inc(ident_done, 1)

        @block.scalar
        def _(act):
            for dst, name in ((wk, "Wk"), (wv, "Wv"), (wd, "W_down_kv"), (wuk, "W_up_k"), (wuv, "W_up_v"),
                              (wqr, "Wq"), (core.Wo, "Wo")):
                act.dma_start(dst[:], I["L0_attn_" + name]).then_inc(wload, 16)
            act.wait_ge(tick_s, 2 + B * NT + 8)
            act.activation(core.xrstd[:, 0:B], core.xrstd[:, 0:B], ACT.Sqrt).then_inc(rooted, 1)

        @block.tensor
        def _(pe):
            pe.wait_ge(ident_done, 3)
            pe.wait_ge(tick_s, 2)
            pe.transpose(ps[:, 0, 0:D], wks[:], core.ident[:]).then_inc(on_pe, 1)
            pe.wait_ge(made, 1)
            pe.matmul(ps[0:LATENT, 1, 0:D], wd[:], wsT[:], start=True, stop=True).then_inc(on_pe, 1)
            pe.wait_ge(made, 2)
            pe.matmul(ps[:, 2, 0:D], mT[:], wuk[:], start=True, stop=True)
            pe.matmul(ps[:, 3, 0:D], mT[:], wuv[:], start=True, stop=True).then_inc(on_pe, 1)

        @block.vector
        def _(v):
            tick = Tally(v, tick_s)
            v.wait_ge(wload, 16 * 7)
            tick.mark(v.tensor_scalar(core.Wq[:], wqr[:], QSCALE, None, ALU.mult))
            tick.mark(v.tensor_tensor(wks[:], wk[:], wv[:], ALU.add))
            v.wait_ge(on_pe, 1)
            v.tensor_copy(wsT[:], ps[:, 0, 0:D]).then_inc(made, 1)
            v.wait_ge(on_pe, 2)
            v.tensor_copy(mT[:], ps[0:LATENT, 1, 0:D]).then_inc(made, 1)
            v.wait_ge(on_pe, 3)
            v.tensor_copy(core.Wkr[:], ps[:, 2, 0:D]).then_inc(made, 1)
            v.tensor_copy(core.Wvr[:], ps[:, 3, 0:D]).then_inc(made, 1)
            v.wait_ge(xload, 16 * B)
            for b in range(B):
                for c in range(NT):
                    tick.mark(v.bn_stats(core.xst[:, b, c], core.X[:, b, c]))
            tick.settle()
            moments(v, tick, core.xst[:], core.xmean[:, 0:B], var[:], tmp[:])
            tick.step(v.tensor_scalar(core.xrstd[:, 0:B], var[:], 1e-5, None, ALU.add))
            v.wait_ge(rooted, 1)
            tick.step(v.reciprocal(core.xrstd[:, 0:B], core.xrstd[:, 0:B]))


def attention(core, I):
    nc, B, NT, T = core.nc, core.B, core.NT, core.T
    HG = HEADS // 4
    STEPS = 2 * HG
    X, Y = core.X, core.Y
    with ExitStack() as ctx:
        sb = lambda n, s, d=F32: ctx.enter_context(nc.sbuf_tensor(n, s, d))
        psum = lambda n: ctx.enter_context(nc.psum_tensor(n, [P, 512], F32))
        decay = sb("a_decay", [P, T + (NT - 1) * P])
        Qs = [sb(f"Qs{p}", [SLOTS * HD, HEADS, T], BF16) for p in range(2)]
        Ks = [sb(f"Ks{p}", [SLOTS * HD, HEADS, T], BF16) for p in range(2)]
        V = [sb(f"V{p}", [P, NT, HEADS, VC]) for p in range(2)]
        probs = sb("probs", [P, 2, 4, 2, T])
        xnT = sb("a_xnT", [D, T])
        parts = [sb("qparts", [D, 3, T], BF16), sb("kparts", [D, 3, T], BF16)]
        heads_out = sb("heads_out", [P, NT, D])
        rest = sb("a_rest", [D, T])
        heads_outT = sb("heads_outT", [D, T])
        Osb = sb("Osb", [P, T])
        xn = sb("a_xn", [P, NT, D])
        one_over = sb("one_over", [P, NT, 4])
        S = [ctx.enter_context(nc.psum_tensor(f"S{i}", [P, 2, 512], F32)) for i in range(2)]
        O = [psum(f"O{i}") for i in range(2)]
        OT, M = psum("OT"), psum("M")
        dram = [nc.dram_tensor(f"{n}_parts", [D, 3, T], BF16, kind="Internal").ap() for n in "qk"]

        sem = lambda n: core.sem("a_" + n)
        const, init, xn_done = sem("const"), sem("init"), sem("xn_done")
        m_full, m_free = sem("m_full"), sem("m_free")
        first_part = [sem("q_first"), sem("k_first")]
        low = [sem("q_low"), sem("k_low")]
        stored, spread = [sem("q_stored"), sem("k_stored")], [sem("q_spread"), sem("k_spread")]
        s_full, decayed, exped, pv_done = sem("s_full"), sem("decayed"), sem("exped"), sem("pv_done")
        o_free, ot_full, inverted, heads_done = sem("o_free"), sem("ot_full"), sem("inverted"), sem("heads_done")
        second_part = sem("second_part")
        block = ctx.enter_context(nc.Block())

        FIRST = dict(xT=1, q=2, k=3, v=4)
        USES = dict(xT=1, q=2, k=3, headsT=4, rows=5, v=6)
        base_of = lambda t: t * 6 + 4

        def pairs(eng, body):
            with eng.Fori(0, B - 1, 2) as i:
                for p in range(2):
                    body(i + p, p)

        @block.sync
        def _(sp):
            sp.dma_start(decay[:], I["decay"]).then_inc(const, 16)

            def spread_parts(u, p, first=False):
                for w in range(2):
                    sp.wait_ge(low[w], u + 1)
                    sp.sem_inc(core.turns, 1)
                    if not first:
                        sp.wait_ge(spread[w], 16 * SLOTS * u)
                    sp.dma_start(dram[w], parts[w][:]).then_inc(stored[w], 16)
                    sp.wait_ge(stored[w], 16 * u + 16)
                    for s in range(SLOTS):
                        src = dram[w][:, SPLIT[s][w], :].rearrange("(h d) t -> d h t", d=HD)
                        sp.dma_start((Qs, Ks)[w][p][s * HD:(s + 1) * HD], src).then_inc(spread[w], 16)

            spread_parts(0, 0, first=True)
            pairs(sp, lambda t, p: spread_parts(t + 1, 1 - p))
            for w in range(2):
                sp.wait_ge(spread[w], 16 * SLOTS * (B + 1))

        @block.gpsimd
        def _(pool):
            pool.memset(heads_out[:], 0.0).then_inc(init, 1)
            pool.memset(Osb[:], 1.0).then_inc(init, 1)
            for p in range(2):
                pool.memset(V[p][:, :, :, 0:HD], 0.0).then_inc(init, 1)
                pool.memset(V[p][:, :, :, HD:HD + 1], 1.0).then_inc(init, 1)
                pool.memset(V[p][:, :, :, HD + 1:VC], 0.0).then_inc(init, 1)
                pool.memset(probs[:, p], 1.0).then_inc(init, 1)

            def lower(u, base, use):
                for w, name in enumerate("qk"):
                    pool.wait_ge(m_free, base + use[name] + 1)
                    pool.sem_inc(core.turns, 1)
                    pool.tensor_copy(parts[w][:, 1], rest[:]).then_inc(second_part, 1)
                    pool.wait_ge(second_part, 2 * u + (w + 1))
                    pool.tensor_tensor(parts[w][:, 2], rest[:], parts[w][:, 1], ALU.subtract).then_inc(low[w], 1)

            lower(0, 0, FIRST)
            pairs(pool, lambda t, p: lower(t + 1, base_of(t), USES))

        @block.scalar
        def _(act):
            def take(n, dst, src=M[:]):
                act.wait_ge(m_full, n)
                act.activation(dst, src, ACT.Copy).then_inc(m_free, 1)

            def take_first(n, w, u, first=False):
                act.wait_ge(m_full, n)
                if not first:
                    act.wait_ge(stored[w], 16 * u)
                act.activation(parts[w][:, 0], M[:], ACT.Copy).then_inc(first_part[w], 1)

            def take_values(n, p):
                take(n, V[p][:, :, :, 0:HD], M[:].rearrange("p (c h d) -> p c h d", c=NT, d=HD))

            def take_rows(b, n):
                take(n, Y[:, b + 1].rearrange("p c d -> p (c d)"))

            def evacuate(y, par):
                act.wait_ge(pv_done, y * 2 + 4)
                act.activation(Osb[:], O[par][:], ACT.Copy).then_inc(o_free, 1)

            act.preload_act_table(ACT.Exp)
            act.sem_inc(exped, 4)
            act.sem_inc(o_free, 1)
            take(1, xnT[:])
            take_first(2, 0, 0, first=True)
            take_first(3, 1, 0, first=True)
            act.wait_ge(init, 10)
            take_values(4, 0)

            def body(t, p):
                base = base_of(t)
                for g in range(STEPS):
                    for j in range(4):
                        act.wait_ge(decayed, t * (4 * STEPS) + (4 * g + j + 3))
                        pr = probs[:, g % 2, j]
                        act.activation(pr, pr, ACT.Exp).then_inc(exped, 1)
                        if j == 0 and g % 2:
                            evacuate(t * HG + (g // 2 - 1), (g // 2 - 1) % 2)
                        if j == 2:
                            if g == 1:
                                take(base + USES["xT"], xnT[:])
                            if g == 2:
                                take_first(base + USES["q"], 0, t + 1)
                            if g == 3:
                                take_first(base + USES["k"], 1, t + 1)
                            if g == 4:
                                take(base + USES["headsT"], heads_outT[:])
                            if g == 5:
                                take_rows(t - 1, base + USES["rows"])
                            if g == 6:
                                take_values(base + USES["v"], 1 - p)

            pairs(act, body)
            evacuate(HG * B - 1, (HG - 1) % 2)
            take(base_of(B) + 1, heads_outT[:])
            take_rows(B - 1, base_of(B) + 2)

        @block.tensor
        def _(pe):
            def scores(g, j, p):
                for kk in range(2):
                    kb, h = 2 * (g % 2) + kk, 4 * (g // 2) + j
                    mm = pe.matmul(S[j % 2][:, kk, :], Ks[p][:, h, kb * P:(kb + 1) * P], Qs[p][:, h, :],
                                   start=True, stop=True)
                mm.then_inc(s_full, 1)

            def values(g, half, p):
                kb = 2 * (g % 2) + half
                for j in range(4):
                    mm = pe.matmul(O[g // 2 % 2][VC * j:VC * (j + 1), :], V[p][:, kb, 4 * (g // 2) + j, :],
                                   probs[:, g % 2, j, half, :], start=(kb == 0), stop=(kb == NT - 1),
                                   skip_group_check=True)
                return mm

            def use_M(n, emit):
                pe.wait_ge(m_free, n)
                emit().then_inc(m_full, 1)

            def tiles_T(src):
                for c in range(NT):
                    mm = pe.transpose(M[:, c * P:(c + 1) * P], src[:, c, :], core.ident[:])
                return mm

            def rows(lhsT, w):
                for c in range(NT):
                    mm = pe.matmul(M[:, c * P:(c + 1) * P], lhsT[:, c * P:(c + 1) * P], w[:],
                                   start=True, stop=True)
                return mm

            def x_T(u, n):
                pe.wait_ge(xn_done, u + 1)
                use_M(n, lambda: tiles_T(xn))

            def project(w, n):
                use_M(n, lambda: pe.matmul(M[:], w[:], xnT[:], start=True, stop=True))

            def out_T(y):
                pe.wait_ge(o_free, y + 3)
                pe.wait_ge(heads_done, y + 3)
                for c in range(NT):
                    mm = pe.transpose(OT[:, c * P:(c + 1) * P], Osb[:, c * P:(c + 1) * P], core.ident[:])
                mm.then_inc(ot_full, 1)

            def heads_T(b, n):
                pe.wait_ge(heads_done, b * HG + (HG + 3))
                use_M(n, lambda: tiles_T(heads_out))

            pe.sem_inc(m_free, 1)
            pe.sem_inc(pv_done, 1)
            x_T(0, 1)
            project(core.Wq, 2)
            project(core.Wkr, 3)
            use_M(4, lambda: rows(xnT, core.Wvr))
            pe.wait_ge(m_free, 5)
            pe.wait_ge(init, 10)
            for half in range(2):
                values(STEPS - 2, half, 1)

            def body(t, p):
                base = base_of(t)
                for g in range(STEPS):
                    G = t * STEPS + g
                    for j in range(4):
                        if g == 0 and j == 0:
                            for w in range(2):
                                pe.wait_ge(spread[w], t * (16 * SLOTS) + 16 * SLOTS)
                        pe.wait_ge(decayed, t * (4 * STEPS) + (4 * g + j + 1))
                        scores(g, j, p)
                        if j == 0 and g % 2 == 0:
                            out_T(t * HG + (g // 2 - 2))
                        if j == 1:
                            if g == 1:
                                x_T(t + 1, base + USES["xT"])
                            if g == 2:
                                project(core.Wq, base + USES["q"])
                            if g == 3:
                                project(core.Wkr, base + USES["k"])
                            if g == 4:
                                heads_T(t - 1, base + USES["headsT"])
                            if g == 5:
                                use_M(base + USES["rows"], lambda: rows(heads_outT, core.Wo))
                            if g == 6:
                                use_M(base + USES["v"], lambda: rows(xnT, core.Wvr))
                        if j == 2:
                            pe.wait_ge(exped, G * 4 + 4)
                            if g % 2:
                                pe.wait_ge(o_free, t * HG + (g // 2 + 1))
                            values((g - 1) % STEPS, 0, p if g else 1 - p)
                        if j == 3:
                            values((g - 1) % STEPS, 1, p if g else 1 - p).then_inc(pv_done, 1)

            pairs(pe, body)
            out_T(HG * B - 2)
            pe.wait_ge(exped, 4 * STEPS * B + 4)
            for half in range(2):
                mm = values(STEPS - 1, half, (B - 1) % 2)
            mm.then_inc(pv_done, 1)
            out_T(HG * B - 1)
            heads_T(B - 1, base_of(B) + 1)
            use_M(base_of(B) + 2, lambda: rows(heads_outT, core.Wo))

        @block.vector
        def _(v):
            v.sem_inc(decayed, 2)
            v.sem_inc(heads_done, 1)

            def layer_norm(u):
                for c in range(NT):
                    op = v.tensor_scalar(xn[:, c], X[:, u, c], core.xmean[:, u, c:c + 1],
                                         core.xrstd[:, u, c:c + 1], ALU.subtract, ALU.mult)
                op.then_inc(xn_done, 1)

            def take_rest(w, u, first=False):
                v.wait_ge(first_part[w], u + 1)
                if w == 1:
                    v.wait_ge(low[0], u + 1)
                elif not first:
                    v.wait_ge(low[1], u)
                v.tensor_tensor(rest[:], M[:], parts[w][:, 0], ALU.subtract).then_inc(m_free, 1)

            ot = OT[:].rearrange("p (c j e) -> p c j e", c=NT, j=4)

            def take_sums(y):
                v.wait_ge(ot_full, y + 3)
                v.wait_ge(inverted, y * 4 + 9)
                v.tensor_scalar(one_over[:], ot[:, :, :, HD], 1e-30, None, ALU.max).then_inc(inverted, 1)

            def invert(y):
                v.wait_ge(inverted, y * 4 + 10)
                v.reciprocal(one_over[:], one_over[:]).then_inc(inverted, 1)

            def normalise(y, hg, heads_read=None):
                v.wait_ge(inverted, y * 4 + 11)
                if heads_read is not None:
                    v.wait_ge(m_full, heads_read)
                dst = heads_out[:, :, hg * 4 * HD:(hg + 1) * 4 * HD].rearrange("p c (j d) -> p c j d", d=HD)
                v.tensor_tensor(dst, ot[:, :, :, 0:HD], one_over[:].unsqueeze(3).to_broadcast([P, NT, 4, HD]),
                                ALU.mult).then_inc(heads_done, 1)
                v.scalar_tensor_tensor(core.fine[:], one_over[:], 2.0 ** -60, core.fine[:], ALU.is_ge, ALU.mult)\
                    .then_inc(inverted, 1)

            def check(y):
                v.wait_ge(inverted, y * 4 + 12)
                v.scalar_tensor_tensor(core.fine[:], one_over[:], 2.0 ** 60, core.fine[:], ALU.is_le, ALU.mult)\
                    .then_inc(inverted, 1)

            def statistics(b, n):
                v.wait_ge(m_free, n + 1)
                for c in range(NT):
                    op = v.bn_stats(core.yst[:, b + 1, c], Y[:, b + 1, c])
                return op

            layer_norm(0)
            take_rest(0, 0, first=True)
            take_rest(1, 0, first=True)
            v.memset(core.fine[:], 1.0).then_inc(inverted, 1)
            v.wait_ge(init, 10)
            v.wait_ge(const, 16)
            full = decay[:]
            decay_of = [bass.AP(full.tensor, full.offset + (NT - 1 - 2 * m) * P, [list(full.ap[0]), [-P, 2], [1, T]])
                        for m in range(2)]

            def body(t, p):
                base = base_of(t)
                for g in range(STEPS):
                    for j in range(4):
                        if j == 0:
                            v.wait_ge(pv_done, t * STEPS + (g + 1))
                        v.wait_ge(s_full, t * (4 * STEPS) + (4 * g + j + 1))
                        v.scalar_tensor_tensor(probs[:, g % 2, j], S[j % 2][:], CEILING, decay_of[g % 2], ALU.min,
                                               ALU.mult).then_inc(decayed, 1)
                        y, hg = t * HG + (g // 2 - 2), (g // 2 - 2) % HG
                        if g % 2 == 0:
                            if j == 1:
                                take_sums(y)
                            if j == 2:
                                invert(y)
                            if j == 3:
                                normalise(y, hg, base + USES["headsT"] if hg == 0 else None)
                        if g % 2 and j == 0:
                            check(y)
                        if j == 1 and g == 0:
                            layer_norm(t + 1)
                        if j == 0:
                            if g == 3:
                                take_rest(0, t + 1)
                            if g == 4:
                                take_rest(1, t + 1)
                            if g == 6:
                                statistics(t - 1, base + USES["rows"])

            pairs(v, body)
            for y, hg in ((HG * B - 2, HG - 2), (HG * B - 1, HG - 1)):
                take_sums(y)
                invert(y)
                normalise(y, hg)
                check(y)
            statistics(B - 1, base_of(B) + 2).then_inc(inverted, 1)
            v.wait_ge(inverted, HG * B * 4 + 10)


class Weights:

    def __init__(self, core, I):
        nc = core.nc
        sb = lambda n, s, d=F32: core.ctx.enter_context(nc.sbuf_tensor("w_" + n, s, d))
        self.loads = []
        F = I["L0_ffn_w_gate"].shape[0]
        self.ints = [sb(f"int{k}", [P, F], I32) for k in range(3)]
        by_block = lambda a: a.rearrange("(m p) d -> p m d", p=P)
        self.swiglu = self.layer(core, "swiglu", [
            *((self.ints[k][:].rearrange("p (m d) -> p m d", d=P), by_block(I["L0_ffn_" + n]))
              for k, n in enumerate(("w_gate", "w_up"))),
            (self.ints[2][:], I["L0_ffn_w_down"])])
        N = I["L1_attn_A_ssm"].shape[1]
        self.A, self.B, self.C = (sb(n, [D, N]) for n in "ABC")
        self.D, self.scale1 = sb("D", [D, 1]), sb("scale1", [D, 1])
        column = lambda a: a.unsqueeze(1)
        row = lambda a: a.unsqueeze(0)
        self.state_space = self.layer(core, "state_space", [
            (self.A[:], I["L1_attn_A_ssm"]), (self.B[:], I["L1_attn_B_ssm"]), (self.C[:], I["L1_attn_C_ssm"]),
            (self.D[:], column(I["L1_attn_D_ssm"])), (self.scale1[:], column(I["L1_attn_scale1"]))])
        F = I["L1_attn_w1"].shape[1]
        self.w1, self.w2, self.b1 = sb("w1", [D, F]), sb("w2", [P, F // P, D]), sb("b1", [P, F // P])
        self.b2, self.scale2 = sb("b2", [1, D]), sb("scale2", [D, 1])
        folded = lambda a: a.rearrange("(m p) -> p m", p=P)
        self.mlp = self.layer(core, "mlp", [
            (self.w1[:], I["L1_attn_w1"]), (self.w2[:], by_block(I["L1_attn_w2"])), (self.b1[:], folded(I["L1_attn_b1"])),
            (self.b2[:], row(I["L1_attn_b2"])), (self.scale2[:], column(I["L1_attn_scale2"]))])
        H = I["L1_ffn_enc_W"].shape[1]
        E, M, HH = I["L1_ffn_We1"].shape
        HC = H // P
        self.encW, self.encb = sb("encW", [D, H]), sb("encb", [P, HC])
        self.s2cW, self.s2cb = sb("s2cW", [P, HC, M]), sb("s2cb", [M, 1])
        self.rW1, self.rb1, self.rW2 = sb("rW1", [M, 64]), sb("rb1", [64, 1]), sb("rW2", [65, E])
        self.We1, self.be1 = sb("We1", [M, E, HH]), sb("be1", [HH, E])
        self.We2, self.be2 = sb("We2", [HH, E, M]), sb("be2", [E, M])
        self.c2sW, self.c2sb = sb("c2sW", [M, H]), sb("c2sb", [P, HC])
        self.decW, self.decb = sb("decW", [P, HC, D]), sb("decb", [1, D])
        self.gain, self.bias = sb("gain", [P, D]), sb("bias", [P, D])
        X = lambda n: I["L1_ffn_" + n]
        self.experts = self.layer(core, "experts", [
            (self.encW[:], X("enc_W")), (self.encb[:], folded(X("enc_b"))), (self.s2cW[:], by_block(X("s2c_W"))),
            (self.s2cb[:], column(X("s2c_b"))), (self.rW1[:], X("rW1")), (self.rb1[:], column(X("rb1"))),
            (self.rW2[0:64], X("rW2")), (self.rW2[64:65], row(X("rb2"))),
            (self.We1[:], X("We1").rearrange("e m h -> m e h")), (self.be1[:], X("be1").rearrange("e h -> h e")),
            (self.We2[:], X("We2").rearrange("e h m -> h e m")), (self.be2[:], X("be2")),
            (self.c2sW[:], X("c2s_W")), (self.c2sb[:], folded(X("c2s_b"))),
            (self.decW[:], by_block(X("dec_W"))), (self.decb[:], row(X("dec_b"))),
            (self.gain[:], X("ln_g").partition_broadcast(P)), (self.bias[:], X("ln_b").partition_broadcast(P))])

    def layer(self, core, name, loads):
        sem = core.sem(name + "_loaded")
        self.loads.append([(dst, src, sem) for dst, src in loads])
        return sem, 16 * len(loads)

    def load(self, nc, eng, n):
        with nc.allow_non_contiguous_dma("biases with their features on partitions"):
            for dst, src, loaded in self.loads[n]:
                eng.dma_start(dst, src).then_inc(loaded, 16)


def check_range(core, W):
    nc = core.nc
    with ExitStack() as ctx:
        least, fine = (ctx.enter_context(nc.sbuf_tensor(n, [P, 1], F32)) for n in ("r_least", "r_fine"))
        count = ctx.enter_context(nc.psum_tensor("r_count", [P, 1], F32))
        steps, least_done, counted = core.sem("r_steps"), core.sem("r_least_done"), core.sem("r_counted")
        known = core.sem("r_known")
        block = ctx.enter_context(nc.Block())

        @block.sync
        def _(sp):
            W.load(nc, sp, 0)
            sp.wait_ge(known, 1)

        @block.gpsimd
        def _(pool):
            pool.wait_ge(known, 1)

        @block.scalar
        def _(act):
            act.wait_ge(known, 1)

        @block.tensor
        def _(pe):
            pe.wait_ge(least_done, 1)
            pe.matmul(count[:], core.ones[:], least[:], start=True, stop=True).then_inc(counted, 1)
            pe.wait_ge(known, 1)

        @block.vector
        def _(v):
            tick = Tally(v, steps)
            v.tensor_reduce(least[:], core.fine[:].rearrange("p c j -> p (c j)"), AX.X, ALU.min).then_inc(least_done, 1)
            v.wait_ge(counted, 1)
            tick.step(v.tensor_scalar(fine[:], count[:], float(P), None, ALU.is_equal))
            v.tensor_copy(core.in_range[:], fine[:]).then_inc(known, 1)
            v.wait_ge(known, 1)


def attention_guarded(core, I):
    nc, B, NT, T = core.nc, core.B, core.NT, core.T
    X, Y = core.X, core.Y
    with ExitStack() as ctx:
        sb = lambda n, s, d=F32: ctx.enter_context(nc.sbuf_tensor("c_" + n, s, d))
        psum = lambda n, s: ctx.enter_context(nc.psum_tensor("c_" + n, s, F32))
        decay = sb("decay", [P, T + (NT - 1) * P])
        xn, xnT = sb("xn", [P, NT, D]), sb("xnT", [D, T])
        qT, kT = sb("qT", [D, T]), sb("kT", [D, T])
        q8, k8 = sb("q8", [HD, HEADS, T]), sb("k8", [HD, HEADS, T])
        qh, kh = sb("qh", [HD, T]), sb("kh", [HD, T])
        V = sb("V", [P, NT, D])
        probs, probsT = sb("probs", [P, T]), sb("probsT", [P, NT, P])
        top, total = sb("top", [P, 1]), sb("total", [P, 1])
        heads_out, heads_outT = sb("heads_out", [P, NT, D]), sb("heads_outT", [D, T])
        M, O = psum("M", [P, 512]), psum("O", [P, HD])
        dram = [nc.dram_tensor(f"c_{n}", [D, T], F32, kind="Internal").ap() for n in "qk"]
        const, moved, relay = core.sem("c_const"), core.sem("c_moved"), core.sem("c_relay")
        before = ["xn", "xT", "take_xT", "q", "take_q", "k", "take_k", "v", "take_v", "spread"]
        tile = ["scores", "clip", "decay", "top", "negate", "exp", "total", "invert", "weigh",
                "probsT", "take_probsT", "out", "take_out"]
        head = ["pick"] + [f"{s}{c}" for c in range(NT) for s in tile]
        after = ["headsT", "take_headsT", "rows", "take_rows"]
        BATCH = len(before) + HEADS * len(head) + len(after)
        block = ctx.enter_context(nc.Block())

        def turn(t, name, h=None):
            if name in before:
                return t * BATCH + (before.index(name) + 1)
            if name in after:
                return t * BATCH + (len(before) + HEADS * len(head) + after.index(name) + 1)
            return t * BATCH + h * len(head) + (len(before) + head.index(name) + 1)

        @block.sync
        def _(sp):
            sp.dma_start(decay[:], I["decay"]).then_inc(const, 16)
            sp.wait_ge(const, 16)
            with sp.Fori(0, B) as t:
                sp.wait_ge(relay, turn(t, "spread"))
                sp.dma_start(dram[0], qT[:]).then_inc(moved, 16)
                sp.dma_start(dram[1], kT[:]).then_inc(moved, 16)
                sp.wait_ge(moved, t * 64 + 32)
                for src, dst in zip(dram, (q8, k8)):
                    sp.dma_start(dst[:], src.rearrange("(h d) t -> d h t", d=HD)).then_inc(moved, 16)
                sp.wait_ge(moved, t * 64 + 64)
                sp.sem_inc(relay, 1)

        @block.gpsimd
        def _(pool):
            pool.wait_ge(const, 16)

        @block.scalar
        def _(act):
            act.preload_act_table(ACT.Exp)
            with act.Fori(0, B) as t:
                with act.Fori(0, HEADS) as h:
                    for c in range(NT):
                        act.wait_ge(relay, turn(t, f"exp{c}", h))
                        act.activation(probs[:], probs[:], ACT.Exp, bias=top[:]).then_inc(relay, 1)

        @block.tensor
        def _(pe):
            def tiles_T(src):
                for c in range(NT):
                    mm = pe.transpose(M[:, tile_of(core, c)], src[:, c, :], core.ident[:])
                mm.then_inc(relay, 1)

            def rows(lhsT, w):
                for c in range(NT):
                    mm = pe.matmul(M[:, tile_of(core, c)], lhsT[:, tile_of(core, c)], w[:], start=True, stop=True)
                mm.then_inc(relay, 1)

            with pe.Fori(0, B) as t:
                pe.wait_ge(relay, turn(t, "xT"))
                tiles_T(xn)
                pe.wait_ge(relay, turn(t, "q"))
                pe.matmul(M[:], core.Wq[:], xnT[:], start=True, stop=True).then_inc(relay, 1)
                pe.wait_ge(relay, turn(t, "k"))
                pe.matmul(M[:], core.Wkr[:], xnT[:], start=True, stop=True).then_inc(relay, 1)
                pe.wait_ge(relay, turn(t, "v"))
                rows(xnT, core.Wvr)
                with pe.Fori(0, HEADS) as h:
                    for c in range(NT):
                        pe.wait_ge(relay, turn(t, f"scores{c}", h))
                        pe.matmul(M[:], qh[:, tile_of(core, c)], kh[:], start=True, stop=True).then_inc(relay, 1)
                        pe.wait_ge(relay, turn(t, f"probsT{c}", h))
                        for k in range(NT):
                            mm = pe.transpose(M[:, tile_of(core, k)], probs[:, tile_of(core, k)], core.ident[:])
                        mm.then_inc(relay, 1)
                        pe.wait_ge(relay, turn(t, f"out{c}", h))
                        for k in range(NT):
                            mm = pe.matmul(O[:], probsT[:, k, :], V[:, k, bass.ds(h * HD, HD)], start=(k == 0),
                                           stop=(k == NT - 1))
                        mm.then_inc(relay, 1)
                pe.wait_ge(relay, turn(t, "headsT"))
                tiles_T(heads_out)
                pe.wait_ge(relay, turn(t, "rows"))
                rows(heads_outT, core.Wo)

        @block.vector
        def _(v):
            v.sem_inc(relay, 1)
            v.wait_ge(const, 16)

            def take(t, name, dst):
                v.wait_ge(relay, turn(t, name))
                v.tensor_copy(dst, M[:]).then_inc(relay, 1)

            with v.Fori(0, B) as t:
                v.wait_ge(relay, turn(t, "xn"))
                for c in range(NT):
                    op = v.tensor_scalar(xn[:, c], X[:, t, c], core.xmean[:, t, c:c + 1],
                                         core.xrstd[:, t, c:c + 1], ALU.subtract, ALU.mult)
                op.then_inc(relay, 1)
                take(t, "take_xT", xnT[:])
                take(t, "take_q", qT[:])
                take(t, "take_k", kT[:])
                take(t, "take_v", V[:].rearrange("p c d -> p (c d)"))
                with v.Fori(0, HEADS) as h:
                    v.wait_ge(relay, turn(t, "pick", h))
                    v.tensor_copy(qh[:], q8[:, h, :])
                    v.tensor_copy(kh[:], k8[:, h, :]).then_inc(relay, 1)
                    for c in range(NT):
                        v.wait_ge(relay, turn(t, f"clip{c}", h))
                        v.tensor_scalar(probs[:], M[:], -1e4, 1e4, ALU.max, ALU.min).then_inc(relay, 1)
                        v.wait_ge(relay, turn(t, f"decay{c}", h))
                        v.tensor_tensor(probs[:], probs[:], decay[:, (NT - 1 - c) * P:(NT - 1 - c) * P + T],
                                        ALU.mult).then_inc(relay, 1)
                        v.wait_ge(relay, turn(t, f"top{c}", h))
                        v.tensor_reduce(top[:], probs[:], AX.X, ALU.max).then_inc(relay, 1)
                        v.wait_ge(relay, turn(t, f"negate{c}", h))
                        v.tensor_scalar(top[:], top[:], -1.0, None, ALU.mult).then_inc(relay, 1)
                        v.wait_ge(relay, turn(t, f"total{c}", h))
                        v.tensor_reduce(total[:], probs[:], AX.X, ALU.add).then_inc(relay, 1)
                        v.wait_ge(relay, turn(t, f"invert{c}", h))
                        v.reciprocal(total[:], total[:]).then_inc(relay, 1)
                        v.wait_ge(relay, turn(t, f"weigh{c}", h))
                        v.tensor_scalar(probs[:], probs[:], total[:], None, ALU.mult).then_inc(relay, 1)
                        v.wait_ge(relay, turn(t, f"take_probsT{c}", h))
                        v.tensor_copy(probsT[:].rearrange("p k q -> p (k q)"), M[:]).then_inc(relay, 1)
                        v.wait_ge(relay, turn(t, f"take_out{c}", h))
                        v.tensor_copy(heads_out[:, c, bass.ds(h * HD, HD)], O[:]).then_inc(relay, 1)
                take(t, "take_headsT", heads_outT[:])
                v.wait_ge(relay, turn(t, "take_rows"))
                v.tensor_copy(Y[:, t + 1].rearrange("p c d -> p (c d)"), M[:])
                for c in range(NT):
                    op = v.bn_stats(core.yst[:, t + 1, c], M[:, tile_of(core, c)])
                op.then_inc(relay, 1)


class Bank:

    def __init__(self, core, ctx, name, shape=None):
        self.t = ctx.enter_context(core.nc.psum_tensor(name, shape or [P, 512], F32))
        self.full, self.free = core.sem(name + "_full"), core.sem(name + "_free")

    def open(self, pe):
        pe.sem_inc(self.free, 1)

    def fill(self, pe, n):
        pe.wait_ge(self.free, n)

    def filled(self, ins):
        ins.then_inc(self.full, 1)

    def read(self, eng, n):
        eng.wait_ge(self.full, n)

    def emptied(self, ins):
        ins.then_inc(self.free, 1)

    def after(self, eng, n):
        eng.wait_ge(self.free, n + 1)


def in_pairs(eng, B, body):
    with eng.Fori(0, B // 2) as i:
        for p in range(2):
            body(i * 2 + p, p, i)


def transposed(core, pe, bank, n, src):
    bank.fill(pe, n)
    for c in range(core.NT):
        mm = pe.transpose(bank.t[:, c * P:(c + 1) * P], src[:, c, :], core.ident[:])
    bank.filled(mm)


def tile_of(core, c):
    return slice(c * P, (c + 1) * P)


def add_normed(core, name, rms=False, affine=None, store=None):
    nc, B, NT = core.nc, core.B, core.NT
    X, Y = core.X, core.Y
    with ExitStack() as ctx:
        sb = lambda n, s, d=F32: ctx.enter_context(nc.sbuf_tensor(f"{name}_{n}", s, d))
        mean, var, tmp, rstd, shift = (sb(n, [P, B, NT]) for n in ("mean", "var", "tmp", "rstd", "shift"))
        sem = lambda n: core.sem(f"{name}_{n}")
        steps, rooted, want_root, shift_done = sem("steps"), sem("rooted"), sem("want_root"), sem("shift_done")
        act_normed, dve_normed, added = sem("act_normed"), sem("dve_normed"), sem("added")
        counted = sem("counted")
        if affine:
            gain, bias, (loaded, NLOAD) = affine
            scaled, shifted = sem("scaled"), sem("shifted")
        if store is not None:
            out = store.rearrange("b (c p) d -> p b c d", p=P)
            stored = sem("stored")
        rounds = 2 if affine else 1
        roots = rounds + (0 if store is not None else 2 if rms else 1)
        act_tiles = [NT, NT // 2] if affine else [NT - 1]
        block = ctx.enter_context(nc.Block())

        if store is not None:
            @block.sync
            def _(sp):
                with sp.Fori(0, B) as t:
                    sp.wait_ge(added, t + 1)
                    sp.sem_inc(core.turns, 1)
                    sp.dma_start(out[:, t], X[:, t]).then_inc(stored, 16)
                sp.wait_ge(stored, 16 * B)

        @block.gpsimd
        def _(pool):
            with pool.Fori(0, B) as t:
                if affine:
                    pool.wait_ge(scaled, t + 1)
                    pool.sem_inc(core.turns, 1)
                    pool.tensor_tensor(Y[:, t + 1], Y[:, t + 1], bias[:].unsqueeze(1).to_broadcast([P, NT, D]),
                                       ALU.add).then_inc(shifted, 1)
                else:
                    pool.wait_ge(act_normed, t + 1)
                    pool.sem_inc(core.turns, 1)
                    pool.wait_ge(dve_normed, t + 1)
                    pool.sem_inc(core.turns, 1)
                    pool.tensor_tensor(X[:, t], X[:, t], Y[:, t + 1], ALU.add).then_inc(added, 1)

        @block.scalar
        def _(act):
            def root(n):
                act.wait_ge(want_root, n)
                act.activation(tmp[:], tmp[:], ACT.Sqrt).then_inc(rooted, 1)

            for k in range(rounds):
                root(k + 1)
                act.wait_ge(shift_done, k + 1)
                with act.Fori(0, B) as t:
                    for c in range(act_tiles[k]):
                        y = Y[:, t + 1, c]
                        op = act.activation(y, y, ACT.Identity, bias=shift[:, t, c:c + 1], scale=rstd[:, t, c:c + 1])
                    op.then_inc(act_normed, 1)
            for k in range(rounds, roots):
                root(k + 1)

        @block.vector
        def _(v):
            tick = Tally(v, steps)

            def inverse_root(n, dst, eps):
                v.tensor_scalar(tmp[:], var[:], eps, None, ALU.add).then_inc(want_root, 1)
                v.wait_ge(rooted, n)
                tick.step(v.reciprocal(dst, tmp[:]))

            def normalise(t, k):
                for c in range(act_tiles[k], NT):
                    y = Y[:, t + 1, c]
                    op = v.tensor_scalar(y, y, rstd[:, t, c:c + 1], shift[:, t, c:c + 1], ALU.mult, ALU.add)
                op.then_inc(dve_normed, 1)

            def statistics(st, src):
                for c in range(NT):
                    op = v.bn_stats(st[:, c], src[:, c])
                op.then_inc(counted, 1)

            for k in range(rounds):
                moments(v, tick, core.yst[:, 1:B + 1], mean[:], var[:], tmp[:])
                inverse_root(k + 1, rstd[:], 1e-5)
                tick.mark(v.scalar_tensor_tensor(shift[:], mean[:], -1.0, rstd[:], ALU.mult, ALU.mult))
                tick.settle()
                v.sem_inc(shift_done, 1)
                if k < rounds - 1:
                    v.wait_ge(loaded, NLOAD)

                    def scale(t):
                        v.wait_ge(act_normed, t + 1)
                        v.tensor_tensor(Y[:, t + 1], Y[:, t + 1], gain[:].unsqueeze(1).to_broadcast([P, NT, D]),
                                        ALU.mult).then_inc(scaled, 1)

                    scale(0)
                    with v.Fori(0, B - 1) as t:
                        scale(t + 1)
                        v.wait_ge(shifted, t + 1)
                        statistics(core.yst[:, t + 1], Y[:, t + 1])
                    v.wait_ge(shifted, B)
                    statistics(core.yst[:, B], Y[:, B])
                    v.wait_ge(counted, B)
            last = rounds - 1
            if store is not None:
                with v.Fori(0, B) as t:
                    normalise(t, last)
                    v.wait_ge(act_normed, t + (B * last + 1))
                    v.wait_ge(dve_normed, t + 1)
                    v.tensor_tensor(X[:, t], X[:, t], Y[:, t + 1], ALU.add).then_inc(added, 1)
            else:
                normalise(0, last)
                with v.Fori(0, B - 1) as t:
                    normalise(t + 1, last)
                    v.wait_ge(added, t + 1)
                    statistics(core.xst[:, t], X[:, t])
                v.wait_ge(added, B)
                statistics(core.xst[:, B - 1], X[:, B - 1])
                v.wait_ge(counted, B)
                moments(v, tick, core.xst[:], core.xmean[:, 0:B], var[:], tmp[:])
                inverse_root(rounds + 1, core.xrstd[:, 0:B], 1e-5)
                if rms:
                    r = core.xrstd[:, 0:B]
                    tick.step(v.tensor_tensor(var[:], var[:], r, ALU.mult))
                    tick.step(v.tensor_tensor(var[:], var[:], r, ALU.mult))
                    inverse_root(rounds + 2, tmp[:], 1e-6)
                    tick.step(v.tensor_tensor(core.urstd[:, 0:B], tmp[:], r, ALU.mult))


def take_transposed(eng_copy, eng, bank, n, dst):
    bank.read(eng, n)
    bank.emptied(eng_copy(dst, bank.t[:, 0:dst.shape[-1]]))


def swiglu(core, I, W):
    nc, B, NT, T = core.nc, core.B, core.NT, core.T
    X, Y = core.X, core.Y
    F = I["L0_ffn_w_gate"].shape[0]
    FC = F // P
    S = 1.0 / 127.0
    with ExitStack() as ctx:
        sb = lambda n, s, d=F32: ctx.enter_context(nc.sbuf_tensor("f_" + n, s, d))
        sem = lambda n: core.sem("f_" + n)
        floats = [sb(f"float{k}", [P, F]) for k in range(3)]
        wT = [sb(f"wT{k}", [P, FC, P]) for k in range(3)]
        xn, xnT = sb("xn", [P, NT, D]), [sb(f"xnT{p}", [D, T]) for p in range(2)]
        gated = [sb(f"gated{p}", [P, T]) for p in range(2)]
        hid = [sb(f"hid{p}", [P, FC, T]) for p in range(2)]
        TP = Bank(core, ctx, "f_TP")
        G = [ctx.enter_context(nc.psum_tensor(f"f_G{p}", [P, 512], F32)) for p in range(2)]
        U = [ctx.enter_context(nc.psum_tensor(f"f_U{p}", [P, 512], F32)) for p in range(2)]
        OUT = [Bank(core, ctx, f"f_OUT{p}") for p in range(2)]
        cast, xn_done = sem("cast"), sem("xn_done")
        gu_full, gated_done, hid_done = sem("gu_full"), sem("gated_done"), sem("hid_done")
        block = ctx.enter_context(nc.Block())
        xT_use = lambda u: u + 4

        @block.sync
        def _(sp):
            for n in range(1, 4):
                W.load(nc, sp, n)

        @block.scalar
        def _(act):
            take_T = lambda u, p: take_transposed(lambda o, i: act.activation(o, i, ACT.Copy), act, TP, xT_use(u),
                                                  xnT[p][:])
            act.preload_act_table(ACT.Silu)
            take_T(0, 0)

            def body(t, p, i):
                for m in range(FC):
                    n = t * FC + m
                    act.wait_ge(gu_full, n + 1)
                    act.wait_ge(hid_done, n + 1)
                    act.activation(gated[(p + m) % 2][:], G[(p + m) % 2][:], ACT.Silu, scale=S)\
                       .then_inc(gated_done, 1)
                take_T(t + 1, 1 - p)

            in_pairs(act, B, body)

        @block.tensor
        def _(pe):
            for bank in (TP, *OUT):
                bank.open(pe)
            for k in range(3):
                pe.wait_ge(cast, k + 1)
                TP.fill(pe, k + 1)
                for m in range(FC):
                    mm = pe.transpose(TP.t[:, tile_of(core, m)], floats[k][:, tile_of(core, m)], core.ident[:])
                TP.filled(mm)

            def x_T(u):
                pe.wait_ge(xn_done, u + 1)
                transposed(core, pe, TP, xT_use(u), xn)

            x_T(0)

            def body(t, p, i):
                TP.after(pe, xT_use(t))
                for m in range(FC):
                    b = (p + m) % 2
                    pe.wait_ge(hid_done, t * FC + (m + 1))
                    pe.matmul(G[b][:], wT[0][:, m, :], xnT[p][:], start=True, stop=True)
                    pe.matmul(U[b][:], wT[1][:, m, :], xnT[p][:], start=True, stop=True).then_inc(gu_full, 1)
                x_T(t + 1)
                pe.wait_ge(hid_done, t * FC + (FC + 2))
                OUT[p].fill(pe, i + 1)
                for c in range(NT):
                    for m in range(FC):
                        mm = pe.matmul(OUT[p].t[:, tile_of(core, c)], hid[p][:, m, tile_of(core, c)], wT[2][:, m, :],
                                       start=(m == 0), stop=(m == FC - 1))
                OUT[p].filled(mm)

            in_pairs(pe, B, body)

        @block.vector
        def _(v):
            v.sem_inc(hid_done, 2)
            v.wait_ge(*W.swiglu)
            for k in range(3):
                v.tensor_copy(floats[k][:], W.ints[k][:]).then_inc(cast, 1)
            for k in range(3):
                take_transposed(v.tensor_copy, v, TP, k + 1, wT[k][:].rearrange("p m d -> p (m d)"))

            def layer_norm(u):
                for c in range(NT):
                    op = v.tensor_scalar(xn[:, c], X[:, u, c], core.xmean[:, u, c:c + 1],
                                         core.xrstd[:, u, c:c + 1], ALU.subtract, ALU.mult)
                op.then_inc(xn_done, 1)

            layer_norm(0)
            TP.after(v, xT_use(0))

            def body(t, p, i):
                layer_norm(t + 1)
                for m in range(FC):
                    n = t * FC + m
                    v.wait_ge(gated_done, n + 1)
                    v.scalar_tensor_tensor(hid[p][:, m], U[(p + m) % 2][:], S * S, gated[(p + m) % 2][:], ALU.mult,
                                           ALU.mult).then_inc(hid_done, 1)
                OUT[p].read(v, i + 1)
                v.tensor_copy(Y[:, t + 1].rearrange("p c d -> p (c d)"), OUT[p].t[:])
                for c in range(NT):
                    op = v.bn_stats(core.yst[:, t + 1, c], OUT[p].t[:, tile_of(core, c)])
                OUT[p].emptied(op)

            in_pairs(v, B, body)


def state_space(core, I, W):
    nc, B, NT, T = core.nc, core.B, core.NT, core.T
    X, Y = core.X, core.Y
    N = I["L1_attn_A_ssm"].shape[1]
    lo, hi = math.log(0.001), math.log(0.1)
    dt = [math.exp(lo + (hi - lo) * n / (N - 1)) for n in range(N)]
    FLY = 4
    with ExitStack() as ctx:
        sb = lambda n, s, d=F32: ctx.enter_context(nc.sbuf_tensor("m_" + n, s, d))
        sem = lambda n: core.sem("m_" + n)
        A, Bs, C, Ds, s1 = W.A, W.B, W.C, W.D, W.scale1
        dA, coef = sb("dA", [D, N]), sb("coef", [D, N])
        diag = sb("diag", [D, N + 1, D])
        u, uT = sb("u", [P, NT, D]), [sb(f"uT{p}", [D, T]) for p in range(2)]
        state = sb("state", [D, FLY, T])
        ysb = sb("ysb", [D, T])
        shift = sb("shift", [P, B, NT])
        TP = Bank(core, ctx, "m_TP")
        YT = [Bank(core, ctx, f"m_YT{p}") for p in range(2)]
        Z = Bank(core, ctx, "m_Z")
        dA_done, steps, diag_done = sem("dA_done"), sem("steps"), sem("diag_done")
        u_done, scanned, summed, a_done, shift_done = (sem(n) for n in ("u_done", "scanned", "summed", "a_done", "shift_done"))
        block = ctx.enter_context(nc.Block())
        xT_use = lambda b: b + 1

        @block.scalar
        def _(act):
            act.wait_ge(*W.state_space)
            act.activation(A[:], A[:], ACT.Exp).then_inc(dA_done, 1)
            act.wait_ge(dA_done, 1)
            for n in range(N):
                op = act.activation(dA[:, n:n + 1], A[:, n:n + 1], ACT.Exp, scale=-dt[n])
            op.then_inc(dA_done, 1)
            act.wait_ge(shift_done, 1)

            def take_u(b, p):
                take_transposed(lambda o, i: act.activation(o, i, ACT.Copy), act, TP, xT_use(b), uT[p][:])

            take_u(0, 0)

            def body(t, p, i):
                for c in range(NT):
                    op = act.activation(Y[:, t + 1, c], X[:, t, c], ACT.Identity, bias=shift[:, t, c:c + 1],
                                        scale=core.xrstd[:, t, c:c + 1])
                op.then_inc(a_done, 1)
                take_u(t + 1, 1 - p)
                YT[p].read(act, i + 1)
                Z.read(act, t + 1)
                YT[p].emptied(act.activation(ysb[:], YT[p].t[:], ACT.Copy))

            in_pairs(act, B, body)

        @block.tensor
        def _(pe):
            for bank in (TP, *YT):
                bank.open(pe)
            pe.sem_inc(summed, FLY)

            def u_T(b):
                pe.wait_ge(u_done, b + 1)
                transposed(core, pe, TP, xT_use(b), u)

            u_T(0)
            pe.wait_ge(diag_done, 1)

            def body(t, p, i):
                u_T(t + 1)
                TP.after(pe, xT_use(t))
                YT[p].fill(pe, i + 1)
                for n in range(N):
                    pe.wait_ge(scanned, t * N + (n + 1))
                    pe.matmul(YT[p].t[:], diag[:, n, :], state[:, n % FLY, :], start=(n == 0), stop=False)\
                      .then_inc(summed, 1)
                YT[p].filled(pe.matmul(YT[p].t[:], diag[:, N, :], uT[p][:], start=False, stop=True))
                YT[p].after(pe, i + 1)
                Z.fill(pe, t + 2)
                for c in range(NT):
                    mm = pe.transpose(Z.t[:, tile_of(core, c)], ysb[:, tile_of(core, c)], core.ident[:])
                Z.filled(mm)

            in_pairs(pe, B, body)

        @block.vector
        def _(v):
            tick = Tally(v, steps)
            tick.step(v.memset(Z.t[:], 0.0))
            v.sem_inc(Z.full, 1)
            v.sem_inc(Z.free, 1)
            v.sem_inc(a_done, 1)
            v.scalar_tensor_tensor(shift[:], core.xmean[:, 0:B], -1.0, core.xrstd[:, 0:B], ALU.mult, ALU.mult)\
             .then_inc(shift_done, 1)

            def rms_norm(b):
                for c in range(NT):
                    op = v.tensor_scalar(u[:, c], X[:, b, c], core.xmean[:, b, c:c + 1],
                                         core.urstd[:, b, c:c + 1], ALU.subtract, ALU.mult)
                op.then_inc(u_done, 1)

            rms_norm(0)
            v.wait_ge(dA_done, 2)
            tick.step(v.tensor_scalar(coef[:], dA[:], -1.0, 1.0, ALU.mult, ALU.add))
            tick.step(v.reciprocal(A[:], A[:]))
            tick.step(v.tensor_tensor(coef[:], coef[:], Bs[:], ALU.mult))
            tick.step(v.tensor_tensor(coef[:], coef[:], A[:], ALU.mult))
            tick.step(v.tensor_tensor(coef[:], coef[:], C[:], ALU.mult))
            tick.step(v.tensor_scalar(coef[:], coef[:], s1[:], None, ALU.mult))
            tick.step(v.tensor_tensor(Ds[:], Ds[:], s1[:], ALU.mult))
            for n in range(N + 1):
                by = coef[:, n:n + 1] if n < N else Ds[:]
                op = v.tensor_scalar(diag[:, n], core.ident[:], by, None, ALU.mult)
            op.then_inc(diag_done, 1)

            def finish(b):
                Z.read(v, b + 2)
                v.wait_ge(a_done, b + 2)
                y = Y[:, b + 1].rearrange("p c d -> p (c d)")
                Z.emptied(v.tensor_tensor(y, y, Z.t[:], ALU.add))
                Z.after(v, b + 2)
                for c in range(NT):
                    v.bn_stats(core.yst[:, b + 1, c], Y[:, b + 1, c])

            def body(t, p, i):
                TP.after(v, xT_use(t))
                for n in range(N):
                    v.wait_ge(summed, t * N + (n + 1))
                    v.tensor_tensor_scan(state[:, n % FLY, :], dA[:, n:n + 1].to_broadcast([D, T]), uT[p][:], 0.0,
                                         ALU.mult, ALU.add).then_inc(scanned, 1)
                    if n == 0:
                        rms_norm(t + 1)
                    if n == FLY + 1:
                        finish(t - 1)

            in_pairs(v, B, body)
            finish(B - 1)


def mlp(core, I, W):
    nc, B, NT, T = core.nc, core.B, core.NT, core.T
    Y = core.Y
    F = I["L1_attn_w1"].shape[1]
    FC = F // P
    with ExitStack() as ctx:
        sb = lambda n, s, d=F32: ctx.enter_context(nc.sbuf_tensor("g_" + n, s, d))
        sem = lambda n: core.sem("g_" + n)
        w1, w2, b1, b2, s2 = W.w1, W.w2, W.b1, W.b2, W.scale2
        mean, var, tmp, rstd = (sb(n, [P, B, NT]) for n in ("mean", "var", "tmp", "rstd"))
        yn, ynT = sb("yn", [P, NT, D]), [sb(f"ynT{p}", [D, T]) for p in range(2)]
        hid = [sb(f"hid{p}", [P, FC, T]) for p in range(2)]
        TP = Bank(core, ctx, "g_TP")
        H = [Bank(core, ctx, f"g_H{k}") for k in range(FC)]
        OUT = [Bank(core, ctx, f"g_OUT{p}") for p in range(2)]
        steps, scaled, rooted, want_root = (sem(n) for n in ("steps", "scaled", "rooted", "want_root"))
        yn_done = sem("yn_done")
        block = ctx.enter_context(nc.Block())
        yT_use = lambda b: b + 1

        @block.scalar
        def _(act):
            act.wait_ge(want_root, 1)
            act.activation(tmp[:], tmp[:], ACT.Sqrt).then_inc(rooted, 1)
            act.preload_act_table(ACT.Gelu)
            act.wait_ge(*W.mlp)

            def body(t, p, i):
                for m in range(FC):
                    H[m].read(act, t + 1)
                    H[m].emptied(act.activation(hid[p][:, m], H[m].t[:], ACT.Gelu, bias=b1[:, m:m + 1]))

            in_pairs(act, B, body)

        @block.tensor
        def _(pe):
            for bank in (TP, *H, *OUT):
                bank.open(pe)
            pe.wait_ge(scaled, 1)

            def y_T(b):
                pe.wait_ge(yn_done, b + 1)
                transposed(core, pe, TP, yT_use(b), yn)

            y_T(0)

            def body(t, p, i):
                TP.after(pe, yT_use(t))
                for m in range(FC):
                    H[m].fill(pe, t + 1)
                    H[m].filled(pe.matmul(H[m].t[:], w1[:, tile_of(core, m)], ynT[p][:], start=True, stop=True))
                y_T(t + 1)
                OUT[p].fill(pe, i + 1)
                for c in range(NT):
                    o = OUT[p].t[:, tile_of(core, c)]
                    pe.matmul(o, core.ones[0:1, :], b2[:], start=True, stop=False)
                    for m in range(FC):
                        if c == 0:
                            H[m].after(pe, t + 1)
                        mm = pe.matmul(o, hid[p][:, m, tile_of(core, c)], w2[:, m, :], start=False, stop=(m == FC - 1))
                OUT[p].filled(mm)

            in_pairs(pe, B, body)

        @block.vector
        def _(v):
            tick = Tally(v, steps)
            moments(v, tick, core.yst[:, 1:B + 1], mean[:], var[:], tmp[:])
            tick.step(v.tensor_tensor(mean[:], mean[:], mean[:], ALU.mult))
            v.scalar_tensor_tensor(tmp[:], var[:], 1e-6, mean[:], ALU.add, ALU.add).then_inc(want_root, 1)
            v.wait_ge(*W.mlp)
            v.tensor_scalar(w1[:], w1[:], s2[:], None, ALU.mult).then_inc(scaled, 1)
            v.wait_ge(rooted, 1)
            tick.step(v.reciprocal(rstd[:], tmp[:]))

            def rms_norm(b, last=False):
                for c in range(NT):
                    op = v.tensor_scalar(yn[:, c], Y[:, b + 1, c], rstd[:, b, c:c + 1], None, ALU.mult)
                op.then_inc(yn_done, 1)

            def take_T(b, p):
                take_transposed(v.tensor_copy, v, TP, yT_use(b), ynT[p][:])

            rms_norm(0)
            take_T(0, 0)

            def body(t, p, i, last=False):
                rms_norm(t + 1) if not last else v.tensor_copy(yn[:], Y[:, 0]).then_inc(yn_done, 1)
                take_T(t + 1, 1 - p)
                OUT[p].read(v, i + 1)
                y = Y[:, t + 1].rearrange("p c d -> p (c d)")
                OUT[p].emptied(v.tensor_tensor(y, y, OUT[p].t[:], ALU.add))
                OUT[p].after(v, i + 1)
                for c in range(NT):
                    v.bn_stats(core.yst[:, t + 1, c], Y[:, t + 1, c])

            with v.Fori(0, B // 2 - 1) as i:
                for p in range(2):
                    body(i * 2 + p, p, i)
            body(B - 2, 0, B // 2 - 1)
            body(B - 1, 1, B // 2 - 1, last=True)


def experts(core, I, W):
    nc, B, NT, T = core.nc, core.B, core.NT, core.T
    X, Y = core.X, core.Y
    H = I["L1_ffn_enc_W"].shape[1]
    E, M, HH = I["L1_ffn_We1"].shape
    HC = H // P
    BIG = 64.0
    with ExitStack() as ctx:
        sb = lambda n, s, d=F32: ctx.enter_context(nc.sbuf_tensor("e_" + n, s, d))
        sem = lambda n: core.sem("e_" + n)
        encW, encb, s2cW, s2cb, rW1, rb1, rW2 = W.encW, W.encb, W.s2cW, W.s2cb, W.rW1, W.rb1, W.rW2
        We1, be1, We2, be2, c2sW, c2sb = W.We1, W.be1, W.We2, W.be2, W.c2sW, W.c2sb
        decW, decb = W.decW, W.decb
        xn, xnT = sb("xn", [P, NT, D]), [sb(f"xnT{p}", [D, T]) for p in range(2)]
        enc, contT, rT = sb("enc", [P, HC, T]), sb("contT", [M, T]), sb("rT", [65, T])
        hid = [sb(f"hid{p}", [HH, E, T]) for p in range(2)]
        gates = [sb(f"gates{p}", [P, NT, E]) for p in range(2)]
        gatesT, moeT, dec_in = sb("gatesT", [E, T]), sb("moeT", [M, T]), sb("dec_in", [P, HC, T])
        weighted, moe = sb("weighted", [P, 2, E, M]), sb("moe", [P, NT, M])
        number = sb("number", [P, E])
        logit, hit, cand = sb("logit", [P, NT, E]), sb("hit", [P, NT, E]), sb("cand", [P, NT, E])
        mask = [sb(f"mask{k}", [P, NT, E]) for k in range(2)]
        top = [sb(f"top{k}", [P, NT]) for k in range(2)]
        first, gap, share = sb("first", [P, NT]), sb("gap", [P, 2, NT]), sb("share", [P, 2, NT])

        TP = Bank(core, ctx, "e_TP")
        EB = [Bank(core, ctx, f"e_E{m}") for m in range(HC)]
        FB = Bank(core, ctx, "e_F")
        HB = [Bank(core, ctx, f"e_H{k}") for k in range(2)]
        GB = [Bank(core, ctx, f"e_G{k}") for k in range(2)]
        steps, init, xn_done = sem("steps"), sem("init"), sem("xn_done")
        gap_done, share_done, gates_done, moe_done = (sem(n) for n in ("gap_done", "share_done", "gates_done",
                                                                       "moe_done"))
        xT_use = lambda u: u * 2 + 1
        dec_use = lambda t: t * 2 + 2
        enc_use, c2s_use = (lambda t: t * 2 + 1), (lambda t: t * 2 + 2)
        cont_use, router_use, gatesT_use, moeT_use, logits_use = (lambda t, k=k: t * 5 + k for k in range(1, 6))
        block = ctx.enter_context(nc.Block())

        @block.gpsimd
        def _(pool):
            for k in range(E):
                pool.memset(number[:, k:k + 1], float(k)).then_inc(init, 1)
            pool.wait_ge(init, E)
            pool.memset(rT[64:65], 1.0).then_inc(init, 1)
            pool.wait_ge(init, E + 1)
            pool.memset(hid[1][:], 0.0).then_inc(init, 1)
            pool.memset(gates[1][:], 0.0).then_inc(init, 1)

        @block.scalar
        def _(act):
            act.preload_act_table(ACT.Sigmoid)
            act.wait_ge(*W.experts)

            def body(t, p, i):
                for m in range(HC):
                    EB[m].read(act, enc_use(t))
                    EB[m].emptied(act.activation(enc[:, m], EB[m].t[:], ACT.Sigmoid, bias=encb[:, m:m + 1]))
                FB.read(act, router_use(t))
                FB.emptied(act.activation(rT[0:64], FB.t[0:64], ACT.Tanh, bias=rb1[:]))
                for e in range(0, E, 2):
                    HB[0].read(act, t * (E // 2) + (e // 2 + 1))
                    HB[0].emptied(act.activation(hid[p][:, e], HB[0].t[:], ACT.Relu, bias=be1[:, e:e + 1]))
                    if e == E // 2:
                        for m in range(HC):
                            EB[m].read(act, c2s_use(t))
                            EB[m].emptied(act.activation(dec_in[:, m], EB[m].t[:], ACT.Sigmoid, bias=c2sb[:, m:m + 1]))
                take_decoded(t - 1, dec_use(t))
                act.wait_ge(gap_done, t + 1)
                act.activation(share[:], gap[:], ACT.Sigmoid).then_inc(share_done, 1)

            def take_decoded(b, n):
                TP.read(act, n)
                TP.emptied(act.activation(Y[:, b + 1].rearrange("p c d -> p (c d)"), TP.t[:], ACT.Sigmoid))

            in_pairs(act, B, body)
            for m in range(HC):
                EB[m].read(act, c2s_use(B) - 1)
                EB[m].emptied(act.activation(dec_in[:, m], EB[m].t[:], ACT.Sigmoid, bias=c2sb[:, m:m + 1]))
            take_decoded(B - 1, dec_use(B))

        @block.tensor
        def _(pe):
            for bank in (TP, *EB, FB, *HB, *GB):
                bank.open(pe)
            pe.wait_ge(*W.experts)
            pe.wait_ge(init, E + 3)

            def x_T(u):
                pe.wait_ge(xn_done, u + 1)
                transposed(core, pe, TP, xT_use(u), xn)

            def encoder(t, p):
                TP.after(pe, xT_use(t))
                for m in range(HC):
                    EB[m].fill(pe, enc_use(t))
                    EB[m].filled(pe.matmul(EB[m].t[:], encW[:, tile_of(core, m)], xnT[p][:], start=True, stop=True))

            def cells(t):
                for m in range(HC):
                    EB[m].after(pe, enc_use(t))
                FB.fill(pe, cont_use(t))
                for m in range(HC):
                    mm = pe.matmul(FB.t[0:M], s2cW[:, m, :], enc[:, m, :], start=(m == 0), stop=(m == HC - 1))
                FB.filled(mm)

            def router(t):
                FB.fill(pe, router_use(t))
                pe.sem_inc(core.turns, 1)
                FB.filled(pe.matmul(FB.t[0:64], rW1[:], contT[:], start=True, stop=True))

            def expert_in(t, e):
                HB[e % 2].fill(pe, t * (E // 2) + (e // 2 + 1))
                HB[e % 2].filled(pe.matmul(HB[e % 2].t[:], We1[:, e, :], contT[:], start=True, stop=True))

            def logits(t):
                FB.fill(pe, logits_use(t))
                for c in range(NT):
                    mm = pe.matmul(FB.t[:, c * E:(c + 1) * E], rT[:, tile_of(core, c)], rW2[:], start=True, stop=True)
                FB.filled(mm)

            def expert_out(t, c, q):
                if c == 0:
                    for k in range(2):
                        HB[k].fill(pe, t * (E // 2) + 1)
                GB[c % 2].fill(pe, t * 2 + (c // 2 + 1))
                for e in range(E):
                    mm = pe.matmul(GB[c % 2].t[:, e * M:(e + 1) * M], hid[q][:, e, tile_of(core, c)], We2[:, e, :],
                                   start=True, stop=True)
                GB[c % 2].filled(mm)

            def gates_T(t, q, n):
                pe.wait_ge(gates_done, t + 1)
                FB.fill(pe, n)
                for c in range(NT):
                    mm = pe.matmul(FB.t[0:E, tile_of(core, c)], gates[q][:, c, :], core.ident[:], start=True, stop=True)
                FB.filled(mm)

            def moe_T(t, n):
                pe.wait_ge(moe_done, t + 1)
                FB.fill(pe, n)
                for c in range(NT):
                    o = FB.t[0:M, tile_of(core, c)]
                    pe.matmul(o, moe[:, c, :], core.ident[:], start=True, stop=False)
                    mm = pe.matmul(o, be2[:], gatesT[:, tile_of(core, c)], start=False, stop=True)
                FB.filled(mm)

            def spikes(n_moe, n):
                FB.after(pe, n_moe)
                for m in range(HC):
                    EB[m].fill(pe, n)
                    EB[m].filled(pe.matmul(EB[m].t[:], c2sW[:, tile_of(core, m)], moeT[:], start=True, stop=True))

            def decode(n_spikes, n):
                for m in range(HC):
                    EB[m].after(pe, n_spikes)
                TP.fill(pe, n)
                for c in range(NT):
                    o = TP.t[:, tile_of(core, c)]
                    pe.matmul(o, core.ones[0:1, :], decb[:], start=True, stop=False)
                    for m in range(HC):
                        mm = pe.matmul(o, dec_in[:, m, tile_of(core, c)], decW[:, m, :], start=False, stop=(m == HC - 1))
                TP.filled(mm)

            x_T(0)

            def body(t, p, i):
                expert_out(t, 0, 1 - p)
                encoder(t, p)
                expert_out(t, 1, 1 - p)
                cells(t)
                expert_out(t, 2, 1 - p)
                router(t)
                expert_out(t, 3, 1 - p)
                gates_T(t, 1 - p, gatesT_use(t))
                for e in range(E // 2):
                    expert_in(t, e)
                moe_T(t, moeT_use(t))
                expert_in(t, E // 2)
                spikes(moeT_use(t), c2s_use(t))
                for e in range(E // 2 + 1, E):
                    expert_in(t, e)
                logits(t)
                decode(c2s_use(t), dec_use(t))
                x_T(t + 1)

            in_pairs(pe, B, body)
            q = (B - 1) % 2
            for c in range(NT):
                expert_out(B, c, q)
            gates_T(B, q, cont_use(B))
            moe_T(B, router_use(B))
            spikes(router_use(B), enc_use(B))
            decode(enc_use(B), dec_use(B))

        @block.vector
        def _(v):
            tick = Tally(v, steps, per=12)

            def layer_norm(u):
                for c in range(NT):
                    op = v.tensor_scalar(xn[:, c], X[:, u, c], core.xmean[:, u, c:c + 1],
                                         core.xrstd[:, u, c:c + 1], ALU.subtract, ALU.mult)
                op.then_inc(xn_done, 1)

            def take_T(u, p):
                take_transposed(v.tensor_copy, v, TP, xT_use(u), xnT[p][:])

            def expert_hidden(t, e, p):
                HB[1].read(v, t * (E // 2) + (e // 2 + 1))
                HB[1].emptied(v.tensor_scalar(hid[p][:, e], HB[1].t[:], be1[:, e:e + 1], 0.0, ALU.add, ALU.max))

            def weigh_tile(t, c, q):
                if c == 0:
                    v.wait_ge(gates_done, t + 1)
                GB[c % 2].read(v, t * 2 + (c // 2 + 1))
                g = gates[q][:, c, :].unsqueeze(2).to_broadcast([P, E, M])
                GB[c % 2].emptied(v.tensor_tensor(weighted[:, c % 2], GB[c % 2].t[:].rearrange("p (e m) -> p e m", e=E),
                                                  g, ALU.mult))
                GB[c % 2].after(v, t * 2 + (c // 2 + 1))
                op = v.tensor_reduce(moe[:, c, :], weighted[:, c % 2].rearrange("p e m -> p m e"), AX.X, ALU.add)
                if c == NT - 1:
                    op.then_inc(moe_done, 1)

            def choose(t, p):
                tick.begin(t)
                wide = lambda a: a.unsqueeze(2).to_broadcast([P, NT, E])
                numbers = number[:].unsqueeze(1).to_broadcast([P, NT, E])
                FB.read(v, logits_use(t))
                FB.emptied(v.tensor_copy(logit[:].rearrange("p c e -> p (c e)"), FB.t[:, 0:NT * E]))
                FB.after(v, logits_use(t))
                for k in range(2):
                    tick.step(v.tensor_reduce(top[k][:], logit[:], AX.X, ALU.max))
                    tick.step(v.tensor_tensor(hit[:], logit[:], wide(top[k][:]), ALU.is_equal))
                    tick.step(v.scalar_tensor_tensor(cand[:], hit[:], -BIG, numbers, ALU.mult, ALU.add))
                    tick.step(v.tensor_reduce(first[:], cand[:], AX.X, ALU.min))
                    tick.step(v.tensor_tensor(mask[k][:], cand[:], wide(first[:]), ALU.is_equal))
                    if k == 0:
                        tick.step(v.scalar_tensor_tensor(logit[:], mask[0][:], -3e38, logit[:], ALU.mult, ALU.add))
                v.tensor_tensor(gap[:, 0], top[0][:], top[1][:], ALU.subtract)
                v.tensor_tensor(gap[:, 1], top[1][:], top[0][:], ALU.subtract).then_inc(gap_done, 1)

            def gate(t, p):
                wide = lambda a: a.unsqueeze(2).to_broadcast([P, NT, E])
                v.wait_ge(share_done, t + 1)
                v.tensor_tensor(hit[:], mask[0][:], wide(share[:, 0]), ALU.mult)
                tick.step(v.tensor_tensor(cand[:], mask[1][:], wide(share[:, 1]), ALU.mult))
                v.tensor_tensor(gates[p][:], hit[:], cand[:], ALU.add).then_inc(gates_done, 1)

            def take(n, rows, dst, bias=None):
                FB.read(v, n)
                if bias is None:
                    FB.emptied(v.tensor_copy(dst, FB.t[0:rows]))
                else:
                    FB.emptied(v.tensor_scalar(dst, FB.t[0:rows], bias, None, ALU.add))

            def statistics(b, n):
                TP.after(v, n)
                for c in range(NT):
                    v.bn_stats(core.yst[:, b + 1, c], Y[:, b + 1, c])

            v.sem_inc(gates_done, 1)
            v.wait_ge(*W.experts)
            v.wait_ge(init, E + 3)
            layer_norm(0)
            take_T(0, 0)

            def body(t, p, i):
                layer_norm(t + 1)
                weigh_tile(t, 0, 1 - p)
                weigh_tile(t, 1, 1 - p)
                take(cont_use(t), M, contT[:], s2cb[:])
                weigh_tile(t, 2, 1 - p)
                weigh_tile(t, 3, 1 - p)
                take(gatesT_use(t), E, gatesT[:])
                expert_hidden(t, 1, p)
                expert_hidden(t, 3, p)
                take(moeT_use(t), M, moeT[:])
                expert_hidden(t, 5, p)
                expert_hidden(t, 7, p)
                choose(t, p)
                statistics(t - 1, dec_use(t))
                take_T(t + 1, 1 - p)
                gate(t, p)

            in_pairs(v, B, body)
            q = (B - 1) % 2
            for c in range(NT):
                weigh_tile(B, c, q)
            take(cont_use(B), E, gatesT[:])
            take(router_use(B), M, moeT[:])
            statistics(B - 1, dec_use(B))


def program(nc, I, out):
    B, S, _ = I["L0_attn_x"].shape
    with ExitStack() as ctx:
        core = Core(nc, ctx, B, S // P)
        setup(core, I)
        attention(core, I)
        W = Weights(core, I)
        check_range(core, W)
        with nc.If(nc.values_load(core.in_range[0:1, 0:1], min_val=0, max_val=1) == 0):
            attention_guarded(core, I)
        add_normed(core, "r1")
        swiglu(core, I, W)
        add_normed(core, "r2", rms=True)
        state_space(core, I, W)
        mlp(core, I, W)
        add_normed(core, "r3")
        experts(core, I, W)
        add_normed(core, "r4", affine=(W.gain, W.bias, W.experts), store=out)


def kernel(**inputs):
    import numpy as np
    import concourse.bacc as bacc
    from concourse import mybir
    from concourse.bass_utils import run_bass_kernel_spmd as launch

    nc = bacc.Bacc("TRN2", target_bir_lowering=False, num_devices=1)
    arrays = {name: np.ascontiguousarray(a) for name, a in inputs.items()}
    B, S, width = arrays["L0_attn_x"].shape
    tiles = S // 128
    distance = np.arange(S + (tiles - 1) * 128)[None, :] - (tiles - 1) * 128 - np.arange(128)[:, None]
    arrays["decay"] = np.exp(-1e-4 * np.abs(distance)).astype(np.float32)
    I = {name: nc.dram_tensor(name, a.shape, mybir.dt.from_np(a.dtype), kind="ExternalInput").ap()
         for name, a in arrays.items()}
    out = nc.dram_tensor("out", (B, S, width), mybir.dt.float32, kind="ExternalOutput").ap()
    program(nc, I, out)
    r = launch(nc, [arrays], core_ids=[0])
    return r.results[0]["out"]
```

```python
import math
from contextlib import ExitStack

import concourse.bass as bass
from concourse import mybir

F32 = mybir.dt.float32
BF16 = mybir.dt.bfloat16
I32 = mybir.dt.int32
ALU = mybir.AluOpType
ACT = mybir.ActivationFunctionType
AX = mybir.AxisListType

P = 128
D = 128
HEADS, HD = 16, 8
LATENT = 32
SLOTS = 6
PARTS = 3
SPLIT = ((0, 0), (0, 1), (0, 2), (1, 0), (1, 1), (2, 0))
VC = 32
CEILING = 60.0
QSCALE = 1.0 / (float(D) ** 0.5 + 1e-8)


class Tally:

    def __init__(self, eng, sem, per=0, start=0):
        self.eng, self.sem, self.per, self.start, self.turn, self.n = eng, sem, per, start, 0, 0

    def begin(self, turn):
        assert self.n in (0, self.per), (self.n, self.per)
        self.turn, self.n = turn, 0

    def mark(self, ins):
        ins.then_inc(self.sem, 1)
        self.n += 1

    def settle(self):
        self.eng.wait_ge(self.sem, self.turn * self.per + (self.start + self.n))

    def step(self, ins):
        self.mark(ins)
        self.settle()


class Core:

    def __init__(self, nc, ctx, B, NT):
        self.nc, self.ctx, self.B, self.NT, self.T = nc, ctx, B, NT, NT * P
        sb = lambda n, s, d=F32: ctx.enter_context(nc.sbuf_tensor(n, s, d))
        XY = sb("XY", [P, 2 * B + 1, NT, D])
        self.X, self.Y = XY[:, 0:B + 1], XY[:, B:2 * B + 1]
        self.xmean = sb("xmean", [P, B + 1, NT])
        self.xrstd = sb("xrstd", [P, B + 1, NT])
        self.urstd = sb("urstd", [P, B + 1, NT])
        self.xst = sb("xst", [P, B, NT, 6])
        self.yst = sb("yst", [P, B + 1, NT, 6])
        self.fine = sb("fine", [P, NT, 4])
        self.in_range = sb("in_range", [P, 1], I32)
        self.ident = sb("ident", [P, P])
        self.ones = sb("ones", [P, P])
        self.Wq, self.Wkr, self.Wvr, self.Wo = (sb(n, [D, D]) for n in ("Wq", "Wkr", "Wvr", "Wo"))
        self.turns = self.sem("turns")

    def sem(self, name):
        return self.ctx.enter_context(self.nc.semaphore(name))


def moments(v, tick, st, mean, var, tmp):
    tick.mark(v.tensor_tensor(mean, st[..., 1], st[..., 4], ALU.add))
    tick.mark(v.tensor_tensor(var, st[..., 2], st[..., 5], ALU.add))
    tick.step(v.tensor_tensor(tmp, st[..., 1], st[..., 4], ALU.subtract))
    tick.step(v.tensor_tensor(tmp, tmp, tmp, ALU.mult))
    tick.mark(v.tensor_scalar(mean, mean, 0.5, None, ALU.mult))
    tick.step(v.tensor_scalar(tmp, tmp, 0.25, None, ALU.mult))
    tick.step(v.scalar_tensor_tensor(var, var, 1.0 / D, tmp, ALU.mult, ALU.add))


def pool_norm(core, pool, b, dst, scale, halfway, n, done):
    wide = lambda a: a[:, b].unsqueeze(2).to_broadcast([P, core.NT, D])
    pool.tensor_tensor(dst[:], core.X[:, b], wide(core.xmean), ALU.subtract).then_inc(halfway, 1)
    pool.wait_ge(halfway, n)
    pool.sem_inc(core.turns, 1)
    pool.tensor_tensor(dst[:], dst[:], wide(scale), ALU.mult).then_inc(done, 1)


def setup(core, I):
    nc, B, NT = core.nc, core.B, core.NT
    with ExitStack() as ctx:
        sb = lambda n, s, d=F32: ctx.enter_context(nc.sbuf_tensor(n, s, d))
        wk, wv, wks = sb("wk", [D, D]), sb("wv", [D, D]), sb("wks", [D, D])
        wsT = sb("wsT", [D, D])
        wd = sb("wd", [D, LATENT])
        wuk, wuv = sb("wuk", [LATENT, D]), sb("wuv", [LATENT, D])
        mT = sb("mT", [LATENT, D])
        wqr = sb("wqr", [D, D])
        tmp, var = sb("s_tmp", [P, B, NT]), sb("s_var", [P, B, NT])
        ps = ctx.enter_context(nc.psum_tensor("s_ps", [P, 4, 512], F32))
        xload, wload = core.sem("xload"), core.sem("wload")
        made, ident_done, tick_s = core.sem("setup_made"), core.sem("ident_done"), core.sem("setup_dve")
        on_pe, rooted = core.sem("setup_pe"), core.sem("setup_root")
        half = B // 2
        xv = I["L0_attn_x"].rearrange("b (c p) d -> p b c d", p=P)
        block = ctx.enter_context(nc.Block())

        @block.sync
        def _(sp):
            for n in range(2):
                for b in range(n * half, (n + 1) * half):
                    sp.dma_start(core.X[:, b], xv[:, b]).then_inc(xload, 16)
            sp.wait_ge(xload, 16 * B)

        @block.gpsimd
        def _(pool):
            pool.memset(core.ident[:], 0.0).then_inc(ident_done, 1)
            pool.memset(core.ones[:], 1.0).then_inc(ident_done, 1)
            pool.wait_ge(ident_done, 2)
            pool.affine_select(out=core.ident[:], in_=core.ident[:], compare_op=ALU.not_equal, fill=1.0,
                               base=0, pattern=[[-1, P]], channel_multiplier=1).then_inc(ident_done, 1)
            pool.memset(core.X[:, B], 0.0).then_inc(ident_done, 1)
            pool.memset(core.xmean[:, B], 0.0).then_inc(ident_done, 1)
            pool.memset(core.xrstd[:, B], 0.0).then_inc(ident_done, 1)
            pool.memset(core.urstd[:, B], 0.0).then_inc(ident_done, 1)

        @block.scalar
        def _(act):
            for dst, name in ((wk, "Wk"), (wv, "Wv"), (wd, "W_down_kv"), (wuk, "W_up_k"), (wuv, "W_up_v"),
                              (wqr, "Wq"), (core.Wo, "Wo")):
                act.dma_start(dst[:], I["L0_attn_" + name]).then_inc(wload, 16)
            act.wait_ge(tick_s, 2 + B * NT + 8)
            act.activation(core.xrstd[:, 0:B], core.xrstd[:, 0:B], ACT.Sqrt).then_inc(rooted, 1)

        @block.tensor
        def _(pe):
            pe.wait_ge(ident_done, 3)
            pe.wait_ge(tick_s, 2)
            pe.transpose(ps[:, 0, 0:D], wks[:], core.ident[:]).then_inc(on_pe, 1)
            pe.wait_ge(made, 1)
            pe.matmul(ps[0:LATENT, 1, 0:D], wd[:], wsT[:], start=True, stop=True).then_inc(on_pe, 1)
            pe.wait_ge(made, 2)
            pe.matmul(ps[:, 2, 0:D], mT[:], wuk[:], start=True, stop=True)
            pe.matmul(ps[:, 3, 0:D], mT[:], wuv[:], start=True, stop=True).then_inc(on_pe, 1)

        @block.vector
        def _(v):
            tick = Tally(v, tick_s)
            v.wait_ge(wload, 16 * 7)
            tick.mark(v.tensor_scalar(core.Wq[:], wqr[:], QSCALE, None, ALU.mult))
            tick.mark(v.tensor_tensor(wks[:], wk[:], wv[:], ALU.add))
            v.wait_ge(on_pe, 1)
            v.tensor_copy(wsT[:], ps[:, 0, 0:D]).then_inc(made, 1)
            v.wait_ge(on_pe, 2)
            v.tensor_copy(mT[:], ps[0:LATENT, 1, 0:D]).then_inc(made, 1)
            v.wait_ge(on_pe, 3)
            v.tensor_copy(core.Wkr[:], ps[:, 2, 0:D]).then_inc(made, 1)
            v.tensor_copy(core.Wvr[:], ps[:, 3, 0:D]).then_inc(made, 1)
            v.wait_ge(xload, 16 * B)
            for b in range(B):
                for c in range(NT):
                    tick.mark(v.bn_stats(core.xst[:, b, c], core.X[:, b, c]))
            tick.settle()
            moments(v, tick, core.xst[:], core.xmean[:, 0:B], var[:], tmp[:])
            tick.step(v.tensor_scalar(core.xrstd[:, 0:B], var[:], 1e-5, None, ALU.add))
            v.wait_ge(rooted, 1)
            tick.step(v.reciprocal(core.xrstd[:, 0:B], core.xrstd[:, 0:B]))


def attention(core, I):
    nc, B, NT, T = core.nc, core.B, core.NT, core.T
    HG = HEADS // 4
    STEPS = 2 * HG
    X, Y = core.X, core.Y
    with ExitStack() as ctx:
        sb = lambda n, s, d=F32: ctx.enter_context(nc.sbuf_tensor(n, s, d))
        psum = lambda n: ctx.enter_context(nc.psum_tensor(n, [P, 512], F32))
        decay = sb("a_decay", [P, T + (NT - 1) * P])
        Qs = [sb(f"Qs{p}", [SLOTS * HD, HEADS, T], BF16) for p in range(2)]
        Ks = [sb(f"Ks{p}", [SLOTS * HD, HEADS, T], BF16) for p in range(2)]
        V = [sb(f"V{p}", [P, NT, HEADS, VC]) for p in range(2)]
        probs = sb("probs", [P, 2, 4, 2, T])
        xnT = sb("a_xnT", [D, T])
        parts = [sb("qparts", [D, 3, T], BF16), sb("kparts", [D, 3, T], BF16)]
        heads_out = sb("heads_out", [P, NT, D])
        rest = sb("a_rest", [D, T])
        heads_outT = sb("heads_outT", [D, T])
        Osb = sb("Osb", [P, T])
        xn = sb("a_xn", [P, NT, D])
        one_over = sb("one_over", [P, NT, 4])
        S = [ctx.enter_context(nc.psum_tensor(f"S{i}", [P, 2, 512], F32)) for i in range(2)]
        O = [psum(f"O{i}") for i in range(2)]
        OT, M = psum("OT"), psum("M")
        dram = [nc.dram_tensor(f"{n}_parts", [D, 3, T], BF16, kind="Internal").ap() for n in "qk"]

        sem = lambda n: core.sem("a_" + n)
        const, init, xn_done = sem("const"), sem("init"), sem("xn_done")
        m_full, m_free = sem("m_full"), sem("m_free")
        first_part = [sem("q_first"), sem("k_first")]
        low = [sem("q_low"), sem("k_low")]
        stored, spread = [sem("q_stored"), sem("k_stored")], [sem("q_spread"), sem("k_spread")]
        s_full, decayed, exped, pv_done = sem("s_full"), sem("decayed"), sem("exped"), sem("pv_done")
        o_free, ot_full, inverted, heads_done = sem("o_free"), sem("ot_full"), sem("inverted"), sem("heads_done")
        second_part, centred = sem("second_part"), sem("centred")
        block = ctx.enter_context(nc.Block())

        FIRST = dict(xT=1, q=2, k=3, v=4)
        USES = dict(xT=1, q=2, k=3, headsT=4, rows=5, v=6)
        base_of = lambda t: t * 6 + 4

        def pairs(eng, body):
            with eng.Fori(0, B - 1, 2) as i:
                for p in range(2):
                    body(i + p, p)

        @block.sync
        def _(sp):
            sp.dma_start(decay[:], I["decay"]).then_inc(const, 16)

            def spread_parts(u, p, first=False):
                for w in range(2):
                    sp.wait_ge(low[w], u + 1)
                    sp.sem_inc(core.turns, 1)
                    if not first:
                        sp.wait_ge(spread[w], 16 * SLOTS * u)
                    sp.dma_start(dram[w], parts[w][:]).then_inc(stored[w], 16)
                    sp.wait_ge(stored[w], 16 * u + 16)
                    for s in range(SLOTS):
                        src = dram[w][:, SPLIT[s][w], :].rearrange("(h d) t -> d h t", d=HD)
                        sp.dma_start((Qs, Ks)[w][p][s * HD:(s + 1) * HD], src).then_inc(spread[w], 16)

            spread_parts(0, 0, first=True)
            pairs(sp, lambda t, p: spread_parts(t + 1, 1 - p))
            for w in range(2):
                sp.wait_ge(spread[w], 16 * SLOTS * (B + 1))

        @block.gpsimd
        def _(pool):
            layer_norm = lambda u: pool_norm(core, pool, u, xn, core.xrstd, centred, u + 1, xn_done)
            layer_norm(0)
            pool.memset(heads_out[:], 0.0).then_inc(init, 1)
            pool.memset(Osb[:], 1.0).then_inc(init, 1)
            for p in range(2):
                pool.memset(V[p][:, :, :, 0:HD], 0.0).then_inc(init, 1)
                pool.memset(V[p][:, :, :, HD:HD + 1], 1.0).then_inc(init, 1)
                pool.memset(V[p][:, :, :, HD + 1:VC], 0.0).then_inc(init, 1)
                pool.memset(probs[:, p], 1.0).then_inc(init, 1)

            def lower(u, base, use):
                for w, name in enumerate("qk"):
                    pool.wait_ge(m_free, base + use[name] + 1)
                    pool.sem_inc(core.turns, 1)
                    pool.tensor_copy(parts[w][:, 1], rest[:]).then_inc(second_part, 1)
                    pool.wait_ge(second_part, 2 * u + (w + 1))
                    pool.tensor_tensor(parts[w][:, 2], rest[:], parts[w][:, 1], ALU.subtract).then_inc(low[w], 1)

            def body(t, p):
                layer_norm(t + 1)
                lower(t + 1, base_of(t), USES)

            lower(0, 0, FIRST)
            pairs(pool, body)

        @block.scalar
        def _(act):
            def take(n, dst, src=M[:]):
                act.wait_ge(m_full, n)
                act.activation(dst, src, ACT.Copy).then_inc(m_free, 1)

            def take_first(n, w, u, first=False):
                act.wait_ge(m_full, n)
                if not first:
                    act.wait_ge(stored[w], 16 * u)
                act.activation(parts[w][:, 0], M[:], ACT.Copy).then_inc(first_part[w], 1)

            def take_values(n, p):
                take(n, V[p][:, :, :, 0:HD], M[:].rearrange("p (c h d) -> p c h d", c=NT, d=HD))

            def take_rows(b, n):
                take(n, Y[:, b + 1].rearrange("p c d -> p (c d)"))

            def evacuate(y, par):
                act.wait_ge(pv_done, y * 2 + 4)
                act.activation(Osb[:], O[par][:], ACT.Copy).then_inc(o_free, 1)

            act.preload_act_table(ACT.Exp)
            act.sem_inc(exped, 4)
            act.sem_inc(o_free, 1)
            take(1, xnT[:])
            take_first(2, 0, 0, first=True)
            take_first(3, 1, 0, first=True)
            act.wait_ge(init, 10)
            take_values(4, 0)

            def body(t, p):
                base = base_of(t)
                for g in range(STEPS):
                    for j in range(4):
                        act.wait_ge(decayed, t * (4 * STEPS) + (4 * g + j + 3))
                        pr = probs[:, g % 2, j]
                        act.activation(pr, pr, ACT.Exp).then_inc(exped, 1)
                        if j == 0 and g % 2:
                            evacuate(t * HG + (g // 2 - 1), (g // 2 - 1) % 2)
                        if j == 1:
                            if g == 1:
                                take(base + USES["xT"], xnT[:])
                            if g == 2:
                                take_first(base + USES["q"], 0, t + 1)
                            if g == 3:
                                take_first(base + USES["k"], 1, t + 1)
                            if g == 4:
                                take(base + USES["headsT"], heads_outT[:])
                            if g == 5:
                                take_rows(t - 1, base + USES["rows"])
                            if g == 6:
                                take_values(base + USES["v"], 1 - p)

            pairs(act, body)
            evacuate(HG * B - 1, (HG - 1) % 2)
            take(base_of(B) + 1, heads_outT[:])
            take_rows(B - 1, base_of(B) + 2)

        @block.tensor
        def _(pe):
            def scores(g, j, p):
                for kk in range(2):
                    kb, h = 2 * (g % 2) + kk, 4 * (g // 2) + j
                    mm = pe.matmul(S[j % 2][:, kk, :], Ks[p][:, h, kb * P:(kb + 1) * P], Qs[p][:, h, :],
                                   start=True, stop=True)
                mm.then_inc(s_full, 1)

            def values(g, half, p):
                kb = 2 * (g % 2) + half
                for j in range(4):
                    mm = pe.matmul(O[g // 2 % 2][VC * j:VC * (j + 1), :], V[p][:, kb, 4 * (g // 2) + j, :],
                                   probs[:, g % 2, j, half, :], start=(kb == 0), stop=(kb == NT - 1),
                                   skip_group_check=True)
                return mm

            def use_M(n, emit):
                pe.wait_ge(m_free, n)
                emit().then_inc(m_full, 1)

            def tiles_T(src):
                for c in range(NT):
                    mm = pe.transpose(M[:, c * P:(c + 1) * P], src[:, c, :], core.ident[:])
                return mm

            def rows(lhsT, w):
                for c in range(NT):
                    mm = pe.matmul(M[:, c * P:(c + 1) * P], lhsT[:, c * P:(c + 1) * P], w[:],
                                   start=True, stop=True)
                return mm

            def x_T(u, n):
                pe.wait_ge(xn_done, u + 1)
                use_M(n, lambda: tiles_T(xn))

            def project(w, n):
                use_M(n, lambda: pe.matmul(M[:], w[:], xnT[:], start=True, stop=True))

            def out_T(y):
                pe.wait_ge(o_free, y + 3)
                pe.wait_ge(heads_done, y + 3)
                for c in range(NT):
                    mm = pe.transpose(OT[:, c * P:(c + 1) * P], Osb[:, c * P:(c + 1) * P], core.ident[:])
                mm.then_inc(ot_full, 1)

            def heads_T(b, n):
                pe.wait_ge(heads_done, b * HG + (HG + 3))
                use_M(n, lambda: tiles_T(heads_out))

            pe.sem_inc(m_free, 1)
            pe.sem_inc(pv_done, 1)
            x_T(0, 1)
            project(core.Wq, 2)
            project(core.Wkr, 3)
            use_M(4, lambda: rows(xnT, core.Wvr))
            pe.wait_ge(m_free, 5)
            pe.wait_ge(init, 10)
            for half in range(2):
                values(STEPS - 2, half, 1)

            def body(t, p):
                base = base_of(t)
                for g in range(STEPS):
                    G = t * STEPS + g
                    for j in range(4):
                        if g == 0 and j == 0:
                            for w in range(2):
                                pe.wait_ge(spread[w], t * (16 * SLOTS) + 16 * SLOTS)
                        pe.wait_ge(decayed, t * (4 * STEPS) + (4 * g + j + 1))
                        scores(g, j, p)
                        if j == 0 and g % 2 == 0:
                            out_T(t * HG + (g // 2 - 2))
                        if j == 1:
                            if g == 1:
                                x_T(t + 1, base + USES["xT"])
                            if g == 2:
                                project(core.Wq, base + USES["q"])
                            if g == 3:
                                project(core.Wkr, base + USES["k"])
                            if g == 4:
                                heads_T(t - 1, base + USES["headsT"])
                            if g == 5:
                                use_M(base + USES["rows"], lambda: rows(heads_outT, core.Wo))
                            if g == 6:
                                use_M(base + USES["v"], lambda: rows(xnT, core.Wvr))
                        if j == 2:
                            pe.wait_ge(exped, G * 4 + 4)
                            if g % 2:
                                pe.wait_ge(o_free, t * HG + (g // 2 + 1))
                            values((g - 1) % STEPS, 0, p if g else 1 - p)
                        if j == 3:
                            values((g - 1) % STEPS, 1, p if g else 1 - p).then_inc(pv_done, 1)

            pairs(pe, body)
            out_T(HG * B - 2)
            pe.wait_ge(exped, 4 * STEPS * B + 4)
            for half in range(2):
                mm = values(STEPS - 1, half, (B - 1) % 2)
            mm.then_inc(pv_done, 1)
            out_T(HG * B - 1)
            heads_T(B - 1, base_of(B) + 1)
            use_M(base_of(B) + 2, lambda: rows(heads_outT, core.Wo))

        @block.vector
        def _(v):
            v.sem_inc(decayed, 2)
            v.sem_inc(heads_done, 1)

            def take_rest(w, u, first=False):
                v.wait_ge(first_part[w], u + 1)
                if w == 1:
                    v.wait_ge(low[0], u + 1)
                elif not first:
                    v.wait_ge(low[1], u)
                v.tensor_tensor(rest[:], M[:], parts[w][:, 0], ALU.subtract).then_inc(m_free, 1)

            ot = OT[:].rearrange("p (c j e) -> p c j e", c=NT, j=4)

            def take_sums(y):
                v.wait_ge(ot_full, y + 3)
                v.wait_ge(inverted, y * 4 + 9)
                v.tensor_scalar(one_over[:], ot[:, :, :, HD], 1e-30, None, ALU.max).then_inc(inverted, 1)

            def invert(y):
                v.wait_ge(inverted, y * 4 + 10)
                v.reciprocal(one_over[:], one_over[:]).then_inc(inverted, 1)

            def normalise(y, hg, heads_read=None):
                v.wait_ge(inverted, y * 4 + 11)
                if heads_read is not None:
                    v.wait_ge(m_full, heads_read)
                dst = heads_out[:, :, hg * 4 * HD:(hg + 1) * 4 * HD].rearrange("p c (j d) -> p c j d", d=HD)
                v.tensor_tensor(dst, ot[:, :, :, 0:HD], one_over[:].unsqueeze(3).to_broadcast([P, NT, 4, HD]),
                                ALU.mult).then_inc(heads_done, 1)
                v.scalar_tensor_tensor(core.fine[:], one_over[:], 2.0 ** -60, core.fine[:], ALU.is_ge, ALU.mult)\
                    .then_inc(inverted, 1)

            def check(y):
                v.wait_ge(inverted, y * 4 + 12)
                v.scalar_tensor_tensor(core.fine[:], one_over[:], 2.0 ** 60, core.fine[:], ALU.is_le, ALU.mult)\
                    .then_inc(inverted, 1)

            def statistics(b, n):
                v.wait_ge(m_free, n + 1)
                for c in range(NT):
                    op = v.bn_stats(core.yst[:, b + 1, c], Y[:, b + 1, c])
                return op

            take_rest(0, 0, first=True)
            take_rest(1, 0, first=True)
            v.memset(core.fine[:], 1.0).then_inc(inverted, 1)
            v.wait_ge(init, 10)
            v.wait_ge(const, 16)
            full = decay[:]
            decay_of = [bass.AP(full.tensor, full.offset + (NT - 1 - 2 * m) * P, [list(full.ap[0]), [-P, 2], [1, T]])
                        for m in range(2)]

            def body(t, p):
                base = base_of(t)
                for g in range(STEPS):
                    for j in range(4):
                        if j == 0:
                            v.wait_ge(pv_done, t * STEPS + (g + 1))
                        v.wait_ge(s_full, t * (4 * STEPS) + (4 * g + j + 1))
                        v.scalar_tensor_tensor(probs[:, g % 2, j], S[j % 2][:], CEILING, decay_of[g % 2], ALU.min,
                                               ALU.mult).then_inc(decayed, 1)
                        y, hg = t * HG + (g // 2 - 2), (g // 2 - 2) % HG
                        if g % 2 == 0:
                            if j == 1:
                                take_sums(y)
                            if j == 2:
                                invert(y)
                            if j == 3:
                                normalise(y, hg, base + USES["headsT"] if hg == 0 else None)
                        if g % 2 and j == 0:
                            check(y)
                        if j == 3:
                            if g == 2:
                                take_rest(0, t + 1)
                            if g == 3:
                                take_rest(1, t + 1)
                            if g == 5:
                                statistics(t - 1, base + USES["rows"])

            pairs(v, body)
            for y, hg in ((HG * B - 2, HG - 2), (HG * B - 1, HG - 1)):
                take_sums(y)
                invert(y)
                normalise(y, hg)
                check(y)
            statistics(B - 1, base_of(B) + 2).then_inc(inverted, 1)
            v.wait_ge(inverted, HG * B * 4 + 10)


class Weights:

    def __init__(self, core, I):
        nc = core.nc
        sb = lambda n, s, d=F32: core.ctx.enter_context(nc.sbuf_tensor("w_" + n, s, d))
        self.loads = []
        F = I["L0_ffn_w_gate"].shape[0]
        self.ints = [sb(f"int{k}", [P, F], I32) for k in range(3)]
        by_block = lambda a: a.rearrange("(m p) d -> p m d", p=P)
        self.swiglu = self.layer(core, "swiglu", [
            *((self.ints[k][:].rearrange("p (m d) -> p m d", d=P), by_block(I["L0_ffn_" + n]))
              for k, n in enumerate(("w_gate", "w_up"))),
            (self.ints[2][:], I["L0_ffn_w_down"])])
        N = I["L1_attn_A_ssm"].shape[1]
        self.A, self.B, self.C = (sb(n, [D, N]) for n in "ABC")
        self.D, self.scale1 = sb("D", [D, 1]), sb("scale1", [D, 1])
        column = lambda a: a.unsqueeze(1)
        row = lambda a: a.unsqueeze(0)
        self.state_space = self.layer(core, "state_space", [
            (self.A[:], I["L1_attn_A_ssm"]), (self.B[:], I["L1_attn_B_ssm"]), (self.C[:], I["L1_attn_C_ssm"]),
            (self.D[:], column(I["L1_attn_D_ssm"])), (self.scale1[:], column(I["L1_attn_scale1"]))])
        F = I["L1_attn_w1"].shape[1]
        self.w1, self.w2, self.b1 = sb("w1", [D, F]), sb("w2", [P, F // P, D]), sb("b1", [P, F // P])
        self.b2, self.scale2 = sb("b2", [1, D]), sb("scale2", [D, 1])
        folded = lambda a: a.rearrange("(m p) -> p m", p=P)
        self.mlp = self.layer(core, "mlp", [
            (self.w1[:], I["L1_attn_w1"]), (self.w2[:], by_block(I["L1_attn_w2"])), (self.b1[:], folded(I["L1_attn_b1"])),
            (self.b2[:], row(I["L1_attn_b2"])), (self.scale2[:], column(I["L1_attn_scale2"]))])
        H = I["L1_ffn_enc_W"].shape[1]
        E, M, HH = I["L1_ffn_We1"].shape
        HC = H // P
        self.encW, self.encb = sb("encW", [D, H]), sb("encb", [P, HC])
        self.s2cW, self.s2cb = sb("s2cW", [P, HC, M]), sb("s2cb", [2 * M, 1])
        self.rW1, self.rb1, self.rW2 = sb("rW1", [2 * M, 64]), sb("rb1", [64, 1]), sb("rW2", [65, E])
        self.We1, self.be1 = sb("We1", [2 * M, E, HH]), sb("be1", [HH, E])
        self.We2, self.be2 = sb("We2", [HH, E, M]), sb("be2", [PARTS * E, M])
        self.c2sW, self.c2sb = sb("c2sW", [2 * M, H]), sb("c2sb", [P, HC])
        halves = [slice(k * M, (k + 1) * M) for k in range(2)]
        self.decW, self.decb = sb("decW", [P, HC, D]), sb("decb", [1, D])
        self.G = PARTS * E
        self.number = sb("number", [P, E])
        self.select, self.select32 = sb("select", [self.G, E, P], BF16), sb("select32", [self.G, E, P])
        self.ident16 = sb("ident16", [P, P], BF16)
        self.constants = core.sem("constants")
        self.gain, self.bias = sb("gain", [P, D]), sb("bias", [P, D])
        X = lambda n: I["L1_ffn_" + n]
        self.experts = self.layer(core, "experts", [
            (self.encW[:], X("enc_W")), (self.encb[:], folded(X("enc_b"))), (self.s2cW[:], by_block(X("s2c_W"))),
            (self.s2cb[0:M], column(X("s2c_b"))), *((self.rW1[h], X("rW1")) for h in halves),
            (self.rb1[:], column(X("rb1"))),
            (self.rW2[0:64], X("rW2")), (self.rW2[64:65], row(X("rb2"))),
            *((self.We1[h], X("We1").rearrange("e m h -> m e h")) for h in halves), (self.be1[:], X("be1").rearrange("e h -> h e")),
            (self.We2[:], X("We2").rearrange("e h m -> h e m")), 
            *((self.be2[k * E:(k + 1) * E], X("be2")) for k in range(PARTS)),
            *((self.c2sW[h], X("c2s_W")) for h in halves), (self.c2sb[:], folded(X("c2s_b"))),
            (self.decW[:], by_block(X("dec_W"))), (self.decb[:], row(X("dec_b"))),
            (self.gain[:], X("ln_g").partition_broadcast(P)), (self.bias[:], X("ln_b").partition_broadcast(P))])

    def layer(self, core, name, loads):
        sem = core.sem(name + "_loaded")
        self.loads.append([(dst, src, sem) for dst, src in loads])
        return sem, 16 * len(loads)

    def make_constants(self, core, pool):
        made = Tally(pool, self.constants)
        E = self.number.shape[1]
        for k in range(E):
            made.mark(pool.memset(self.number[:, k:k + 1], float(k)))
        made.step(pool.memset(self.select32[:], 0.0))
        for k in range(PARTS):
            made.step(pool.affine_select(out=self.select32[:], in_=self.select32[:], compare_op=ALU.not_equal,
                                         fill=1.0, base=-k * E, pattern=[[-1, E], [0, P]], channel_multiplier=1))
        made.step(pool.tensor_copy(self.select[:], self.select32[:]))
        made.step(pool.tensor_copy(self.ident16[:], core.ident[:]))
        made.step(pool.memset(self.s2cb[self.s2cb.shape[0] // 2:], 0.0))
        self.made = made.n

    def load(self, nc, eng, n):
        with nc.allow_non_contiguous_dma("biases with their features on partitions"):
            for dst, src, loaded in self.loads[n]:
                eng.dma_start(dst, src).then_inc(loaded, 16)


def check_range(core, W):
    nc = core.nc
    with ExitStack() as ctx:
        least, fine = (ctx.enter_context(nc.sbuf_tensor(n, [P, 1], F32)) for n in ("r_least", "r_fine"))
        count = ctx.enter_context(nc.psum_tensor("r_count", [P, 1], F32))
        steps, least_done, counted = core.sem("r_steps"), core.sem("r_least_done"), core.sem("r_counted")
        known = core.sem("r_known")
        block = ctx.enter_context(nc.Block())

        @block.sync
        def _(sp):
            W.load(nc, sp, 0)
            sp.wait_ge(known, 1)

        @block.gpsimd
        def _(pool):
            pool.wait_ge(known, 1)

        @block.scalar
        def _(act):
            act.wait_ge(known, 1)

        @block.tensor
        def _(pe):
            pe.wait_ge(least_done, 1)
            pe.matmul(count[:], core.ones[:], least[:], start=True, stop=True).then_inc(counted, 1)
            pe.wait_ge(known, 1)

        @block.vector
        def _(v):
            tick = Tally(v, steps)
            v.tensor_reduce(least[:], core.fine[:].rearrange("p c j -> p (c j)"), AX.X, ALU.min).then_inc(least_done, 1)
            v.wait_ge(counted, 1)
            tick.step(v.tensor_scalar(fine[:], count[:], float(P), None, ALU.is_equal))
            v.tensor_copy(core.in_range[:], fine[:]).then_inc(known, 1)
            v.wait_ge(known, 1)


def attention_guarded(core, I):
    nc, B, NT, T = core.nc, core.B, core.NT, core.T
    X, Y = core.X, core.Y
    with ExitStack() as ctx:
        sb = lambda n, s, d=F32: ctx.enter_context(nc.sbuf_tensor("c_" + n, s, d))
        psum = lambda n, s: ctx.enter_context(nc.psum_tensor("c_" + n, s, F32))
        decay = sb("decay", [P, T + (NT - 1) * P])
        xn, xnT = sb("xn", [P, NT, D]), sb("xnT", [D, T])
        qT, kT = sb("qT", [D, T]), sb("kT", [D, T])
        q8, k8 = sb("q8", [HD, HEADS, T]), sb("k8", [HD, HEADS, T])
        qh, kh = sb("qh", [HD, T]), sb("kh", [HD, T])
        V = sb("V", [P, NT, D])
        probs, probsT = sb("probs", [P, T]), sb("probsT", [P, NT, P])
        top, total = sb("top", [P, 1]), sb("total", [P, 1])
        heads_out, heads_outT = sb("heads_out", [P, NT, D]), sb("heads_outT", [D, T])
        M, O = psum("M", [P, 512]), psum("O", [P, HD])
        dram = [nc.dram_tensor(f"c_{n}", [D, T], F32, kind="Internal").ap() for n in "qk"]
        const, moved, relay = core.sem("c_const"), core.sem("c_moved"), core.sem("c_relay")
        before = ["xn", "xT", "take_xT", "q", "take_q", "k", "take_k", "v", "take_v", "spread"]
        tile = ["scores", "clip", "decay", "top", "negate", "exp", "total", "invert", "weigh",
                "probsT", "take_probsT", "out", "take_out"]
        head = ["pick"] + [f"{s}{c}" for c in range(NT) for s in tile]
        after = ["headsT", "take_headsT", "rows", "take_rows"]
        BATCH = len(before) + HEADS * len(head) + len(after)
        block = ctx.enter_context(nc.Block())

        def turn(t, name, h=None):
            if name in before:
                return t * BATCH + (before.index(name) + 1)
            if name in after:
                return t * BATCH + (len(before) + HEADS * len(head) + after.index(name) + 1)
            return t * BATCH + h * len(head) + (len(before) + head.index(name) + 1)

        @block.sync
        def _(sp):
            sp.dma_start(decay[:], I["decay"]).then_inc(const, 16)
            sp.wait_ge(const, 16)
            with sp.Fori(0, B) as t:
                sp.wait_ge(relay, turn(t, "spread"))
                sp.dma_start(dram[0], qT[:]).then_inc(moved, 16)
                sp.dma_start(dram[1], kT[:]).then_inc(moved, 16)
                sp.wait_ge(moved, t * 64 + 32)
                for src, dst in zip(dram, (q8, k8)):
                    sp.dma_start(dst[:], src.rearrange("(h d) t -> d h t", d=HD)).then_inc(moved, 16)
                sp.wait_ge(moved, t * 64 + 64)
                sp.sem_inc(relay, 1)

        @block.gpsimd
        def _(pool):
            pool.wait_ge(const, 16)

        @block.scalar
        def _(act):
            act.preload_act_table(ACT.Exp)
            with act.Fori(0, B) as t:
                with act.Fori(0, HEADS) as h:
                    for c in range(NT):
                        act.wait_ge(relay, turn(t, f"exp{c}", h))
                        act.activation(probs[:], probs[:], ACT.Exp, bias=top[:]).then_inc(relay, 1)

        @block.tensor
        def _(pe):
            def tiles_T(src):
                for c in range(NT):
                    mm = pe.transpose(M[:, tile_of(core, c)], src[:, c, :], core.ident[:])
                mm.then_inc(relay, 1)

            def rows(lhsT, w):
                for c in range(NT):
                    mm = pe.matmul(M[:, tile_of(core, c)], lhsT[:, tile_of(core, c)], w[:], start=True, stop=True)
                mm.then_inc(relay, 1)

            with pe.Fori(0, B) as t:
                pe.wait_ge(relay, turn(t, "xT"))
                tiles_T(xn)
                pe.wait_ge(relay, turn(t, "q"))
                pe.matmul(M[:], core.Wq[:], xnT[:], start=True, stop=True).then_inc(relay, 1)
                pe.wait_ge(relay, turn(t, "k"))
                pe.matmul(M[:], core.Wkr[:], xnT[:], start=True, stop=True).then_inc(relay, 1)
                pe.wait_ge(relay, turn(t, "v"))
                rows(xnT, core.Wvr)
                with pe.Fori(0, HEADS) as h:
                    for c in range(NT):
                        pe.wait_ge(relay, turn(t, f"scores{c}", h))
                        pe.matmul(M[:], qh[:, tile_of(core, c)], kh[:], start=True, stop=True).then_inc(relay, 1)
                        pe.wait_ge(relay, turn(t, f"probsT{c}", h))
                        for k in range(NT):
                            mm = pe.transpose(M[:, tile_of(core, k)], probs[:, tile_of(core, k)], core.ident[:])
                        mm.then_inc(relay, 1)
                        pe.wait_ge(relay, turn(t, f"out{c}", h))
                        for k in range(NT):
                            mm = pe.matmul(O[:], probsT[:, k, :], V[:, k, bass.ds(h * HD, HD)], start=(k == 0),
                                           stop=(k == NT - 1))
                        mm.then_inc(relay, 1)
                pe.wait_ge(relay, turn(t, "headsT"))
                tiles_T(heads_out)
                pe.wait_ge(relay, turn(t, "rows"))
                rows(heads_outT, core.Wo)

        @block.vector
        def _(v):
            v.sem_inc(relay, 1)
            v.wait_ge(const, 16)

            def take(t, name, dst):
                v.wait_ge(relay, turn(t, name))
                v.tensor_copy(dst, M[:]).then_inc(relay, 1)

            with v.Fori(0, B) as t:
                v.wait_ge(relay, turn(t, "xn"))
                for c in range(NT):
                    op = v.tensor_scalar(xn[:, c], X[:, t, c], core.xmean[:, t, c:c + 1],
                                         core.xrstd[:, t, c:c + 1], ALU.subtract, ALU.mult)
                op.then_inc(relay, 1)
                take(t, "take_xT", xnT[:])
                take(t, "take_q", qT[:])
                take(t, "take_k", kT[:])
                take(t, "take_v", V[:].rearrange("p c d -> p (c d)"))
                with v.Fori(0, HEADS) as h:
                    v.wait_ge(relay, turn(t, "pick", h))
                    v.tensor_copy(qh[:], q8[:, h, :])
                    v.tensor_copy(kh[:], k8[:, h, :]).then_inc(relay, 1)
                    for c in range(NT):
                        v.wait_ge(relay, turn(t, f"clip{c}", h))
                        v.tensor_scalar(probs[:], M[:], -1e4, 1e4, ALU.max, ALU.min).then_inc(relay, 1)
                        v.wait_ge(relay, turn(t, f"decay{c}", h))
                        v.tensor_tensor(probs[:], probs[:], decay[:, (NT - 1 - c) * P:(NT - 1 - c) * P + T],
                                        ALU.mult).then_inc(relay, 1)
                        v.wait_ge(relay, turn(t, f"top{c}", h))
                        v.tensor_reduce(top[:], probs[:], AX.X, ALU.max).then_inc(relay, 1)
                        v.wait_ge(relay, turn(t, f"negate{c}", h))
                        v.tensor_scalar(top[:], top[:], -1.0, None, ALU.mult).then_inc(relay, 1)
                        v.wait_ge(relay, turn(t, f"total{c}", h))
                        v.tensor_reduce(total[:], probs[:], AX.X, ALU.add).then_inc(relay, 1)
                        v.wait_ge(relay, turn(t, f"invert{c}", h))
                        v.reciprocal(total[:], total[:]).then_inc(relay, 1)
                        v.wait_ge(relay, turn(t, f"weigh{c}", h))
                        v.tensor_scalar(probs[:], probs[:], total[:], None, ALU.mult).then_inc(relay, 1)
                        v.wait_ge(relay, turn(t, f"take_probsT{c}", h))
                        v.tensor_copy(probsT[:].rearrange("p k q -> p (k q)"), M[:]).then_inc(relay, 1)
                        v.wait_ge(relay, turn(t, f"take_out{c}", h))
                        v.tensor_copy(heads_out[:, c, bass.ds(h * HD, HD)], O[:]).then_inc(relay, 1)
                take(t, "take_headsT", heads_outT[:])
                v.wait_ge(relay, turn(t, "take_rows"))
                v.tensor_copy(Y[:, t + 1].rearrange("p c d -> p (c d)"), M[:])
                for c in range(NT):
                    op = v.bn_stats(core.yst[:, t + 1, c], M[:, tile_of(core, c)])
                op.then_inc(relay, 1)


class Bank:

    def __init__(self, core, ctx, name, shape=None):
        self.t = ctx.enter_context(core.nc.psum_tensor(name, shape or [P, 512], F32))
        self.full, self.free = core.sem(name + "_full"), core.sem(name + "_free")

    def open(self, pe):
        pe.sem_inc(self.free, 1)

    def fill(self, pe, n):
        pe.wait_ge(self.free, n)

    def filled(self, ins):
        ins.then_inc(self.full, 1)

    def read(self, eng, n):
        eng.wait_ge(self.full, n)

    def emptied(self, ins):
        ins.then_inc(self.free, 1)

    def after(self, eng, n):
        eng.wait_ge(self.free, n + 1)


def in_pairs(eng, B, body):
    with eng.Fori(0, B // 2) as i:
        for p in range(2):
            body(i * 2 + p, p, i)


def transposed(core, pe, bank, n, src):
    bank.fill(pe, n)
    for c in range(core.NT):
        mm = pe.transpose(bank.t[:, c * P:(c + 1) * P], src[:, c, :], core.ident[:])
    bank.filled(mm)


def tile_of(core, c):
    return slice(c * P, (c + 1) * P)


def by_batch(eng, count, body):
    step = max(k for k in range(1, 6) if count % k == 0)
    with eng.Fori(0, count // step) as i:
        for k in range(step):
            body(i * step + k)


def add_normed(core, name, rms=False, affine=None, store=None):
    nc, B, NT = core.nc, core.B, core.NT
    X, Y = core.X, core.Y
    with ExitStack() as ctx:
        sb = lambda n, s, d=F32: ctx.enter_context(nc.sbuf_tensor(f"{name}_{n}", s, d))
        mean, var, tmp, rstd, shift = (sb(n, [P, B, NT]) for n in ("mean", "var", "tmp", "rstd", "shift"))
        sem = lambda n: core.sem(f"{name}_{n}")
        steps, rooted, want_root, shift_done = sem("steps"), sem("rooted"), sem("want_root"), sem("shift_done")
        act_normed, dve_normed, added = sem("act_normed"), sem("dve_normed"), sem("added")
        counted = sem("counted")
        if affine:
            gain, bias, (loaded, NLOAD) = affine
            scaled, shifted = sem("scaled"), sem("shifted")
        if store is not None:
            out = store.rearrange("b (c p) d -> p b c d", p=P)
            stored = sem("stored")
        rounds = 2 if affine else 1
        roots = rounds + (0 if store is not None else 2 if rms else 1)
        act_tiles = [NT, NT // 2] if affine else [NT - 1]
        block = ctx.enter_context(nc.Block())

        if store is not None:
            @block.sync
            def _(sp):
                def leave(t):
                    sp.wait_ge(added, t + 1)
                    sp.sem_inc(core.turns, 1)
                    sp.dma_start(out[:, t], X[:, t]).then_inc(stored, 16)

                by_batch(sp, B, leave)
                sp.wait_ge(stored, 16 * B)

        @block.gpsimd
        def _(pool):
            def add(t):
                if affine:
                    pool.wait_ge(scaled, t + 1)
                    pool.sem_inc(core.turns, 1)
                    pool.tensor_tensor(Y[:, t + 1], Y[:, t + 1], bias[:].unsqueeze(1).to_broadcast([P, NT, D]),
                                       ALU.add).then_inc(shifted, 1)
                else:
                    pool.wait_ge(act_normed, t + 1)
                    pool.sem_inc(core.turns, 1)
                    pool.wait_ge(dve_normed, t + 1)
                    pool.sem_inc(core.turns, 1)
                    pool.tensor_tensor(X[:, t], X[:, t], Y[:, t + 1], ALU.add).then_inc(added, 1)

            by_batch(pool, B, add)

        @block.scalar
        def _(act):
            def root(n):
                act.wait_ge(want_root, n)
                act.activation(tmp[:], tmp[:], ACT.Sqrt).then_inc(rooted, 1)

            for k in range(rounds):
                root(k + 1)
                act.wait_ge(shift_done, k + 1)

                def normalise(t):
                    for c in range(act_tiles[k]):
                        y = Y[:, t + 1, c]
                        op = act.activation(y, y, ACT.Identity, bias=shift[:, t, c:c + 1], scale=rstd[:, t, c:c + 1])
                    op.then_inc(act_normed, 1)

                by_batch(act, B, normalise)
            for k in range(rounds, roots):
                root(k + 1)

        @block.vector
        def _(v):
            tick = Tally(v, steps)

            def inverse_root(n, dst, eps):
                v.tensor_scalar(tmp[:], var[:], eps, None, ALU.add).then_inc(want_root, 1)
                v.wait_ge(rooted, n)
                tick.step(v.reciprocal(dst, tmp[:]))

            def normalise(t, k):
                for c in range(act_tiles[k], NT):
                    y = Y[:, t + 1, c]
                    op = v.tensor_scalar(y, y, rstd[:, t, c:c + 1], shift[:, t, c:c + 1], ALU.mult, ALU.add)
                op.then_inc(dve_normed, 1)

            def statistics(st, src):
                for c in range(NT):
                    op = v.bn_stats(st[:, c], src[:, c])
                op.then_inc(counted, 1)

            for k in range(rounds):
                moments(v, tick, core.yst[:, 1:B + 1], mean[:], var[:], tmp[:])
                inverse_root(k + 1, rstd[:], 1e-5)
                tick.mark(v.scalar_tensor_tensor(shift[:], mean[:], -1.0, rstd[:], ALU.mult, ALU.mult))
                tick.settle()
                v.sem_inc(shift_done, 1)
                if k < rounds - 1:
                    v.wait_ge(loaded, NLOAD)

                    def scale(t):
                        v.wait_ge(act_normed, t + 1)
                        v.tensor_tensor(Y[:, t + 1], Y[:, t + 1], gain[:].unsqueeze(1).to_broadcast([P, NT, D]),
                                        ALU.mult).then_inc(scaled, 1)

                    def body(t):
                        scale(t + 1)
                        v.wait_ge(shifted, t + 1)
                        statistics(core.yst[:, t + 1], Y[:, t + 1])

                    scale(0)
                    by_batch(v, B - 1, body)
                    v.wait_ge(shifted, B)
                    statistics(core.yst[:, B], Y[:, B])
                    v.wait_ge(counted, B)
            last = rounds - 1
            if store is not None:
                def body(t):
                    normalise(t, last)
                    v.wait_ge(act_normed, t + (B * last + 1))
                    v.wait_ge(dve_normed, t + 1)
                    v.tensor_tensor(X[:, t], X[:, t], Y[:, t + 1], ALU.add).then_inc(added, 1)

                by_batch(v, B, body)
            else:
                def body(t):
                    normalise(t + 1, last)
                    v.wait_ge(added, t + 1)
                    statistics(core.xst[:, t], X[:, t])

                normalise(0, last)
                by_batch(v, B - 1, body)
                v.wait_ge(added, B)
                statistics(core.xst[:, B - 1], X[:, B - 1])
                v.wait_ge(counted, B)
                moments(v, tick, core.xst[:], core.xmean[:, 0:B], var[:], tmp[:])
                inverse_root(rounds + 1, core.xrstd[:, 0:B], 1e-5)
                if rms:
                    r = core.xrstd[:, 0:B]
                    tick.step(v.tensor_tensor(var[:], var[:], r, ALU.mult))
                    tick.step(v.tensor_tensor(var[:], var[:], r, ALU.mult))
                    inverse_root(rounds + 2, tmp[:], 1e-6)
                    tick.step(v.tensor_tensor(core.urstd[:, 0:B], tmp[:], r, ALU.mult))


def take_transposed(eng_copy, eng, bank, n, dst):
    bank.read(eng, n)
    bank.emptied(eng_copy(dst, bank.t[:, 0:dst.shape[-1]]))


def swiglu(core, I, W):
    nc, B, NT, T = core.nc, core.B, core.NT, core.T
    X, Y = core.X, core.Y
    F = I["L0_ffn_w_gate"].shape[0]
    FC = F // P
    S = 1.0 / 127.0
    with ExitStack() as ctx:
        sb = lambda n, s, d=F32: ctx.enter_context(nc.sbuf_tensor("f_" + n, s, d))
        sem = lambda n: core.sem("f_" + n)
        floats = [sb(f"float{k}", [P, F]) for k in range(3)]
        wT = [sb(f"wT{k}", [P, FC, P]) for k in range(3)]
        xn, xnT = sb("xn", [P, NT, D]), [sb(f"xnT{p}", [D, T]) for p in range(2)]
        gated = [sb(f"gated{p}", [P, T]) for p in range(2)]
        hid = [sb(f"hid{p}", [P, FC, T]) for p in range(2)]
        TP = Bank(core, ctx, "f_TP")
        G = [ctx.enter_context(nc.psum_tensor(f"f_G{p}", [P, 512], F32)) for p in range(2)]
        U = [ctx.enter_context(nc.psum_tensor(f"f_U{p}", [P, 512], F32)) for p in range(2)]
        OUT = [Bank(core, ctx, f"f_OUT{p}") for p in range(2)]
        cast, xn_done, init = sem("cast"), sem("xn_done"), sem("init")
        gu_full, gated_done, hid_done = sem("gu_full"), sem("gated_done"), sem("hid_done")
        block = ctx.enter_context(nc.Block())
        xT_use = lambda u: u + 4

        @block.sync
        def _(sp):
            for n in range(1, 4):
                W.load(nc, sp, n)

        @block.gpsimd
        def _(pool):
            pool.memset(hid[1][:], 0.0).then_inc(init, 1)
            W.make_constants(core, pool)

        @block.scalar
        def _(act):
            take_T = lambda u, p: take_transposed(lambda o, i: act.activation(o, i, ACT.Copy), act, TP, xT_use(u),
                                                  xnT[p][:])
            act.preload_act_table(ACT.Silu)
            take_T(0, 0)

            def body(t, p, i):
                for m in range(FC):
                    n = t * FC + m
                    act.wait_ge(gu_full, n + 1)
                    act.wait_ge(hid_done, n + 1)
                    act.activation(gated[(p + m) % 2][:], G[(p + m) % 2][:], ACT.Silu, scale=S)\
                       .then_inc(gated_done, 1)
                take_T(t + 1, 1 - p)

            in_pairs(act, B, body)

        @block.tensor
        def _(pe):
            for bank in (TP, *OUT):
                bank.open(pe)
            for k in range(3):
                pe.wait_ge(cast, k + 1)
                TP.fill(pe, k + 1)
                for m in range(FC):
                    mm = pe.transpose(TP.t[:, tile_of(core, m)], floats[k][:, tile_of(core, m)], core.ident[:])
                TP.filled(mm)

            def x_T(u):
                pe.wait_ge(xn_done, u + 1)
                transposed(core, pe, TP, xT_use(u), xn)

            x_T(0)

            def body(t, p, i):
                TP.after(pe, xT_use(t))
                for m in range(FC):
                    b = (p + m) % 2
                    pe.wait_ge(hid_done, t * FC + (m + 1))
                    pe.matmul(G[b][:], wT[0][:, m, :], xnT[p][:], start=True, stop=True)
                    pe.matmul(U[b][:], wT[1][:, m, :], xnT[p][:], start=True, stop=True).then_inc(gu_full, 1)
                x_T(t + 1)
                down(1 - p, i + 1)

            def down(q, n):
                OUT[q].fill(pe, n)
                for c in range(NT):
                    for m in range(FC):
                        mm = pe.matmul(OUT[q].t[:, tile_of(core, c)], hid[q][:, m, tile_of(core, c)], wT[2][:, m, :],
                                       start=(m == 0), stop=(m == FC - 1))
                OUT[q].filled(mm)

            pe.wait_ge(init, 1)
            in_pairs(pe, B, body)
            pe.wait_ge(hid_done, B * FC + 2)
            down(1, B // 2 + 1)

        @block.vector
        def _(v):
            v.sem_inc(hid_done, 2)
            v.wait_ge(*W.swiglu)
            for k in range(3):
                v.tensor_copy(floats[k][:], W.ints[k][:]).then_inc(cast, 1)
            for k in range(3):
                take_transposed(v.tensor_copy, v, TP, k + 1, wT[k][:].rearrange("p m d -> p (m d)"))

            def layer_norm(u):
                for c in range(NT):
                    op = v.tensor_scalar(xn[:, c], X[:, u, c], core.xmean[:, u, c:c + 1],
                                         core.xrstd[:, u, c:c + 1], ALU.subtract, ALU.mult)
                op.then_inc(xn_done, 1)

            layer_norm(0)
            TP.after(v, xT_use(0))

            def body(t, p, i):
                layer_norm(t + 1)
                for m in range(FC):
                    n = t * FC + m
                    v.wait_ge(gated_done, n + 1)
                    v.scalar_tensor_tensor(hid[p][:, m], U[(p + m) % 2][:], S * S, gated[(p + m) % 2][:], ALU.mult,
                                           ALU.mult).then_inc(hid_done, 1)
                take_out(t - 1, 1 - p, i + 1)

            def take_out(b, q, n):
                OUT[q].read(v, n)
                v.tensor_copy(Y[:, b + 1].rearrange("p c d -> p (c d)"), OUT[q].t[:])
                for c in range(NT):
                    op = v.bn_stats(core.yst[:, b + 1, c], OUT[q].t[:, tile_of(core, c)])
                OUT[q].emptied(op)

            v.wait_ge(init, 1)
            in_pairs(v, B, body)
            take_out(B - 1, 1, B // 2 + 1)


def state_space(core, I, W):
    nc, B, NT, T = core.nc, core.B, core.NT, core.T
    X, Y = core.X, core.Y
    N = I["L1_attn_A_ssm"].shape[1]
    lo, hi = math.log(0.001), math.log(0.1)
    dt = [math.exp(lo + (hi - lo) * n / (N - 1)) for n in range(N)]
    FLY = 8
    PAIRS, SINGLES = N // 4, N // 2
    pair_of, single_of = (lambda n: n // 4), (lambda n: n // 4 * 2 + n % 4 - 2)
    paired_member = lambda n: n % 4 < 2
    state_of = lambda r: r // 2 * 4 + r % 2
    with ExitStack() as ctx:
        sb = lambda n, s, d=F32: ctx.enter_context(nc.sbuf_tensor("m_" + n, s, d))
        sem = lambda n: core.sem("m_" + n)
        A, Bs, C, Ds, s1 = W.A, W.B, W.C, W.D, W.scale1
        dA, coef = sb("dA", [D, N]), sb("coef", [D, N])
        diag = sb("diag", [D, N + 1, D])
        u, uT = sb("u", [P, NT, D]), [sb(f"uT{p}", [D, T]) for p in range(2)]
        state = sb("state", [D, FLY, T])
        weighted_u, both = sb("weighted_u", [D, N // 2, T]), sb("both", [D, 2, T])
        ysb = sb("ysb", [D, T])
        shift = sb("shift", [P, B, NT])
        TP = Bank(core, ctx, "m_TP")
        YT = [Bank(core, ctx, f"m_YT{p}") for p in range(2)]
        Z = Bank(core, ctx, "m_Z")
        dA_done, steps, diag_done = sem("dA_done"), sem("steps"), sem("diag_done")
        u_done, scanned, summed, a_done, shift_done = (sem(n) for n in ("u_done", "scanned", "summed", "a_done", "shift_done"))
        weighted, paired, both_used = sem("weighted"), sem("paired"), sem("both_used")
        block = ctx.enter_context(nc.Block())
        xT_use = lambda b: b + 1

        @block.gpsimd
        def _(pool):
            pool.sem_inc(paired, 2)

            def body(t, p, i):
                for m in range(PAIRS):
                    pool.wait_ge(both_used, t * PAIRS + (m + 1))
                    pool.wait_ge(scanned, t * N + (4 * m + 2 + FLY))
                    pool.tensor_tensor(both[:, m % 2], state[:, 4 * m % FLY], state[:, (4 * m + 1) % FLY],
                                       ALU.add).then_inc(paired, 1)

            in_pairs(pool, B, body)

        @block.scalar
        def _(act):
            act.wait_ge(*W.state_space)
            act.activation(A[:], A[:], ACT.Exp).then_inc(dA_done, 1)
            act.wait_ge(dA_done, 1)
            for n in range(N):
                op = act.activation(dA[:, n:n + 1], A[:, n:n + 1], ACT.Exp, scale=-dt[n])
            op.then_inc(dA_done, 1)
            act.wait_ge(shift_done, 1)

            def take_u(b, p):
                take_transposed(lambda o, i: act.activation(o, i, ACT.Copy), act, TP, xT_use(b), uT[p][:])

            def weigh_u(t, p, first=False):
                for r in range(N // 2):
                    n = state_of(r)
                    if not first:
                        act.wait_ge(scanned, t * N + (n + 1 + FLY - N))
                    act.activation(weighted_u[:, r], uT[p][:], ACT.Copy, scale=coef[:, n:n + 1]).then_inc(weighted, 1)

            take_u(0, 0)
            act.wait_ge(diag_done, 1)
            TP.after(act, xT_use(0))
            weigh_u(0, 0, first=True)

            def body(t, p, i):
                for c in range(NT):
                    op = act.activation(Y[:, t + 1, c], X[:, t, c], ACT.Identity, bias=shift[:, t, c:c + 1],
                                        scale=core.xrstd[:, t, c:c + 1])
                op.then_inc(a_done, 1)
                take_u(t + 1, 1 - p)
                TP.after(act, xT_use(t + 1))
                weigh_u(t + 1, 1 - p)
                YT[p].read(act, i + 1)
                Z.read(act, t + 1)
                YT[p].emptied(act.activation(ysb[:], YT[p].t[:], ACT.Copy))

            in_pairs(act, B, body)

        @block.tensor
        def _(pe):
            for bank in (TP, *YT, Z):
                bank.open(pe)
            pe.sem_inc(summed, SINGLES // 2)
            pe.sem_inc(both_used, 2)

            def u_T(b):
                pe.wait_ge(u_done, b + 1)
                transposed(core, pe, TP, xT_use(b), u)

            u_T(0)
            pe.wait_ge(diag_done, 1)

            def body(t, p, i):
                u_T(t + 1)
                TP.after(pe, xT_use(t))
                YT[p].fill(pe, i + 1)
                for m in range(PAIRS):
                    for n in (4 * m + 2, 4 * m + 3):
                        pe.wait_ge(scanned, t * N + (n + 1 + FLY))
                        pe.matmul(YT[p].t[:], diag[:, n, :], state[:, n % FLY, :], start=(n == 2), stop=False)\
                          .then_inc(summed, 1)
                    pe.wait_ge(paired, t * PAIRS + (m + 3))
                    pe.matmul(YT[p].t[:], core.ident[:], both[:, m % 2, :], start=False, stop=False)\
                      .then_inc(both_used, 1)
                    if m == 0:
                        sum_T(t - 1, 1 - p, i + p)
                YT[p].filled(pe.matmul(YT[p].t[:], diag[:, N, :], uT[p][:], start=False, stop=True))

            def sum_T(b, q, n):
                YT[q].after(pe, n)
                Z.fill(pe, b + 2)
                for c in range(NT):
                    mm = pe.transpose(Z.t[:, tile_of(core, c)], ysb[:, tile_of(core, c)], core.ident[:])
                Z.filled(mm)

            in_pairs(pe, B, body)
            sum_T(B - 1, 1, B // 2)

        @block.vector
        def _(v):
            tick = Tally(v, steps)
            tick.step(v.memset(ysb[:], 0.0))
            v.sem_inc(a_done, 1)
            v.sem_inc(scanned, FLY)
            v.scalar_tensor_tensor(shift[:], core.xmean[:, 0:B], -1.0, core.xrstd[:, 0:B], ALU.mult, ALU.mult)\
             .then_inc(shift_done, 1)

            def rms_norm(b):
                for c in range(NT):
                    op = v.tensor_scalar(u[:, c], X[:, b, c], core.xmean[:, b, c:c + 1],
                                         core.urstd[:, b, c:c + 1], ALU.subtract, ALU.mult)
                op.then_inc(u_done, 1)

            rms_norm(0)
            v.wait_ge(dA_done, 2)
            tick.step(v.tensor_scalar(coef[:], dA[:], -1.0, 1.0, ALU.mult, ALU.add))
            tick.step(v.reciprocal(A[:], A[:]))
            tick.step(v.tensor_tensor(coef[:], coef[:], Bs[:], ALU.mult))
            tick.step(v.tensor_tensor(coef[:], coef[:], A[:], ALU.mult))
            tick.step(v.tensor_tensor(coef[:], coef[:], C[:], ALU.mult))
            tick.step(v.tensor_scalar(coef[:], coef[:], s1[:], None, ALU.mult))
            tick.step(v.tensor_tensor(Ds[:], Ds[:], s1[:], ALU.mult))
            for n in range(N + 1):
                by = coef[:, n:n + 1] if n < N else Ds[:]
                op = v.tensor_scalar(diag[:, n], core.ident[:], by, None, ALU.mult)
            op.then_inc(diag_done, 1)

            def finish(b):
                Z.read(v, b + 2)
                v.wait_ge(a_done, b + 2)
                y = Y[:, b + 1].rearrange("p c d -> p (c d)")
                Z.emptied(v.tensor_tensor(y, y, Z.t[:], ALU.add))
                Z.after(v, b + 2)
                for c in range(NT):
                    v.bn_stats(core.yst[:, b + 1, c], Y[:, b + 1, c])

            def body(t, p, i):
                TP.after(v, xT_use(t))
                for n in range(N):
                    if paired_member(n):
                        v.wait_ge(paired, t * PAIRS + (pair_of(n) + 1))
                        v.wait_ge(weighted, t * (N // 2) + (n // 4 * 2 + n % 4 + 1))
                        source = weighted_u[:, n // 4 * 2 + n % 4, :]
                    else:
                        v.wait_ge(summed, t * SINGLES + (single_of(n) + 1))
                        source = uT[p][:]
                    v.tensor_tensor_scan(state[:, n % FLY, :], dA[:, n:n + 1].to_broadcast([D, T]), source, 0.0,
                                         ALU.mult, ALU.add).then_inc(scanned, 1)
                    if n == 0:
                        rms_norm(t + 1)
                    if n == 11:
                        finish(t - 1)

            in_pairs(v, B, body)
            finish(B - 1)


def mlp(core, I, W):
    nc, B, NT, T = core.nc, core.B, core.NT, core.T
    Y = core.Y
    F = I["L1_attn_w1"].shape[1]
    FC = F // P
    with ExitStack() as ctx:
        sb = lambda n, s, d=F32: ctx.enter_context(nc.sbuf_tensor("g_" + n, s, d))
        sem = lambda n: core.sem("g_" + n)
        w1, w2, b1, b2, s2 = W.w1, W.w2, W.b1, W.b2, W.scale2
        mean, var, tmp, rstd = (sb(n, [P, B, NT]) for n in ("mean", "var", "tmp", "rstd"))
        yn, ynT = sb("yn", [P, NT, D]), [sb(f"ynT{p}", [D, T]) for p in range(2)]
        hid = [sb(f"hid{p}", [P, FC, T]) for p in range(2)]
        TP = Bank(core, ctx, "g_TP")
        H = [Bank(core, ctx, f"g_H{k}") for k in range(FC)]
        OUT = [Bank(core, ctx, f"g_OUT{p}") for p in range(2)]
        steps, scaled, rooted, want_root = (sem(n) for n in ("steps", "scaled", "rooted", "want_root"))
        yn_done = sem("yn_done")
        block = ctx.enter_context(nc.Block())
        yT_use = lambda b: b + 1

        @block.scalar
        def _(act):
            act.wait_ge(want_root, 1)
            act.activation(tmp[:], tmp[:], ACT.Sqrt).then_inc(rooted, 1)
            act.preload_act_table(ACT.Gelu)
            act.wait_ge(*W.mlp)

            def body(t, p, i):
                for m in range(FC):
                    H[m].read(act, t + 1)
                    H[m].emptied(act.activation(hid[p][:, m], H[m].t[:], ACT.Gelu, bias=b1[:, m:m + 1]))

            in_pairs(act, B, body)

        @block.tensor
        def _(pe):
            for bank in (TP, *H, *OUT):
                bank.open(pe)
            pe.wait_ge(scaled, 1)

            def y_T(b):
                pe.wait_ge(yn_done, b + 1)
                transposed(core, pe, TP, yT_use(b), yn)

            y_T(0)

            def body(t, p, i):
                TP.after(pe, yT_use(t))
                for m in range(FC):
                    H[m].fill(pe, t + 1)
                    H[m].filled(pe.matmul(H[m].t[:], w1[:, tile_of(core, m)], ynT[p][:], start=True, stop=True))
                y_T(t + 1)
                OUT[p].fill(pe, i + 1)
                for c in range(NT):
                    o = OUT[p].t[:, tile_of(core, c)]
                    pe.matmul(o, core.ones[0:1, :], b2[:], start=True, stop=False)
                    for m in range(FC):
                        if c == 0:
                            H[m].after(pe, t + 1)
                        mm = pe.matmul(o, hid[p][:, m, tile_of(core, c)], w2[:, m, :], start=False, stop=(m == FC - 1))
                OUT[p].filled(mm)

            in_pairs(pe, B, body)

        @block.vector
        def _(v):
            tick = Tally(v, steps)
            moments(v, tick, core.yst[:, 1:B + 1], mean[:], var[:], tmp[:])
            tick.step(v.tensor_tensor(mean[:], mean[:], mean[:], ALU.mult))
            v.scalar_tensor_tensor(tmp[:], var[:], 1e-6, mean[:], ALU.add, ALU.add).then_inc(want_root, 1)
            v.wait_ge(*W.mlp)
            v.tensor_scalar(w1[:], w1[:], s2[:], None, ALU.mult).then_inc(scaled, 1)
            v.wait_ge(rooted, 1)
            tick.step(v.reciprocal(rstd[:], tmp[:]))

            def rms_norm(b, last=False):
                for c in range(NT):
                    op = v.tensor_scalar(yn[:, c], Y[:, b + 1, c], rstd[:, b, c:c + 1], None, ALU.mult)
                op.then_inc(yn_done, 1)

            def take_T(b, p):
                take_transposed(v.tensor_copy, v, TP, yT_use(b), ynT[p][:])

            rms_norm(0)
            take_T(0, 0)

            def body(t, p, i, last=False):
                rms_norm(t + 1) if not last else v.tensor_copy(yn[:], Y[:, 0]).then_inc(yn_done, 1)
                take_T(t + 1, 1 - p)
                OUT[p].read(v, i + 1)
                y = Y[:, t + 1].rearrange("p c d -> p (c d)")
                OUT[p].emptied(v.tensor_tensor(y, y, OUT[p].t[:], ALU.add))
                OUT[p].after(v, i + 1)
                for c in range(NT):
                    v.bn_stats(core.yst[:, t + 1, c], Y[:, t + 1, c])

            with v.Fori(0, B // 2 - 1) as i:
                for p in range(2):
                    body(i * 2 + p, p, i)
            body(B - 2, 0, B // 2 - 1)
            body(B - 1, 1, B // 2 - 1, last=True)


def experts(core, I, W):
    nc, B, NT, T = core.nc, core.B, core.NT, core.T
    X, Y = core.X, core.Y
    H = I["L1_ffn_enc_W"].shape[1]
    E, M, HH = I["L1_ffn_We1"].shape
    HC = H // P
    G = PARTS * E
    BIG = 64.0
    with ExitStack() as ctx:
        sb = lambda n, s, d=F32: ctx.enter_context(nc.sbuf_tensor("e_" + n, s, d))
        sem = lambda n: core.sem("e_" + n)
        encW, encb, s2cW, s2cb, rW1, rb1, rW2 = W.encW, W.encb, W.s2cW, W.s2cb, W.rW1, W.rb1, W.rW2
        We1, be1, We2, be2, c2sW, c2sb = W.We1, W.be1, W.We2, W.be2, W.c2sW, W.c2sb
        decW, decb, number, select, ident16 = W.decW, W.decb, W.number, W.select, W.ident16
        xn, xnT = sb("xn", [P, NT, D]), [sb(f"xnT{p}", [D, T]) for p in range(2)]
        enc, contT, rT = sb("enc", [P, HC, T]), sb("contT", [2 * M, T]), sb("rT", [65, T])
        moeT, dec_in = sb("moeT", [2 * M, T]), sb("dec_in", [P, HC, T])
        hid = [sb(f"hid{p}", [HH, E, T]) for p in range(2)]
        gates = [sb(f"gates{p}", [P, NT, PARTS, E], BF16) for p in range(2)]
        gatesT, gatesT32 = sb("gatesT", [G, T], BF16), sb("gatesT32", [G, T])
        logit, hit, cand = sb("logit", [P, NT, E]), sb("hit", [P, NT, E]), sb("cand", [P, NT, E])
        mask = [sb(f"mask{k}", [P, NT, E]) for k in range(2)]
        top = [sb(f"top{k}", [P, NT]) for k in range(2)]
        first, gap, share = sb("first", [P, NT]), sb("gap", [P, 2, NT]), sb("share", [P, 2, NT])

        TP = Bank(core, ctx, "e_TP")
        EB = [Bank(core, ctx, f"e_E{m}") for m in range(HC)]
        FB = Bank(core, ctx, "e_F")
        HB = [Bank(core, ctx, f"e_H{k}") for k in range(2)]
        GB = [Bank(core, ctx, f"e_G{k}") for k in range(2)]
        steps, init, xn_done = sem("steps"), sem("init"), sem("xn_done")
        centred = sem("centred")
        gap_done, share_done, gates_done = sem("gap_done"), sem("share_done"), sem("gates_done")
        logits_use, next_xT_use, dec_use = (lambda t, k=k: t * 3 + k for k in range(2, 5))
        enc_use, c2s_use = (lambda t: t * 2 + 1), (lambda t: t * 2 + 2)
        cont_use, router_use, moe_use = (lambda t, k=k: t * 3 + k for k in range(1, 4))
        gate_use = lambda t, e: t * (E // 2 + e % 2) + (e // 2 + 1 + e % 2)
        gatesT_use = lambda t: t * (E // 2 + 1) + 1
        hid_use = lambda t, e: t * (E // 2) + (e // 2 + 2)
        block = ctx.enter_context(nc.Block())

        @block.gpsimd
        def _(pool):
            layer_norm = lambda b: pool_norm(core, pool, b, xn, core.xrstd, centred, b + 1, xn_done)
            layer_norm(0)
            pool.wait_ge(xn_done, 1)
            made = Tally(pool, init)
            made.step(pool.memset(rT[64:65], 1.0))
            made.step(pool.memset(gates[1][:], 0.0))
            made.step(pool.memset(contT[:], 0.0))
            made.step(pool.memset(hid[1][:], 0.0))
            TP.after(pool, 1)

            def body(t, p, i):
                pool.wait_ge(TP.free, t * 3 + 1)
                pool.sem_inc(core.turns, 1)
                layer_norm(t + 1)

            in_pairs(pool, B, body)

        @block.scalar
        def _(act):
            act.preload_act_table(ACT.Sigmoid)
            act.wait_ge(*W.experts)

            def expert_hidden(t, e, p):
                HB[e % 2].read(act, hid_use(t, e))
                HB[e % 2].emptied(act.activation(hid[p][:, e], HB[e % 2].t[:], ACT.Relu, bias=be1[:, e:e + 1]))

            def cells_to_spikes(n):
                for m in range(HC):
                    EB[m].read(act, n)
                    EB[m].emptied(act.activation(dec_in[:, m], EB[m].t[:], ACT.Sigmoid, bias=c2sb[:, m:m + 1]))

            def take_decoded(b, n):
                TP.read(act, n)
                TP.emptied(act.activation(Y[:, b + 1].rearrange("p c d -> p (c d)"), TP.t[:], ACT.Sigmoid))

            def body(t, p, i):
                for m in range(HC):
                    EB[m].read(act, enc_use(t))
                    EB[m].emptied(act.activation(enc[:, m], EB[m].t[:], ACT.Sigmoid, bias=encb[:, m:m + 1]))
                for e in (6, 7):
                    expert_hidden(t - 1, e, 1 - p)
                FB.read(act, router_use(t))
                FB.emptied(act.activation(rT[0:64], FB.t[0:64], ACT.Tanh, bias=rb1[:]))
                for e in range(5):
                    expert_hidden(t, e, p)
                cells_to_spikes(c2s_use(t))
                expert_hidden(t, 5, p)
                act.wait_ge(gap_done, t + 1)
                act.activation(share[:], gap[:], ACT.Sigmoid).then_inc(share_done, 1)
                take_decoded(t - 1, dec_use(t))

            in_pairs(act, B, body)
            for e in (6, 7):
                expert_hidden(B - 1, e, (B - 1) % 2)
            cells_to_spikes(enc_use(B))
            take_decoded(B - 1, logits_use(B))

        @block.tensor
        def _(pe):
            for bank in (TP, *EB, FB, *HB, *GB):
                bank.open(pe)
            pe.wait_ge(*W.experts)
            pe.wait_ge(W.constants, W.made)
            pe.wait_ge(init, 3)

            def x_T(u, n):
                pe.wait_ge(xn_done, u + 1)
                transposed(core, pe, TP, n, xn)

            def encoder(t, p):
                pe.wait_ge(TP.free, t * 3 + 1)
                for m in range(HC):
                    EB[m].fill(pe, enc_use(t))
                    EB[m].filled(pe.matmul(EB[m].t[:], encW[:, tile_of(core, m)], xnT[p][:], start=True, stop=True))

            def gates_T(t, q):
                pe.wait_ge(gates_done, t * PARTS + 1)
                GB[1].fill(pe, gatesT_use(t))
                for c in range(NT):
                    mm = pe.matmul(GB[1].t[0:G, tile_of(core, c)], gates[q][:, c].rearrange("p k e -> p (k e)"), ident16[:],
                                   start=True, stop=True)
                GB[1].filled(mm)

            def cells(t):
                for m in range(HC):
                    EB[m].after(pe, enc_use(t))
                FB.fill(pe, cont_use(t))
                for m in range(HC):
                    mm = pe.matmul(FB.t[m * M:(m + 1) * M], s2cW[:, m, :], enc[:, m, :], start=True, stop=True,
                                   skip_group_check=True)
                FB.filled(mm)

            def router(t):
                FB.fill(pe, router_use(t))
                FB.filled(pe.matmul(FB.t[0:64], rW1[:], contT[:], start=True, stop=True))

            def expert_in(t, e):
                HB[e % 2].fill(pe, hid_use(t, e))
                HB[e % 2].filled(pe.matmul(HB[e % 2].t[:], We1[:, e, :], contT[:], start=True, stop=True))

            def logits(t):
                FB.after(pe, router_use(t))
                TP.fill(pe, logits_use(t))
                for c in range(NT):
                    mm = pe.matmul(TP.t[:, c * E:(c + 1) * E], rT[:, tile_of(core, c)], rW2[:], start=True, stop=True)
                TP.filled(mm)

            def spread_gate(t, e):
                if e == 0:
                    GB[1].after(pe, gatesT_use(t))
                GB[e % 2].fill(pe, gate_use(t, e))
                GB[e % 2].filled(pe.matmul(GB[e % 2].t[:], select[:, e, :], gatesT[:], start=True, stop=True))

            def output_bias(n):
                FB.fill(pe, n)
                pe.matmul(FB.t[0:M], be2[:], gatesT32[:], start=True, stop=False, skip_group_check=True)

            def expert_out(t, e, q):
                GB[e % 2].after(pe, gate_use(t, e))
                h = e % 2
                return pe.matmul(FB.t[h * M:(h + 1) * M], We2[:, e, :], hid[q][:, e, :], start=(e == 1),
                                 stop=(e >= E - 2), skip_group_check=True)

            def spikes(n_moe, n):
                FB.after(pe, n_moe)
                for m in range(HC):
                    EB[m].fill(pe, n)
                    EB[m].filled(pe.matmul(EB[m].t[:], c2sW[:, tile_of(core, m)], moeT[:], start=True, stop=True))

            def decode(n_spikes, n):
                for m in range(HC):
                    EB[m].after(pe, n_spikes)
                TP.fill(pe, n)
                for c in range(NT):
                    o = TP.t[:, tile_of(core, c)]
                    pe.matmul(o, core.ones[0:1, :], decb[:], start=True, stop=False)
                    for m in range(HC):
                        mm = pe.matmul(o, dec_in[:, m, tile_of(core, c)], decW[:, m, :], start=False, stop=(m == HC - 1))
                TP.filled(mm)

            x_T(0, 1)
            TP.after(pe, 1)

            def body(t, p, i):
                encoder(t, p)
                expert_in(t - 1, 6)
                expert_in(t - 1, 7)
                cells(t)
                gates_T(t, 1 - p)
                router(t)
                expert_in(t, 0)
                spread_gate(t, 0)
                spread_gate(t, 1)
                expert_in(t, 1)
                logits(t)
                output_bias(moe_use(t))
                for e in range(E):
                    mm = expert_out(t, e, 1 - p)
                    if e + 2 < E:
                        spread_gate(t, e + 2)
                    if e in (1, 3, 5):
                        expert_in(t, (e + 3) // 2)
                FB.filled(mm)
                x_T(t + 1, next_xT_use(t))
                spikes(moe_use(t), c2s_use(t))
                expert_in(t, 5)
                decode(c2s_use(t), dec_use(t))

            in_pairs(pe, B, body)
            q = (B - 1) % 2
            expert_in(B - 1, 6)
            expert_in(B - 1, 7)
            gates_T(B, q)
            spread_gate(B, 0)
            spread_gate(B, 1)
            output_bias(cont_use(B))
            for e in range(E):
                mm = expert_out(B, e, q)
                if e + 2 < E:
                    spread_gate(B, e + 2)
            FB.filled(mm)
            spikes(cont_use(B), enc_use(B))
            decode(enc_use(B), logits_use(B))

        @block.vector
        def _(v):
            tick = Tally(v, steps, per=14)
            wide = lambda a: a.unsqueeze(2).to_broadcast([P, NT, E])

            def take_gates(n):
                GB[1].read(v, n)
                v.tensor_copy(gatesT[:], GB[1].t[0:G])
                GB[1].emptied(v.tensor_copy(gatesT32[:], GB[1].t[0:G]))

            def weigh(t, e, q):
                if e < 2:
                    HB[e].after(v, hid_use(t - 1, E - 2))
                GB[e % 2].read(v, gate_use(t, e))
                GB[e % 2].emptied(v.tensor_tensor(hid[q][:, e], hid[q][:, e], GB[e % 2].t[:], ALU.mult))

            def take_logits(t):
                TP.read(v, logits_use(t))
                TP.emptied(v.tensor_copy(logit[:].rearrange("p c e -> p (c e)"), TP.t[:, 0:NT * E]))

            def take_moe(n):
                FB.read(v, n)
                FB.emptied(v.tensor_copy(moeT[:], FB.t[:]))

            def choose(t):
                tick.begin(t)
                numbers = number[:].unsqueeze(1).to_broadcast([P, NT, E])
                TP.after(v, logits_use(t))
                for k in range(2):
                    tick.step(v.tensor_reduce(top[k][:], logit[:], AX.X, ALU.max))
                    tick.step(v.tensor_tensor(hit[:], logit[:], wide(top[k][:]), ALU.is_equal))
                    tick.step(v.scalar_tensor_tensor(cand[:], hit[:], -BIG, numbers, ALU.mult, ALU.add))
                    tick.step(v.tensor_reduce(first[:], cand[:], AX.X, ALU.min))
                    tick.step(v.tensor_tensor(mask[k][:], cand[:], wide(first[:]), ALU.is_equal))
                    if k == 0:
                        tick.step(v.scalar_tensor_tensor(logit[:], mask[0][:], -3e38, logit[:], ALU.mult, ALU.add))
                v.tensor_tensor(gap[:, 0], top[0][:], top[1][:], ALU.subtract)
                v.tensor_tensor(gap[:, 1], top[1][:], top[0][:], ALU.subtract).then_inc(gap_done, 1)

            def gate(t, p):
                part = lambda k: gates[p][:, :, k, :]
                v.wait_ge(share_done, t + 1)
                v.tensor_tensor(hit[:], mask[0][:], wide(share[:, 0]), ALU.mult)
                tick.step(v.tensor_tensor(cand[:], mask[1][:], wide(share[:, 1]), ALU.mult))
                tick.step(v.tensor_tensor(hit[:], hit[:], cand[:], ALU.add))
                tick.step(v.tensor_copy(part(0), hit[:]))
                v.tensor_tensor(hit[:], hit[:], part(0), ALU.subtract).then_inc(gates_done, 1)
                v.wait_ge(gates_done, t * PARTS + 2)
                v.tensor_copy(part(1), hit[:]).then_inc(gates_done, 1)
                v.wait_ge(gates_done, t * PARTS + 3)
                v.tensor_tensor(part(2), hit[:], part(1), ALU.subtract).then_inc(gates_done, 1)

            v.sem_inc(gates_done, 1)
            v.wait_ge(*W.experts)
            v.wait_ge(W.constants, W.made)
            v.wait_ge(init, 4)
            take_transposed(v.tensor_copy, v, TP, 1, xnT[0][:])

            def body(t, p, i):
                FB.read(v, cont_use(t))
                FB.emptied(v.tensor_scalar(contT[:], FB.t[:], s2cb[:], None, ALU.add))
                take_gates(gatesT_use(t))
                weigh(t, 0, 1 - p)
                weigh(t, 1, 1 - p)
                take_logits(t)
                for e in range(2, E):
                    weigh(t, e, 1 - p)
                take_moe(moe_use(t))
                take_transposed(v.tensor_copy, v, TP, next_xT_use(t), xnT[1 - p][:])
                choose(t)
                gate(t, p)
                TP.after(v, dec_use(t))
                for c in range(NT):
                    v.bn_stats(core.yst[:, t, c], Y[:, t, c])

            in_pairs(v, B, body)
            q = (B - 1) % 2
            take_gates(gatesT_use(B))
            for e in range(E):
                weigh(B, e, q)
            take_moe(cont_use(B))
            TP.after(v, logits_use(B))
            for c in range(NT):
                v.bn_stats(core.yst[:, B, c], Y[:, B, c])


def program(nc, I, out):
    B, S, _ = I["L0_attn_x"].shape
    with ExitStack() as ctx:
        core = Core(nc, ctx, B, S // P)
        setup(core, I)
        attention(core, I)
        W = Weights(core, I)
        check_range(core, W)
        with nc.If(nc.values_load(core.in_range[0:1, 0:1], min_val=0, max_val=1) == 0):
            attention_guarded(core, I)
        add_normed(core, "r1")
        swiglu(core, I, W)
        add_normed(core, "r2", rms=True)
        state_space(core, I, W)
        mlp(core, I, W)
        add_normed(core, "r3")
        experts(core, I, W)
        add_normed(core, "r4", affine=(W.gain, W.bias, W.experts), store=out)


def kernel(**inputs):
    import numpy as np
    import concourse.bacc as bacc
    from concourse import mybir
    from concourse.bass_utils import run_bass_kernel_spmd as launch

    nc = bacc.Bacc("TRN2", target_bir_lowering=False, num_devices=1)
    arrays = {name: np.ascontiguousarray(a) for name, a in inputs.items()}
    B, S, width = arrays["L0_attn_x"].shape
    tiles = S // 128
    distance = np.arange(S + (tiles - 1) * 128)[None, :] - (tiles - 1) * 128 - np.arange(128)[:, None]
    arrays["decay"] = np.exp(-1e-4 * np.abs(distance)).astype(np.float32)
    I = {name: nc.dram_tensor(name, a.shape, mybir.dt.from_np(a.dtype), kind="ExternalInput").ap()
         for name, a in arrays.items()}
    out = nc.dram_tensor("out", (B, S, width), mybir.dt.float32, kind="ExternalOutput").ap()
    program(nc, I, out)
    r = launch(nc, [arrays], core_ids=[0])
    return r.results[0]["out"]
```
